# Optimizing a Trainium2 kernel written in Bass

```python
import numpy as np
import jax
import jax.numpy as jnp

def _softmax(x, axis=-1):
    return jax.nn.softmax(x, axis=axis)

def _gelu(x):
    return jax.nn.gelu(x, approximate=True)

def _silu(x):
    return jax.nn.silu(x)

def _sigmoid(x):
    return jax.nn.sigmoid(x)

def _layernorm(x, axis=-1, eps=1e-05):
    m = jnp.mean(x, axis=axis, keepdims=True)
    v = jnp.var(x, axis=axis, keepdims=True)
    return (x - m) / jnp.sqrt(v + eps)

def _scatter_add(tgt, idx, src, axis=0):
    return tgt.at[idx].add(src)

def _segment_sum(src, seg, n):
    return jax.ops.segment_sum(src, seg, n)
kernel_name = 'mk_gps_d1_gnn_r8_6fa1f9'

def setup_inputs(seed: int=0):
    np.random.seed(seed)
    _w = jnp.asarray

    def _rec_inputs():
        import jax
        import jax.numpy as jnp
        _gk = jax.random.key(seed)
        x = -0.0002117 + 1 * jax.random.normal(jax.random.fold_in(_gk, 1), (6250, 512), jnp.float32)
        _s = jax.random.randint(jax.random.fold_in(_gk, 2), (50000,), 0, 6250, jnp.int32)
        _d = jax.random.randint(jax.random.fold_in(_gk, 3), (50000,), 0, 6250, jnp.int32)
        _loop = jnp.arange(6250, dtype=jnp.int32)
        src = jnp.concatenate([_s, _d, _loop])
        dst = jnp.concatenate([_d, _s, _loop])
        _o = jnp.argsort(dst, stable=True)
        src = src[_o]
        dst = dst[_o]
        edge_attr_64 = 0.000189758 + 1.00013 * jax.random.normal(jax.random.fold_in(_gk, 12), (106250, 64), jnp.float32)
        return (x, src, dst, edge_attr_64)
    x, src, dst, edge_attr_64 = _rec_inputs()

    def _L0_gnn_setup():
        import jax, jax.numpy as jnp
        import numpy as np
        N_NODES = 6250
        N_EDGES = 100000
        NODE_IN = 512
        EDGE_IN = 64
        HID = 1024
        key = jax.random.key(seed)
        ks = jax.random.split(key, 6)
        x = jax.random.normal(ks[0], (N_NODES, NODE_IN), dtype=jnp.float32)
        edge_index = jax.random.randint(ks[1], (2, N_EDGES), 0, N_NODES, dtype=jnp.int64)
        edge_attr = jax.random.normal(ks[2], (N_EDGES, EDGE_IN), dtype=jnp.float32)
        u = jnp.zeros((1, 16), dtype=jnp.float32)
        batch = jnp.zeros((N_NODES,), dtype=jnp.int64)
        s1 = 1.0 / np.sqrt(NODE_IN + EDGE_IN)
        s2 = 1.0 / np.sqrt(HID)
        W1 = jax.random.normal(ks[3], (NODE_IN + EDGE_IN, HID), dtype=jnp.float32) * s1
        b1 = jnp.zeros((HID,), dtype=jnp.float32)
        W2 = jax.random.normal(ks[4], (HID, NODE_IN), dtype=jnp.float32) * s2
        b2 = jnp.zeros((NODE_IN,), dtype=jnp.float32)
        return {'x': x, 'edge_index': edge_index, 'edge_attr': edge_attr, 'u': u, 'batch': batch, 'W1': W1, 'b1': b1, 'W2': W2, 'b2': b2}
    _L0_gnn_all = _L0_gnn_setup()
    _L0_gnn_in = {k: v for k, v in _L0_gnn_all.items() if k in ('u', 'W1', 'b1', 'W2', 'b2')}
    del _L0_gnn_all

    def _L0_mix_setup():
        import jax, jax.numpy as jnp
        import numpy as np
        key = jax.random.key(seed)
        k1, k2, k3 = jax.random.split(key, 3)
        B, S, E = (4, 512, 512)
        x = jax.random.normal(k1, (B, S, E), dtype=jnp.float32)
        lim_qkv = float(np.sqrt(6.0 / (E + 3 * E)))
        W_qkv = jax.random.uniform(k2, (3 * E, E), minval=-lim_qkv, maxval=lim_qkv, dtype=jnp.float32)
        b_qkv = jnp.zeros((3 * E,), dtype=jnp.float32)
        lim_out = float(np.sqrt(6.0 / (E + E)))
        W_out = jax.random.uniform(k3, (E, E), minval=-lim_out, maxval=lim_out, dtype=jnp.float32)
        b_out = jnp.zeros((E,), dtype=jnp.float32)
        return {'x': x, 'W_qkv': W_qkv, 'b_qkv': b_qkv, 'W_out': W_out, 'b_out': b_out}
    _L0_mix_all = _L0_mix_setup()
    _L0_mix_in = {k: v for k, v in _L0_mix_all.items() if k in ('W_qkv', 'b_qkv', 'W_out', 'b_out')}
    del _L0_mix_all

    def _L0_ffn_setup():
        import jax, jax.numpy as jnp
        import numpy as np
        B, S, D, E, O = (1024, 256, 512, 16, 512)
        key = jax.random.key(seed)
        k_x, k_wg, k_bg, k_we, k_be = jax.random.split(key, 5)
        scale_g = 1.0 / np.sqrt(D)
        scale_e = 1.0 / np.sqrt(D)
        return {'x': jax.random.normal(k_x, (B, S, D), dtype=jnp.float32), 'Wg': jax.random.uniform(k_wg, (D, E), jnp.float32, -scale_g, scale_g), 'bg': jax.random.uniform(k_bg, (E,), jnp.float32, -scale_g, scale_g), 'We': jax.random.uniform(k_we, (E, D, O), jnp.float32, -scale_e, scale_e), 'be': jax.random.uniform(k_be, (E, O), jnp.float32, -scale_e, scale_e)}
    _L0_ffn_all = _L0_ffn_setup()
    _L0_ffn_in = {k: v for k, v in _L0_ffn_all.items() if k in ('Wg', 'bg', 'We', 'be')}
    del _L0_ffn_all
    return {'x': x, 'src': src, 'dst': dst, 'edge_attr_64': edge_attr_64, 'L0_gnn_u': _L0_gnn_in['u'], 'L0_gnn_W1': _L0_gnn_in['W1'], 'L0_gnn_b1': _L0_gnn_in['b1'], 'L0_gnn_W2': _L0_gnn_in['W2'], 'L0_gnn_b2': _L0_gnn_in['b2'], 'L0_mix_W_qkv': _L0_mix_in['W_qkv'], 'L0_mix_b_qkv': _L0_mix_in['b_qkv'], 'L0_mix_W_out': _L0_mix_in['W_out'], 'L0_mix_b_out': _L0_mix_in['b_out'], 'L0_ffn_Wg': _L0_ffn_in['Wg'], 'L0_ffn_bg': _L0_ffn_in['bg'], 'L0_ffn_We': _L0_ffn_in['We'], 'L0_ffn_be': _L0_ffn_in['be']}

def reference(x, src, dst, edge_attr_64, L0_gnn_u, L0_gnn_W1, L0_gnn_b1, L0_gnn_W2, L0_gnn_b2, L0_mix_W_qkv, L0_mix_b_qkv, L0_mix_W_out, L0_mix_b_out, L0_ffn_Wg, L0_ffn_bg, L0_ffn_We, L0_ffn_be):
    import jax
    import jax.numpy as jnp

    def _L0_gnn_ref(x, edge_index, edge_attr, u, batch, W1, b1, W2, b2):
        import jax, jax.numpy as jnp
        import numpy as np
        N_NODES = 6250
        N_EDGES = 100000
        NODE_IN = 512
        EDGE_IN = 64
        HID = 1024
        col = edge_index[1]
        summed = jax.ops.segment_sum(edge_attr, col, num_segments=x.shape[0])
        count = jax.ops.segment_sum(jnp.ones((edge_attr.shape[0],), dtype=x.dtype), col, num_segments=x.shape[0])
        agg = summed / jnp.maximum(count, 1.0)[:, None]
        h = jnp.concatenate([x, agg], axis=-1)
        h = jax.nn.relu(h @ W1 + b1)
        return x + h @ W2 + b2

    def _L0_mix_ref(x, W_qkv, b_qkv, W_out, b_out):
        import jax, jax.numpy as jnp
        import numpy as np
        B, S, E = x.shape
        H = 8
        D = E // H
        qkv = x @ W_qkv.T + b_qkv
        qkv = qkv.reshape(B, S, H, 3 * D)
        q, k, v = jnp.split(qkv, 3, axis=-1)
        q = jax.nn.sigmoid(q)
        k = jax.nn.sigmoid(k)
        i = jnp.sum(q * jnp.sum(k, axis=1, keepdims=True), axis=3, keepdims=True)
        o = jnp.sum(k * jnp.sum(q, axis=1, keepdims=True), axis=3, keepdims=True)
        i_hat = jnp.sum(q * jnp.sum(k / o, axis=1, keepdims=True), axis=3, keepdims=True)
        o_hat = jnp.sum(k * jnp.sum(q / i, axis=1, keepdims=True), axis=3, keepdims=True)
        vw = v * jax.nn.softmax(o_hat, axis=1)
        kv = jnp.einsum('bshd,bshe->bsde', k, vw)
        r = jnp.einsum('bshd,bsde->bshe', q / i, kv) * jax.nn.sigmoid(i_hat)
        values = r.reshape(B, S, E)
        return values @ W_out.T + b_out

    def _L0_ffn_ref(x, Wg, bg, We, be):
        import jax, jax.numpy as jnp
        import numpy as np
        B, S, D, E, O = (1024, 256, 512, 16, 512)
        scores = jax.nn.softmax(jnp.mean(x, axis=1) @ Wg + bg, axis=-1)
        idx = jnp.argmax(scores, axis=-1)
        gate = jnp.take_along_axis(scores, idx[:, None], axis=-1)
        W_sel = We[idx]
        b_sel = be[idx]
        y = jnp.einsum('bsd,bdo->bso', x, W_sel) + b_sel[:, None, :]
        return gate[:, :, None] * y
    edge_index = jnp.stack([src, dst])
    batch0 = jnp.zeros((6250,), jnp.int32)
    xn = _layernorm(x, axis=-1)
    x = x + _L0_gnn_ref(xn, edge_index, edge_attr_64, L0_gnn_u, batch0, L0_gnn_W1, L0_gnn_b1, L0_gnn_W2, L0_gnn_b2) + _L0_mix_ref(xn[None], L0_mix_W_qkv, L0_mix_b_qkv, L0_mix_W_out, L0_mix_b_out)[0]
    x = x + _L0_ffn_ref(_layernorm(x, axis=-1)[None], L0_ffn_Wg, L0_ffn_bg, L0_ffn_We, L0_ffn_be)[0]
    return x

_drawn_inputs = setup_inputs


def setup_inputs(seed=0):
    import zlib

    import numpy as np

    out = dict(_drawn_inputs(seed))
    spreads = {'L0_gnn_u': (0.0, 0.1),
     'L0_gnn_b1': (0.0, 0.1),
     'L0_gnn_b2': (0.0, 0.1),
     'L0_mix_b_qkv': (0.0, 2.0),
     'L0_mix_b_out': (0.0, 0.1)}
    factors = {'L0_mix_W_qkv': 200.0,
     'L0_mix_W_out': 200.0,
     'L0_ffn_Wg': 28.439,
     'L0_ffn_bg': 200.0,
     'L0_ffn_be': 8.0}
    for name, (base, spread) in spreads.items():
        noise = np.random.default_rng([zlib.crc32(name.encode()), seed]).standard_normal(out[name].shape)
        drawn = base * np.exp(spread * noise) if base else spread * noise
        out[name] = jnp.asarray(drawn.astype(out[name].dtype))
    for name, factor in factors.items():
        out[name] = (out[name] * factor).astype(out[name].dtype)
    return out
```

```python
from contextlib import ExitStack

import concourse.bass as bass
from concourse import mybir

ALU = mybir.AluOpType
ACT = mybir.ActivationFunctionType
AX = mybir.AxisListType
F32 = mybir.dt.float32
F32R = mybir.dt.float32r
I32 = mybir.dt.int32

P = 128
TOKENS = 6250
DIM = 512
HEADS = 8
HDIM = DIM // HEADS
EDGES = 106250
EDIM = 64
HID = 1024
EXPERTS = 16
CH = DIM // P
QK = 2 * CH
JH = HID // P
BT = 512
FULL = TOKENS // BT
TAIL = TOKENS - FULL * BT
NB = FULL + 1
GT = P // HEADS
EPS = 1e-5
MID = TOKENS // 2
TABLES = 4
TROWS = 6400
ECOLS = EDIM + 1


def subtiles(n):
    return [min(P, n - s) for s in range(0, n, P)]


def over_blocks(eng, unroll, body):
    looped = (FULL - 1) // unroll
    with eng.Fori(0, looped) as i:
        for k in range(unroll):
            body(i * unroll + k, k, BT, BT)
    for b in range(looped * unroll, NB):
        sizes = [BT] * FULL + [TAIL, 0]
        body(b, b % unroll, sizes[b], sizes[b + 1])


def landed(b, k, unroll, dmas=1):
    return (b - k) * (16 * dmas // unroll) + 16 * dmas


def cols(b, n):
    return bass.ds(b * BT, n)


class Edges:

    def __init__(self, ctx, nc, c, name, first_edge, tiles, tail_tiles, tail_rows, unroll, scattered, psum):
        self.c, self.first, self.tiles, self.unroll = c, first_edge, tiles, unroll
        self.tail_tiles, self.tail_rows = tail_tiles, tail_rows
        self.quads = tiles // 4
        self.scattered = dict(scattered)
        self.last_edge = first_edge + FULL * tiles * P + tail_tiles * tail_rows

        def sb(what, shape, dt=F32):
            return ctx.enter_context(nc.sbuf_tensor(f"{name}_{what}", shape, dt))

        def sem(what):
            return ctx.enter_context(nc.semaphore(f"{name}_{what}"))

        self.attr = [sb(f"attr{k}", [P, tiles, ECOLS]) for k in range(unroll)]
        self.dst = [sb(f"dst{k}", [P, tiles], I32) for k in range(unroll)]
        self.dst_f = [sb(f"dst_f{k}", [P, tiles]) for k in range(unroll)]
        self.dst_r = [sb(f"dst_r{k}", [P, tiles], F32R) for k in range(unroll)]
        self.later = [sb(f"later{k}", [P, tiles]) for k in range(unroll)]
        self.row_a = [sb(f"row_a{k}", [P, tiles]) for k in range(unroll)]
        self.row_b = [sb(f"row_b{k}", [P, tiles]) for k in range(unroll)]
        self.row = [sb(f"row{k}", [P, tiles], I32) for k in range(unroll)]
        self.sums = [sb(f"sums{k}", [P, tiles, ECOLS]) for k in range(unroll)]
        self.sel = [sb(f"sel{k}", [P, 4, P]) for k in range(2)]
        self.p_dst, self.p_sum = psum

        self.edges_in = [sem(f"edges_in{k}") for k in range(unroll)]
        self.ones_set = sem("ones_set")
        self.dst_ready = sem("dst_ready")
        self.spread = sem("spread")
        self.selected = sem("selected")
        self.summed = sem("summed")
        self.kept = sem("kept")
        self.row_step = sem("row_step")
        self.rows_ready = sem("rows_ready")
        self.sums_free = sem("sums_free")

    def shape(self, n):
        return (self.tiles, P) if n == BT else (self.tail_tiles, self.tail_rows)

    def quads_of(self, n):
        m = self.shape(n)[0]
        return [(q, min(4, m - q)) for q in range(0, m, 4)]

    def load(self, sp, b, k, n, guard):
        m, rows = self.shape(n)
        if guard is not None:
            sp.wait_ge(self.summed, guard)
        at = self.first + b * (self.tiles * P)
        sp.dma_start(self.dst[k][0:rows, 0:m],
                     self.c.dst[bass.ds(at, m * rows)].rearrange("(p m) -> p m", m=m)).then_inc(self.edges_in[k], 16)
        sp.dma_start(self.attr[k][0:rows, 0:m, 0:EDIM],
                     self.c.edge_attr[bass.ds(at, m * rows), :].rearrange("(p m) d -> p m d", m=m)
                     ).then_inc(self.edges_in[k], 16)

    def load_first(self, sp):
        sp.wait_ge(self.ones_set, self.unroll)
        self.load(sp, 0, 0, BT, None)

    def load_next(self, sp, b, k, after):
        if after:
            self.load(sp, b + 1, (k + 1) % self.unroll, after, self.quads * b)

    def begin_dve(self, dve):
        for k in range(self.unroll):
            dve.memset(self.attr[k][:, :, EDIM:ECOLS], 1.0).then_inc(self.ones_set, 1)

    def prepare(self, dve, b, k, n):
        m, rows = self.shape(n)
        dve.wait_ge(self.edges_in[k], landed(b, k, self.unroll, 2))
        dve.tensor_scalar(self.dst_f[k][0:rows, 0:m], self.dst[k][0:rows, 0:m], float(-MID), None,
                          ALU.add).then_inc(self.row_step, 1)
        dve.wait_ge(self.row_step, b * 3 + 1)
        dve.tensor_copy(self.dst_r[k][0:rows, 0:m], self.dst_f[k][0:rows, 0:m]).then_inc(self.dst_ready, 1)

    def spread_dst(self, pe, b, k, n, q):
        rows = self.shape(n)[1]
        if q == 0:
            pe.wait_ge(self.dst_ready, b + 1)
        pe.wait_ge(self.selected, b * self.quads + q)
        j0, w = self.quads_of(n)[q]
        for j in range(w):
            mm = pe.matmul(self.p_dst[0:rows, j * P:j * P + rows],
                           self.dst_r[k][0:rows, j0 + j:j0 + j + 1].to_broadcast([rows, rows]),
                           self.c.ident_r[0:rows, 0:rows], start=True, stop=True)
        mm.then_inc(self.spread, 1)

    def select(self, dve, b, k, n, q):
        rows = self.shape(n)[1]
        dve.wait_ge(self.spread, b * self.quads + q + 1)
        j0, w = self.quads_of(n)[q]
        for j in range(w):
            t = j0 + j
            op = dve.scalar_tensor_tensor(
                out=self.sel[q % 2][0:rows, j, 0:rows], in0=self.p_dst[0:rows, j * P:j * P + rows],
                scalar=self.dst_f[k][0:rows, t:t + 1], in1=self.c.upper[0:rows, 0:rows],
                op0=ALU.is_equal, op1=ALU.mult, accum_out=self.later[k][0:rows, t:t + 1])
        op.then_inc(self.selected, 1)

    def sum_tile(self, pe, b, k, n, q):
        rows = self.shape(n)[1]
        pe.wait_ge(self.selected, b * self.quads + q + 1)
        pe.wait_ge(self.kept, b * self.quads + q)
        j0, w = self.quads_of(n)[q]
        for j in range(w):
            mm = pe.matmul(self.p_sum[0:rows, j * ECOLS:(j + 1) * ECOLS], self.sel[q % 2][0:rows, j, 0:rows],
                           self.attr[k][0:rows, j0 + j, :], start=True, stop=True)
        mm.then_inc(self.summed, 1)

    def keep(self, act, b, k, n, q):
        rows = self.shape(n)[1]
        act.wait_ge(self.summed, b * self.quads + q + 1)
        if q == 0:
            act.wait_ge(self.sums_free, b + 1)
        j0, w = self.quads_of(n)[q]
        act.activation(self.sums[k][0:rows, j0:j0 + w, :], self.p_sum[0:rows, 0:w * ECOLS]
                       .rearrange("p (w c) -> p w c", w=w), ACT.Copy).then_inc(self.kept, 1)

    def rows(self, dve, b, k, n):
        m, rows = self.shape(n)
        dve.wait_ge(self.selected, b * self.quads + len(self.quads_of(n)))
        dve.wait_ge(self.sums_free, b + 1)
        dve.tensor_scalar(self.row_a[k][0:rows, 0:m], self.dst_f[k][0:rows, 0:m], self.c.spare[0:rows, :],
                          None, ALU.subtract).then_inc(self.row_step, 1)
        dve.wait_ge(self.row_step, b * 3 + 2)
        dve.scalar_tensor_tensor(out=self.row_b[k][0:rows, 0:m], in0=self.later[k][0:rows, 0:m], scalar=1.0,
                                 in1=self.row_a[k][0:rows, 0:m], op0=ALU.is_equal,
                                 op1=ALU.mult).then_inc(self.row_step, 1)
        dve.wait_ge(self.row_step, b * 3 + 3)
        dve.tensor_scalar(self.row[k][0:rows, 0:m], self.row_b[k][0:rows, 0:m], self.c.spare[0:rows, :],
                          float(MID), ALU.add, ALU.add).then_inc(self.rows_ready, 1)

    def begin_pool(self, pool):
        pool.sem_inc(self.sums_free, self.unroll)

    def scatter(self, pool, b, k, n):
        m, rows = self.shape(n)
        pool.wait_ge(self.rows_ready, b + 1)
        pool.wait_ge(self.kept, b * self.quads + len(self.quads_of(n)))
        each = self.tiles // TABLES
        for j in range(m):
            t = j % TABLES
            pool.wait_ge(self.c.scattered[t], (b * each + (j // TABLES + self.scattered[t])) * 16)
            pool.sem_inc(self.c.passed, 1)
            pool.indirect_dma_start(
                self.c.table[t], bass.IndirectOffsetOnAxis(ap=self.row[k][0:rows, j:j + 1], axis=0),
                self.sums[k][0:rows, j, :], None, compute_op=ALU.add).then_inc(self.c.scattered[t], 16)
        for t in range(TABLES):
            done = len([j for j in range(m) if j % TABLES == t])
            pool.wait_ge(self.c.scattered[t], (b * each + (done + self.scattered[t])) * 16)
        pool.sem_inc(self.sums_free, 1)

    def total(self):
        return {t: self.scattered[t] + FULL * (self.tiles // TABLES)
                + len([j for j in range(self.tail_tiles) if j % TABLES == t]) for t in range(TABLES)}


class Weights:

    def __init__(self, ctx, nc, name, items, width):
        self.items = items
        self.raw = [ctx.enter_context(nc.sbuf_tensor(f"{name}_raw{k}", [P, width], F32)) for k in range(2)]
        self.loaded = [ctx.enter_context(nc.semaphore(f"{name}_loaded{k}")) for k in range(2)]
        self.hi_ready = ctx.enter_context(nc.semaphore(f"{name}_hi_ready"))
        self.lo_ready = ctx.enter_context(nc.semaphore(f"{name}_lo_ready"))

    def load(self, sp):
        for i, (src, hi, lo) in enumerate(self.items):
            if i >= 2:
                sp.wait_ge(self.lo_ready, i - 1)
            sp.dma_start(self.raw[i % 2][0:src.shape[0], 0:src.shape[1]], src).then_inc(self.loaded[i % 2], 16)

    def split_hi(self, act):
        for i, (src, hi, lo) in enumerate(self.items):
            act.wait_ge(self.loaded[i % 2], 16 * (i // 2 + 1))
            act.activation(hi, self.raw[i % 2][0:src.shape[0], 0:src.shape[1]], ACT.Copy).then_inc(self.hi_ready, 1)

    def split_lo(self, dve):
        for i, (src, hi, lo) in enumerate(self.items):
            dve.wait_ge(self.hi_ready, i + 1)
            dve.tensor_tensor(lo, self.raw[i % 2][0:src.shape[0], 0:src.shape[1]], hi.bitcast(F32),
                              ALU.subtract).then_inc(self.lo_ready, 1)

    def wait(self, pe):
        pe.wait_ge(self.lo_ready, len(self.items))


def products(pe, out, left, right, first=True, last=True):
    n = 3 * len(left)
    i = 0
    for (lh, ll), (rh, rl) in zip(left, right):
        for a, c in ((lh, rh), (ll, rh), (lh, rl)):
            mm = pe.matmul(out, a, c, start=first and i == 0, stop=last and i == n - 1)
            i += 1
    return mm


class Norm:

    def __init__(self, ctx, nc, c, name, banks, copies, bank_free=None, xn_used=None):
        def sb(what, shape, dt=F32):
            return ctx.enter_context(nc.sbuf_tensor(f"{name}_{what}", shape, dt))

        def sem(what):
            return ctx.enter_context(nc.semaphore(f"{name}_{what}"))

        self.c, self.banks = c, banks
        self.x = [sb(f"x{k}", [P, CH, DIM]) for k in range(2)]
        self.xn = [sb(f"xn{k}", [P, DIM]) for k in range(2)]
        self.hi = [sb(f"xT_hi{k}", [P, CH, BT], F32R) for k in range(copies)]
        self.lo = [sb(f"xT_lo{k}", [P, CH, BT], F32R) for k in range(copies)]
        self.raw = sb("raw", [P, CH, 6])
        self.mv = sb("mv", [P, CH, 2])
        self.std = sb("std", [P, CH])
        self.rstd = sb("rstd", [P, CH])
        self.x_in = [sem(f"x_in{k}") for k in range(2)]
        self.raw_ready = sem("raw_ready")
        self.mv_ready = sem("mv_ready")
        self.std_ready = sem("std_ready")
        self.rstd_ready = sem("rstd_ready")
        self.xn_ready = sem("xn_ready")
        self.turned = sem("turned")
        self.hi_ready = sem("hi_ready")
        self.split = bank_free or sem("split")
        self.xn_used = xn_used

    def load(self, sp, b, k, n):
        if n == BT:
            sp.dma_start(self.x[k][:, :, :], self.c.x[bass.ds(b * BT, n), :].rearrange("(s p) d -> p s d", p=P)
                         ).then_inc(self.x_in[k], 16)
        else:
            sp.dma_start(self.x[k][0:n, 0, :], self.c.x[bass.ds(b * BT, n), :]).then_inc(self.x_in[k], 16)

    def stats(self, dve, b, k, n, s):
        if s == 0:
            dve.wait_ge(self.x_in[k], landed(b, k, 2))
        r = subtiles(n)[s]
        dve.bn_stats(self.raw[0:r, s, :], self.x[k][0:r, s, :]).then_inc(self.raw_ready, 1)

    def aggregate(self, dve, b, k, n):
        dve.wait_ge(self.raw_ready, b * CH + len(subtiles(n)))
        dve.sem_inc(self.c.passed, 1)
        for s, r in enumerate(subtiles(n)):
            op = dve.bn_aggr(self.mv[0:r, s, :], self.raw[0:r, s, :])
        op.then_inc(self.mv_ready, 1)

    def deviation(self, act, b, n):
        r, ns = subtiles(n)[-1], len(subtiles(n))
        act.wait_ge(self.mv_ready, b + 1)
        act.activation(self.std[0:r, 0:ns], self.mv[0:r, 0:ns, 1], ACT.Sqrt,
                       bias=self.c.eps[0:r, :]).then_inc(self.std_ready, 1)

    def invert(self, dve, b, n):
        r, ns = subtiles(n)[-1], len(subtiles(n))
        dve.wait_ge(self.std_ready, b + 1)
        dve.reciprocal(self.rstd[0:r, 0:ns], self.std[0:r, 0:ns]).then_inc(self.rstd_ready, 1)

    def normalise(self, dve, b, k, n, s):
        r = subtiles(n)[s]
        if s == 0:
            dve.wait_ge(self.rstd_ready, b + 1)
        if not isinstance(b, int) or b * CH + s >= 2:
            dve.wait_ge(self.turned, b * CH + (s - 1))
            if self.xn_used is not None:
                dve.wait_ge(self.xn_used, b * CH + (s - 1))
        dve.tensor_scalar(self.xn[s % 2][0:r, :], self.x[k][0:r, s, :], self.mv[0:r, s, 0:1],
                          self.rstd[0:r, s:s + 1], ALU.subtract, ALU.mult).then_inc(self.xn_ready, 1)

    def turn(self, pe, b, n, s, bank_uses):
        r = subtiles(n)[s]
        bank = self.banks[s % len(self.banks)]
        pe.wait_ge(self.xn_ready, b * CH + (s + 1))
        if bank_uses is not None:
            pe.wait_ge(self.split, bank_uses)
        for ch in range(CH):
            mm = pe.transpose(bank[:, ch * P:ch * P + r], self.xn[s % 2][0:r, ch * P:(ch + 1) * P],
                              self.c.ident[0:r, 0:r])
        mm.then_inc(self.turned, 1)

    def views(self, k, n, s):
        r = subtiles(n)[s]
        bank = self.banks[s % len(self.banks)][:, :].rearrange("p (c t) -> p c t", c=CH)[:, :, 0:r]
        return bank, self.hi[k][:, :, s * P:s * P + r], self.lo[k][:, :, s * P:s * P + r]

    def split_hi(self, act, b, k, n, s):
        act.wait_ge(self.turned, b * CH + (s + 1))
        bank, hi, lo = self.views(k, n, s)
        act.activation(hi, bank, ACT.Copy).then_inc(self.hi_ready, 1)

    def split_lo(self, dve, b, k, n, s):
        dve.wait_ge(self.hi_ready, b * CH + (s + 1))
        bank, hi, lo = self.views(k, n, s)
        dve.tensor_tensor(lo, bank, hi.bitcast(F32), ALU.subtract).then_inc(self.split, 1)

    def pairs(self, k, cut):
        return [(self.hi[k][:, c, cut], self.lo[k][:, c, cut]) for c in range(CH)]

    def first_on_dve(self, dve):
        for s in range(CH):
            self.stats(dve, 0, 0, BT, s)
        self.aggregate(dve, 0, 0, BT)
        self.invert(dve, 0, BT)
        for s in range(CH):
            self.normalise(dve, 0, 0, BT, s)
            if s >= 1:
                self.split_lo(dve, 0, 0, BT, s - 1)
        self.split_lo(dve, 0, 0, BT, CH - 1)


class Shared:
    pass


def constants_stage(nc, c):
    with ExitStack() as ctx:
        zero = ctx.enter_context(nc.sbuf_tensor("zero", [P, TROWS // P * ECOLS], F32))
        sel_f = ctx.enter_context(nc.sbuf_tensor("sel_f", [2 * HEADS, QK * P], F32))
        spare_i = ctx.enter_context(nc.sbuf_tensor("spare_i", [P, 1], I32))
        feat_i = ctx.enter_context(nc.sbuf_tensor("feat_i", [P, CH], I32))
        expert_i = ctx.enter_context(nc.sbuf_tensor("expert_i", [1, EXPERTS], I32))
        zero_set, filled, shaped, converted, tables_zero = c.finished = [
            ctx.enter_context(nc.semaphore(name))
            for name in ("zero_set", "filled", "shaped", "converted", "tables_zero")]
        block = ctx.enter_context(nc.Block())

        @block.sync
        def _(sp):
            sp.wait_ge(zero_set, 1)
            for t in range(TABLES):
                sp.dma_start(c.table[t].rearrange("(p a) c -> p (a c)", p=P), zero[:, :]).then_inc(tables_zero, 16)
            sp.dma_start(c.bias_v[:, :], c.b_v.partition_broadcast(P)).then_inc(tables_zero, 16)
            sp.dma_start(c.bias_qk[:, :], c.b_qk).then_inc(tables_zero, 16)
            sp.wait_ge(tables_zero, 16 * (TABLES + 2))

        @block.gpsimd
        def _(pool):
            pool.memset(c.ident[:, :], 0.0)
            pool.memset(sel_f[:, :], 0.0)
            pool.memset(c.row_sel[:, :], 0.0)
            pool.memset(c.upper[:, :], 1.0)
            pool.memset(c.same_token[:, :], 1.0).then_inc(filled, 1)
            pool.wait_ge(filled, 1)
            pool.affine_select(out=c.ident[:, :], in_=c.ident[:, :], compare_op=ALU.not_equal, fill=1.0, base=0,
                               pattern=[[-1, P]], channel_multiplier=1)
            pool.affine_select(out=sel_f[:, :], in_=sel_f[:, :], compare_op=ALU.not_equal, fill=1.0, base=0,
                               pattern=[[-HEADS, 2], [-2, CH], [-1, 2], [0, HDIM]], channel_multiplier=1)
            pool.affine_select(out=c.row_sel[:, :], in_=c.row_sel[:, :], compare_op=ALU.not_equal, fill=1.0,
                               base=0, pattern=[[0, GT], [-1, HEADS]], channel_multiplier=1)
            pool.affine_select(out=c.upper[:, :], in_=c.upper[:, :], compare_op=ALU.is_ge, fill=0.0, base=0,
                               pattern=[[1, P]], channel_multiplier=-1)
            pool.affine_select(out=c.same_token[:, :], in_=c.same_token[:, :], compare_op=ALU.is_ge, fill=0.0,
                               base=0, pattern=[[-HEADS, GT], [0, HEADS]], channel_multiplier=1).then_inc(filled, 1)
            pool.wait_ge(filled, 2)
            pool.affine_select(out=c.same_token[:, :], in_=c.same_token[:, :], compare_op=ALU.is_ge, fill=0.0,
                               base=HEADS - 1, pattern=[[HEADS, GT], [0, HEADS]], channel_multiplier=-1)
            pool.iota(spare_i[:, :], [[0, 1]], base=TOKENS - MID, channel_multiplier=1)
            pool.iota(feat_i[:, :], [[P, CH]], base=0, channel_multiplier=1)
            pool.iota(expert_i[:, :], [[1, EXPERTS]], base=0, channel_multiplier=0).then_inc(shaped, 1)

        @block.vector
        def _(dve):
            dve.memset(zero[:, :], 0.0).then_inc(zero_set, 1)
            dve.memset(c.eps[:, :], EPS)
            dve.memset(c.ones_row[:, :], 1.0)
            dve.wait_ge(shaped, 1)
            dve.tensor_copy(c.ident_r[:, :], c.ident[:, :])
            dve.tensor_copy(c.sel[:, :], sel_f[:, :])
            dve.tensor_copy(c.spare[:, :], spare_i[:, :])
            dve.tensor_copy(c.feat[:, :], feat_i[:, :])
            dve.tensor_copy(c.expert_no[:, :], expert_i[:, :]).then_inc(converted, 1)
            dve.wait_ge(converted, 1)


def project_stage(nc, c):
    with ExitStack() as ctx:
        def sb(what, shape, dt=F32):
            return ctx.enter_context(nc.sbuf_tensor(f"pr_{what}", shape, dt))

        def bank(what):
            return ctx.enter_context(nc.psum_tensor(f"pr_{what}", [P, BT], F32))

        def sem(what):
            return ctx.enter_context(nc.semaphore(f"pr_{what}"))

        W3 = 3 * DIM
        w_hi = sb("w_hi", [P, CH, W3], F32R)
        w_lo = sb("w_lo", [P, CH, W3], F32R)
        qk = [sb(f"qk{k}", [P, QK, BT]) for k in range(2)]
        v = sb("v", [P, CH, DIM])
        part = [sb(f"part{k}", [P, QK]) for k in range(2)]
        turn_banks = [bank(f"turn{k}") for k in range(2)]
        v_bank = [bank(f"v_bank{k}") for k in range(2)]
        qk_bank = [bank(f"qk_bank{k}") for k in range(2)]
        weights = Weights(ctx, nc, "pr_w", [
            (c.w_qkv[i * P:(i + 1) * P, a:a + W3 // 2], w_hi[:, i, a:a + W3 // 2], w_lo[:, i, a:a + W3 // 2])
            for i in range(CH) for a in (0, W3 // 2)], W3 // 2)
        norm = Norm(ctx, nc, c, "pr_norm", turn_banks, 2)
        edges = Edges(ctx, nc, c, "pr_edge", 0, 36, 12, P, 2, {t: 0 for t in range(TABLES)},
                      (bank("dst"), bank("sum")))
        v_mm, v_bank_free = sem("v_mm"), sem("v_bank_free")
        qk_mm, qk_bank_free = sem("qk_mm"), sem("qk_bank_free")
        v_stored, v_free = sem("v_stored"), sem("v_free")
        qk_stored, qk_free = sem("qk_stored"), sem("qk_free")
        added = sem("added")
        c.finished += [v_mm, v_bank_free, qk_mm, qk_bank_free, v_stored, v_free, qk_stored, qk_free, added]
        block = ctx.enter_context(nc.Block())

        def groups(n):
            return [("v", s) for s in range(len(subtiles(n)))] + [("qk", o) for o in range(QK)]

        def slots(n):
            return range(max(len(groups(n)), len(edges.quads_of(n))))

        @block.sync
        def _(sp):
            norm.load(sp, 0, 0, BT)
            norm.load(sp, 1, 1, BT)
            weights.load(sp)
            sp.sem_inc(v_free, 1)
            sp.sem_inc(qk_free, 2)
            edges.load_first(sp)

            def body(b, k, n, after):
                edges.load_next(sp, b, k, after)
                if after and not (isinstance(b, int) and b + 2 >= NB):
                    nn = TAIL if isinstance(b, int) and b + 2 == FULL else BT
                    sp.wait_ge(norm.xn_ready, (b + 1) * CH)
                    norm.load(sp, b + 2, k, nn)
                sp.wait_ge(v_bank_free, b * CH + (2 + len(subtiles(n))))
                if n == BT:
                    sp.dma_start(c.v[cols(b, n), :].rearrange("(s p) d -> p s d", p=P), v[:, :, :]
                                 ).then_inc(v_stored, 16)
                else:
                    sp.dma_start(c.v[cols(b, n), :], v[0:n, 0, :]).then_inc(v_stored, 16)
                sp.wait_ge(v_stored, b * 16 + 16)
                sp.sem_inc(v_free, 1)
                sp.wait_ge(qk_bank_free, b * QK + (2 + QK))
                sp.sem_inc(c.passed, 1)
                sp.dma_start(c.qk[:, cols(b, n)].rearrange("(o p) t -> p o t", p=P), qk[k][:, :, 0:n]
                             ).then_inc(qk_stored, 16)
                sp.wait_ge(qk_stored, b * 16 + 16)
                sp.sem_inc(qk_free, 1)

            over_blocks(sp, 2, body)

        @block.tensor
        def _(pe):
            for s in range(CH):
                norm.turn(pe, 0, BT, s, s - 1 if s >= 2 else None)
            weights.wait(pe)

            def body(b, k, n, after):
                pe.wait_ge(norm.split, b * CH + len(subtiles(n)))
                todo = groups(n)
                quads = edges.quads_of(n)
                for g in slots(n):
                    if g < len(quads):
                        edges.spread_dst(pe, b, k, n, g)
                    if g < len(todo):
                        kind, i = todo[g]
                        if kind == "v":
                            r = subtiles(n)[i]
                            pe.wait_ge(v_bank_free, b * CH + i + 1)
                            products(pe, v_bank[i % 2][0:r, :], norm.pairs(k, slice(i * P, i * P + r)),
                                     [(w_hi[:, ch, 2 * DIM:W3], w_lo[:, ch, 2 * DIM:W3]) for ch in range(CH)]
                                     ).then_inc(v_mm, 1)
                        else:
                            pe.wait_ge(qk_bank_free, b * QK + i + 1)
                            cut = slice(i * P, (i + 1) * P)
                            products(pe, qk_bank[i % 2][:, 0:n],
                                     [(w_hi[:, ch, cut], w_lo[:, ch, cut]) for ch in range(CH)],
                                     norm.pairs(k, slice(0, n))).then_inc(qk_mm, 1)
                    if g < len(quads):
                        edges.sum_tile(pe, b, k, n, g)
                    if after and 7 <= g < 7 + len(subtiles(after)):
                        norm.turn(pe, b + 1, after, g - 7, b * CH + (CH + g - 7 - 1))

            over_blocks(pe, 2, body)

        @block.scalar
        def _(act):
            norm.deviation(act, 0, BT)
            for s in range(CH):
                norm.split_hi(act, 0, 0, BT, s)
            weights.split_hi(act)
            act.sem_inc(qk_bank_free, 2)

            def body(b, k, n, after):
                todo = groups(n)
                for g in slots(n):
                    if g < len(todo) and todo[g][0] == "qk":
                        o = todo[g][1]
                        act.wait_ge(qk_mm, b * QK + o + 1)
                        if o == 0:
                            act.wait_ge(qk_free, b + 1)
                            act.wait_ge(added, b)
                        act.activation(qk[k][:, o, 0:n], qk_bank[o % 2][:, 0:n], ACT.Sigmoid,
                                       bias=c.bias_qk[:, o:o + 1], accum_out=part[k][:, o:o + 1]
                                       ).then_inc(qk_bank_free, 1)
                    if g < len(edges.quads_of(n)):
                        edges.keep(act, b, k, n, g)
                    if after and g == 4:
                        norm.deviation(act, b + 1, after)
                    if after and 7 <= g < 7 + len(subtiles(after)):
                        if g == 7:
                            act.wait_ge(qk_mm, b * QK)
                        norm.split_hi(act, b + 1, 1 - k, after, g - 7)

            over_blocks(act, 2, body)

        @block.vector
        def _(dve):
            edges.begin_dve(dve)
            norm.first_on_dve(dve)
            dve.sem_inc(v_bank_free, 2)
            dve.memset(c.sums[:, :], 0.0).then_inc(added, 1)
            weights.split_lo(dve)

            def body(b, k, n, after):
                todo = groups(n)
                edges.prepare(dve, b, k, n)
                for g in slots(n):
                    if g < len(edges.quads_of(n)):
                        edges.select(dve, b, k, n, g)
                    if g < len(todo) and todo[g][0] == "v":
                        s = todo[g][1]
                        r = subtiles(n)[s]
                        if s == 0:
                            dve.wait_ge(v_free, b + 1)
                        dve.wait_ge(v_mm, b * CH + s + 1)
                        dve.tensor_tensor(v[0:r, s, :], v_bank[s % 2][0:r, :], c.bias_v[0:r, :],
                                          ALU.add).then_inc(v_bank_free, 1)
                    if after and g < len(subtiles(after)):
                        norm.stats(dve, b + 1, 1 - k, after, g)
                    if after and g == 4:
                        norm.aggregate(dve, b + 1, 1 - k, after)
                    if after and g == 5:
                        norm.invert(dve, b + 1, after)
                    if after and 6 <= g < 6 + len(subtiles(after)):
                        norm.normalise(dve, b + 1, 1 - k, after, g - 6)
                    if after and 7 <= g < 7 + len(subtiles(after)):
                        norm.split_lo(dve, b + 1, 1 - k, after, g - 7)
                edges.rows(dve, b, k, n)
                dve.wait_ge(qk_bank_free, b * QK + (2 + QK))
                dve.wait_ge(added, b + 1)
                dve.tensor_tensor(c.sums[:, :], c.sums[:, :], part[k][:, :], ALU.add).then_inc(added, 1)

            over_blocks(dve, 2, body)

        @block.gpsimd
        def _(pool):
            edges.begin_pool(pool)
            over_blocks(pool, 2, lambda b, k, n, after: edges.scatter(pool, b, k, n))

    return edges


def head_matrix(dve, c, src, built):
    dve.memset(c.heads[:, :, :], 0.0).then_inc(built, 1)
    dve.wait_ge(built, 1)
    flat = c.heads[:, :, :].rearrange("p o r -> p (o r)")
    step = 2 * HEADS + 2
    for parity in range(2):
        rows = slice(parity * HDIM, (parity + 1) * HDIM)
        for side, at in ((0, 0), (1, CH * 2 * HEADS + HEADS)):
            a = at + parity
            op = dve.tensor_copy(flat[rows, a:a + (CH - 1) * step + 1:step],
                                 src[rows, (1 - side) * CH:(2 - side) * CH])
    op.then_inc(built, 1)
    return 2


def norms_stage(nc, c, before):
    with ExitStack() as ctx:
        def sb(what, shape, dt=F32):
            return ctx.enter_context(nc.sbuf_tensor(f"nm_{what}", shape, dt))

        def bank(what):
            return ctx.enter_context(nc.psum_tensor(f"nm_{what}", [P, BT], F32))

        def sem(what):
            return ctx.enter_context(nc.semaphore(f"nm_{what}"))

        U = 4
        R = 2 * HEADS
        qk = [sb(f"qk{k}", [P, QK, BT]) for k in range(U)]
        r_hi = [sb(f"r_hi{k}", [R, BT], F32R) for k in range(U)]
        r_lo = [sb(f"r_lo{k}", [R, BT], F32R) for k in range(U)]
        part = [sb(f"part{k}", [P, QK]) for k in range(U)]
        io_bank = bank("io")
        wide = [bank(f"wide{k}") for k in range(4)]
        edges = Edges(ctx, nc, c, "nm_edge", before.last_edge, 16, 2, P, U, before.total(),
                      (bank("dst"), bank("sum")))
        built, qk_in = sem("built"), [sem(f"qk_in{k}") for k in range(U)]
        io_mm, r_step, r_ready = sem("io_mm"), sem("r_step"), sem("r_ready")
        wide_mm, wide_free, added = sem("wide_mm"), sem("wide_free"), sem("added")
        block = ctx.enter_context(nc.Block())

        @block.sync
        def _(sp):
            def load(b, k, n):
                sp.dma_start(qk[k][:, :, 0:n], c.qk[:, cols(b, n)].rearrange("(o p) t -> p o t", p=P)
                             ).then_inc(qk_in[k], 16)

            load(0, 0, BT)
            load(1, 1, BT)
            edges.load_first(sp)

            def body(b, k, n, after):
                edges.load_next(sp, b, k, after)
                if not isinstance(b, int) or b + 2 < NB:
                    sp.wait_ge(wide_free, b * QK + 4)
                    load(b + 2, (k + 2) % U, TAIL if isinstance(b, int) and b + 2 == FULL else BT)

            over_blocks(sp, U, body)

        @block.tensor
        def _(pe):
            def io(b, k, n, o):
                if o == 0:
                    pe.wait_ge(qk_in[k], landed(b, k, U))
                mm = pe.matmul(io_bank[0:R, 0:n], c.heads[:, o, :], qk[k][:, o, 0:n],
                               start=o == 0, stop=o == QK - 1)
                if o == QK - 1:
                    mm.then_inc(io_mm, 1)

            pe.wait_ge(built, 2)
            for o in range(QK):
                io(0, 0, BT, o)

            def widen(b, k, n, o):
                if o == 0:
                    pe.wait_ge(r_ready, b + 1)
                pe.wait_ge(wide_free, b * QK + o + 1)
                for i, r in enumerate((r_hi[k], r_lo[k])):
                    mm = pe.matmul(wide[o % 4][:, 0:n], c.sel[:, o * P:(o + 1) * P], r[:, 0:n],
                                   start=i == 0, stop=i == 1)
                mm.then_inc(wide_mm, 1)

            def body(b, k, n, after):
                quads = edges.quads_of(n)
                for o in range(QK):
                    if after:
                        if o == 0:
                            pe.wait_ge(r_step, b * 2 + 1)
                        io(b + 1, (k + 1) % U, after, o)
                    if o % 2 == 0 and o // 2 < len(quads):
                        edges.spread_dst(pe, b, k, n, o // 2)
                    if o % 2 == 1 and o // 2 < len(quads):
                        edges.sum_tile(pe, b, k, n, o // 2)
                    if o >= CH:
                        widen(b, k, n, 2 * (o - CH))
                        widen(b, k, n, 2 * (o - CH) + 1)

            over_blocks(pe, U, body)

        @block.scalar
        def _(act):
            def body(b, k, n, after):
                for q in range(len(edges.quads_of(n))):
                    edges.keep(act, b, k, n, q)

            over_blocks(act, U, body)

        @block.vector
        def _(dve):
            edges.begin_dve(dve)
            head_matrix(dve, c, c.sums, built)
            dve.memset(c.shares[:, :], 0.0).then_inc(added, 1)
            dve.sem_inc(wide_free, 4)

            def invert(b, k, n):
                dve.wait_ge(io_mm, b + 1)
                dve.reciprocal(c.inverse[:, cols(b, n)], io_bank[0:R, 0:n]).then_inc(r_step, 1)
                dve.wait_ge(r_step, b * 2 + 1)
                dve.sem_inc(c.passed, 1)
                dve.tensor_copy(r_hi[k][:, 0:n], c.inverse[:, cols(b, n)]).then_inc(r_step, 1)
                dve.wait_ge(r_step, b * 2 + 2)
                dve.tensor_tensor(r_lo[k][:, 0:n], c.inverse[:, cols(b, n)], r_hi[k][:, 0:n].bitcast(F32),
                                  ALU.subtract).then_inc(r_ready, 1)

            invert(0, 0, BT)

            def body(b, k, n, after):
                quads = edges.quads_of(n)
                edges.prepare(dve, b, k, n)
                for q in range(len(quads)):
                    edges.select(dve, b, k, n, q)
                for o in range(QK):
                    dve.wait_ge(wide_mm, b * QK + o + 1)
                    dve.tensor_tensor_reduce(wide[o % 4][:, 0:n], qk[k][:, o, 0:n], wide[o % 4][:, 0:n], 1.0, 0.0,
                                             ALU.mult, ALU.add, part[k][:, o:o + 1]).then_inc(wide_free, 1)
                if after:
                    invert(b + 1, (k + 1) % U, after)
                edges.rows(dve, b, k, n)
                dve.wait_ge(wide_free, b * QK + (4 + QK))
                dve.wait_ge(added, b + 1)
                dve.tensor_tensor(c.shares[:, :], c.shares[:, :], part[k][:, :], ALU.add).then_inc(added, 1)

            over_blocks(dve, U, body)

        @block.gpsimd
        def _(pool):
            edges.begin_pool(pool)
            over_blocks(pool, U, lambda b, k, n, after: edges.scatter(pool, b, k, n))

    return edges


def scale_stage(nc, c, before):
    with ExitStack() as ctx:
        def sb(what, shape, dt=F32):
            return ctx.enter_context(nc.sbuf_tensor(f"sc_{what}", shape, dt))

        def bank(what):
            return ctx.enter_context(nc.psum_tensor(f"sc_{what}", [P, BT], F32))

        def sem(what):
            return ctx.enter_context(nc.semaphore(f"sc_{what}"))

        U = 4
        H = HEADS
        qk = [sb(f"qk{k}", [P, QK, BT]) for k in range(U)]
        gate = [sb(f"gate{k}", [H, BT]) for k in range(U)]
        ce = [sb(f"ce{k}", [H, 2, BT]) for k in range(U)]
        ce_hi = [sb(f"ce_hi{k}", [H, 2, BT], F32R) for k in range(U)]
        ce_lo = [sb(f"ce_lo{k}", [H, 2, BT], F32R) for k in range(U)]
        neg_max = [sb(f"neg_max{k}", [H, 1]) for k in range(U)]
        exp_sum = [sb(f"exp_sum{k}", [H, 1]) for k in range(U)]
        neg_maxs = sb("neg_maxs", [H, NB])
        exp_sums = sb("exp_sums", [H, NB])
        top = sb("top", [H, 1])
        rescale = sb("rescale", [H, NB])
        weighted = sb("weighted", [H, NB])
        total = sb("total", [H, 1])
        total_inv = sb("total_inv", [H, 1])
        factor = sb("factor", [H, NB])
        i_bank, o_bank = bank("i_bank"), bank("o_bank")
        wide = [bank(f"wide{k}") for k in range(4)]
        edges = Edges(ctx, nc, c, "sc_edge", before.last_edge, 16, 1, EDGES % P % 16, U, before.total(),
                      (bank("dst"), bank("sum")))
        assert edges.last_edge == EDGES
        built, qk_stored = sem("built"), sem("qk_stored")
        qk_in = [sem(f"qk_in{k}") for k in range(U)]
        io_mm, gated, max_ready, exp_ready = sem("io_mm"), sem("gated"), sem("max_ready"), sem("exp_ready")
        c_ready, hi_ready, ce_ready, noted = sem("c_ready"), sem("hi_ready"), sem("ce_ready"), sem("noted")
        wide_mm, wide_free = sem("wide_mm"), sem("wide_free")
        end_step, end_exp, end_mm = sem("end_step"), sem("end_exp"), sem("end_mm")
        block = ctx.enter_context(nc.Block())

        @block.sync
        def _(sp):
            def load(b, k, n):
                sp.dma_start(qk[k][:, :, 0:n], c.qk[:, cols(b, n)].rearrange("(o p) t -> p o t", p=P)
                             ).then_inc(qk_in[k], 16)

            load(0, 0, BT)
            load(1, 1, BT)
            edges.load_first(sp)

            def body(b, k, n, after):
                edges.load_next(sp, b, k, after)
                sp.wait_ge(qk_stored, b * 16)
                if not isinstance(b, int) or b + 2 < NB:
                    load(b + 2, (k + 2) % U, TAIL if isinstance(b, int) and b + 2 == FULL else BT)
                sp.wait_ge(wide_free, b * QK + (4 + QK))
                sp.dma_start(c.qk_scaled[:, cols(b, n)].rearrange("(o p) t -> p o t", p=P), qk[k][:, :, 0:n]
                             ).then_inc(qk_stored, 16)

            over_blocks(sp, U, body)
            sp.wait_ge(qk_stored, NB * 16)

        @block.tensor
        def _(pe):
            def io(b, k, n, o):
                if o == 0:
                    pe.wait_ge(qk_in[k], landed(b, k, U))
                    pe.wait_ge(gated, b)
                    pe.wait_ge(max_ready, b)
                    pe.wait_ge(exp_ready, b)
                out, row = (i_bank, 0) if o < CH else (o_bank, H)
                mm = pe.matmul(out[0:H, 0:n], c.heads[:, o, row:row + H], qk[k][:, o, 0:n],
                               start=o % CH == 0, stop=o % CH == CH - 1)
                if o % CH == CH - 1:
                    mm.then_inc(io_mm, 1)

            pe.wait_ge(built, 2)
            for o in range(QK):
                io(0, 0, BT, o)

            def widen(b, k, n, o):
                if o == 0:
                    pe.wait_ge(ce_ready, b + 1)
                pe.wait_ge(wide_free, b * QK + o + 1)
                for i, r in enumerate((ce_hi[k], ce_lo[k])):
                    mm = pe.matmul(wide[o % 4][:, 0:n], c.sel[0:H, (o % CH) * P:(o % CH + 1) * P],
                                   r[:, o // CH, 0:n], start=i == 0, stop=i == 1)
                mm.then_inc(wide_mm, 1)

            def body(b, k, n, after):
                quads = edges.quads_of(n)
                for o in range(QK):
                    if after:
                        io(b + 1, (k + 1) % U, after, o)
                    if o % 2 == 0 and o // 2 < len(quads):
                        edges.spread_dst(pe, b, k, n, o // 2)
                    if o % 2 == 1 and o // 2 < len(quads):
                        edges.sum_tile(pe, b, k, n, o // 2)
                    if o >= CH:
                        widen(b, k, n, 2 * (o - CH))
                        widen(b, k, n, 2 * (o - CH) + 1)

            over_blocks(pe, U, body)
            pe.wait_ge(end_step, 7)
            pe.matmul(i_bank[:, 0:NB], c.row_sel[:, :], factor[:, :], start=True, stop=True).then_inc(end_mm, 1)

        @block.scalar
        def _(act):
            def rows(b, k, n):
                act.wait_ge(io_mm, b * 2 + 1)
                act.activation(gate[k][:, 0:n], i_bank[0:H, 0:n], ACT.Sigmoid).then_inc(gated, 1)
                act.wait_ge(max_ready, b + 1)
                act.activation(ce[k][:, 1, 0:n], o_bank[0:H, 0:n], ACT.Exp, bias=neg_max[k][:, :],
                               accum_out=exp_sum[k][:, :]).then_inc(exp_ready, 1)

            rows(0, 0, BT)

            def body(b, k, n, after):
                for q in range(len(edges.quads_of(n))):
                    edges.keep(act, b, k, n, q)
                if after:
                    rows(b + 1, (k + 1) % U, after)

            over_blocks(act, U, body)
            act.wait_ge(end_step, 2)
            act.activation(rescale[:, :], neg_maxs[:, :], ACT.Exp, bias=top[:, :], scale=-1.0).then_inc(end_exp, 1)

        @block.vector
        def _(dve):
            edges.begin_dve(dve)
            head_matrix(dve, c, c.shares, built)
            dve.sem_inc(wide_free, 4)

            def rows(b, k, n):
                dve.wait_ge(io_mm, b * 2 + 2)
                dve.tensor_reduce(neg_max[k][:, :], o_bank[0:H, 0:n], AX.X, ALU.max, negate=True
                                  ).then_inc(max_ready, 1)
                dve.wait_ge(gated, b + 1)
                dve.tensor_tensor(ce[k][:, 0, 0:n], gate[k][:, 0:n], c.inverse[0:H, cols(b, n)], ALU.mult
                                  ).then_inc(c_ready, 1)
                dve.wait_ge(c_ready, b + 1)
                dve.wait_ge(exp_ready, b + 1)
                dve.tensor_copy(ce_hi[k][:, :, 0:n], ce[k][:, :, 0:n]).then_inc(hi_ready, 1)
                dve.wait_ge(hi_ready, b + 1)
                dve.tensor_tensor(ce_lo[k][:, :, 0:n], ce[k][:, :, 0:n], ce_hi[k][:, :, 0:n].bitcast(F32),
                                  ALU.subtract).then_inc(ce_ready, 1)
                dve.wait_ge(max_ready, b + 1)
                dve.tensor_copy(neg_maxs[:, bass.ds(b, 1)], neg_max[k][:, :])
                dve.tensor_copy(exp_sums[:, bass.ds(b, 1)], exp_sum[k][:, :]).then_inc(noted, 1)

            rows(0, 0, BT)

            def body(b, k, n, after):
                edges.prepare(dve, b, k, n)
                for q in range(len(edges.quads_of(n))):
                    edges.select(dve, b, k, n, q)
                for o in range(QK):
                    dve.wait_ge(wide_mm, b * QK + o + 1)
                    dve.tensor_tensor(qk[k][:, o, 0:n], qk[k][:, o, 0:n], wide[o % 4][:, 0:n], ALU.mult
                                      ).then_inc(wide_free, 1)
                if after:
                    rows(b + 1, (k + 1) % U, after)
                edges.rows(dve, b, k, n)

            over_blocks(dve, U, body)
            dve.wait_ge(noted, NB)
            dve.tensor_reduce(top[:, :], neg_maxs[:, :], AX.X, ALU.min).then_inc(end_step, 2)
            dve.wait_ge(end_exp, 1)
            dve.tensor_tensor(weighted[:, :], rescale[:, :], exp_sums[:, :], ALU.mult).then_inc(end_step, 1)
            dve.wait_ge(end_step, 3)
            dve.tensor_reduce(total[:, :], weighted[:, :], AX.X, ALU.add).then_inc(end_step, 1)
            dve.wait_ge(end_step, 4)
            dve.reciprocal(total_inv[:, :], total[:, :]).then_inc(end_step, 1)
            dve.wait_ge(end_step, 5)
            dve.tensor_scalar(factor[:, :], rescale[:, :], total_inv[:, :], None, ALU.mult).then_inc(end_step, 2)
            dve.wait_ge(end_mm, 1)
            dve.tensor_copy(c.factors[:, :], i_bank[:, 0:NB]).then_inc(end_step, 1)
            dve.wait_ge(end_step, 8)

        @block.gpsimd
        def _(pool):
            edges.begin_pool(pool)
            over_blocks(pool, U, lambda b, k, n, after: edges.scatter(pool, b, k, n))

    return edges


def mix_stage(nc, c):
    with ExitStack() as ctx:
        def sb(what, shape, dt=F32):
            return ctx.enter_context(nc.sbuf_tensor(f"mx_{what}", shape, dt))

        def bank(what):
            return ctx.enter_context(nc.psum_tensor(f"mx_{what}", [P, BT], F32))

        def sem(what):
            return ctx.enter_context(nc.semaphore(f"mx_{what}"))

        w1_hi = sb("w1_hi", [P, CH + 1, HID], F32R)
        w1_lo = sb("w1_lo", [P, CH + 1, HID], F32R)
        w2_hi = sb("w2_hi", [P, JH, DIM], F32R)
        w2_lo = sb("w2_lo", [P, JH, DIM], F32R)
        wo_hi = sb("wo_hi", [P, CH, DIM], F32R)
        wo_lo = sb("wo_lo", [P, CH, DIM], F32R)
        b1 = sb("b1", [P, JH])
        bias = sb("bias", [P, DIM])
        with ExitStack() as head:
            bias2 = head.enter_context(nc.sbuf_tensor("mx_bias2", [P, DIM], F32))
            bias_o = head.enter_context(nc.sbuf_tensor("mx_bias_o", [P, DIM], F32))
            bias_in = head.enter_context(nc.semaphore("mx_bias_in"))
            items = [(c.w1[i * P:min((i + 1) * P, DIM + EDIM), :], i, w1_hi, w1_lo) for i in range(CH + 1)]
            items += [(c.w2[i * P:(i + 1) * P, :], i, w2_hi, w2_lo) for i in range(JH)]
            items += [(c.w_out[i * P:(i + 1) * P, :], i, wo_hi, wo_lo) for i in range(CH)]
            weights = Weights(head, nc, "mx_w", [(src, hi[0:src.shape[0], i, :], lo[0:src.shape[0], i, :])
                                                 for src, i, hi, lo in items], HID)
            block = head.enter_context(nc.Block())

            @block.sync
            def _(sp):
                sp.dma_start(b1[:, :], c.b1).then_inc(bias_in, 16)
                sp.dma_start(bias2[:, :], c.b2.partition_broadcast(P)).then_inc(bias_in, 16)
                sp.dma_start(bias_o[:, :], c.b_out.partition_broadcast(P)).then_inc(bias_in, 16)
                weights.load(sp)

            @block.gpsimd
            def _(pool):
                for done in c.finished:
                    pool.sem_clear(done)

            @block.scalar
            def _(act):
                weights.split_hi(act)

            @block.vector
            def _(dve):
                weights.split_lo(dve)
                dve.wait_ge(bias_in, 48)
                dve.tensor_tensor(bias[:, :], bias2[:, :], bias_o[:, :], ALU.add)

        GROUPS = P // GT
        agg_raw = sb("agg_raw", [P, TABLES, CH, ECOLS])
        agg_sum = sb("agg_sum", [P, CH, ECOLS])
        agg_cnt = sb("agg_cnt", [P, CH])
        agg_inv = sb("agg_inv", [P, CH])
        agg_hi = sb("agg_hi", [EDIM, BT], F32R)
        agg_lo = sb("agg_lo", [EDIM, BT], F32R)
        qs = sb("qs", [P, HEADS, P])
        ks = sb("ks", [P, HEADS, P])
        kt = sb("kt", [P, P, HEADS])
        v = [sb(f"v{k}", [P, GROUPS, HDIM]) for k in range(2)]
        near = [sb(f"near{k}", [P, 4, P]) for k in range(2)]
        factor = [sb(f"factor{k}", [P, 1]) for k in range(2)]
        r_hi = [sb(f"r_hi{k}", [P, CH, P], F32R) for k in range(2)]
        r_lo = [sb(f"r_lo{k}", [P, CH, P], F32R) for k in range(2)]
        hid = sb("hid", [P, BT])
        h_hi = sb("h_hi", [P, JH, BT], F32R)
        h_lo = sb("h_lo", [P, JH, BT], F32R)
        x1 = [sb(f"x1_{k}", [P, DIM]) for k in range(2)]
        raw1, mv1, std1, rstd1 = sb("raw1", [P, 6]), sb("mv1", [P, 2]), sb("std1", [P, 1]), sb("rstd1", [P, 1])
        x1n = sb("x1n", [P, DIM])
        x1nT = sb("x1nT", [P, CH, P])
        part = [sb(f"part{k}", [P, CH]) for k in range(2)]
        turn_bank, r_bank = bank("turn"), bank("r")
        s_bank = [bank(f"s{k}") for k in range(2)]
        h_bank = [bank(f"h{k}") for k in range(2)]
        acc = [bank(f"acc{k}") for k in range(2)]
        turn_free = sem("turn_free")
        with_xn, base_ready = sem("with_xn"), sem("base_ready")
        norm = Norm(ctx, nc, c, "mx_norm", [turn_bank], 1, turn_free, with_xn)

        table_in, agg_step, agg_turned, agg_hi_ready = sem("table_in"), sem("agg_step"), sem("agg_turned"), sem("agg_hi_ready")
        qk_in, v_in = sem("qk_in"), [sem(f"v_in{k}") for k in range(2)]
        factor_ready = sem("factor_ready")
        kt_ready = sem("kt_ready")
        scored, near_ready, mixed = sem("scored"), sem("near_ready"), sem("mixed")
        r_hi_ready, r_ready = sem("r_hi_ready"), sem("r_ready")
        h_mm, hid_ready, h_hi_ready, h_ready = sem("h_mm"), sem("hid_ready"), sem("h_hi_ready"), sem("h_ready")
        acc_mm, x1_ready, x1_stored, x1_free = sem("acc_mm"), sem("x1_ready"), sem("x1_stored"), sem("x1_free")
        raw1_ready, mv1_ready, std1_ready, rstd1_ready = sem("raw1_ready"), sem("mv1_ready"), sem("std1_ready"), sem("rstd1_ready")
        x1n_ready, x1n_turned, x1nT_ready, x1nT_stored = sem("x1n_ready"), sem("x1n_turned"), sem("x1nT_ready"), sem("x1nT_stored")
        parts_added = sem("parts_added")
        block = ctx.enter_context(nc.Block())

        AHEAD = 2
        STEPS = BT // (4 * GT)
        SLOTS = JH + CH
        S_SLOT = (0, 1, 2, 3, 6, 7, 8, 9)
        V_SLOT = (1, 2, 3, 4, 7, 8, 9, 10)

        def groups(n, step):
            t0 = step * 4 * GT
            return [(t // P, t % P, min(GT, n - t)) for t in range(t0, min(t0 + 4 * GT, n), GT)]

        def steps(n):
            return [s for s in range(STEPS) if groups(n, s)]

        def last_step(n, sub):
            return max(s for s in steps(n) if groups(n, s)[0][0] == sub)

        def turns(after):
            return CH + (len(subtiles(after)) + 1 if after else 0)

        def turns_before(b):
            if isinstance(b, int) and b == NB - 1:
                return CH + 1 + (FULL - 1) * turns(BT) + turns(TAIL)
            return b * turns(BT) + (CH + 1)

        def turning(n, after):
            subs = len(subtiles(n))
            order = []
            if after:
                order += [(JH, "x", s) for s in range(len(subtiles(after)))][:2]
                order += [(JH + 1, "x1", 0)] if subs > 1 else []
                order += [(JH + 1, "x", s) for s in range(2, len(subtiles(after)))]
                order += [(JH + 1, "agg", 0)]
                order += [(JH + s + 1, "x1", s) for s in range(1, subs - 1)]
            order += [(JH + subs, "x1", subs - 1)]
            if not after and subs > 1:
                raise ValueError("the last block has one subtile")
            return order

        def act_turned(act, b, k, n, after, item, use):
            _, kind, s = item
            if kind == "x":
                norm.split_hi(act, b + 1, 0, after, s)
            elif kind == "agg":
                act.wait_ge(agg_turned, b + 2)
                act.activation(agg_hi[:, 0:after], turn_bank[0:EDIM, 0:after], ACT.Copy).then_inc(agg_hi_ready, 1)
            else:
                r = subtiles(n)[s]
                act.wait_ge(x1n_turned, b * CH + (s + 1))
                act.wait_ge(x1nT_stored, b * (16 * CH) + 16 * s)
                act.wait_ge(parts_added, b * CH + s)
                for ch in range(CH):
                    op = act.activation(x1nT[:, ch, 0:r], turn_bank[:, ch * P:ch * P + r], ACT.Copy,
                                        accum_out=part[s % 2][:, ch:ch + 1])
                op.then_inc(turn_free, 1)

        @block.sync
        def _(sp):
            def load_unit(b, n, u):
                pieces = subtiles(n)[2 * u:2 * u + 2]
                for half, r in enumerate(pieces):
                    at = b * BT + (2 * u + half) * P
                    for dst, row in ((qs, 0), (ks, DIM)):
                        sp.dma_start(dst[half * HDIM:(half + 1) * HDIM, :, 0:r],
                                     c.qk_scaled[row:row + DIM, bass.ds(at, r)].rearrange("(h d) t -> d h t", d=HDIM)
                                     ).then_inc(qk_in, 16)

            def load_v(b, n, s):
                r = subtiles(n)[s]
                rows = c.v.rearrange("t (h e) -> (t h) e", h=HEADS)
                at = b * (BT * HEADS) + s * P * HEADS
                full = r // GT
                sp.dma_start(v[s % 2][:, 0:full, :],
                             rows[bass.ds(at, full * P), :].rearrange("(g p) e -> p g e", p=P)
                             ).then_inc(v_in[s % 2], 16)
                if r % GT:
                    left = (r % GT) * HEADS
                    sp.dma_start(v[s % 2][0:left, full, :], rows[bass.ds(at + full * P, left), :]
                                 ).then_inc(v_in[s % 2], 16)

            def load_tables(b, n):
                for t in range(TABLES):
                    if n == BT:
                        sp.dma_start(agg_raw[:, t, :, :], c.table[t][bass.ds(b * BT, n), :]
                                     .rearrange("(s p) e -> p s e", p=P)).then_inc(table_in, 16)
                    else:
                        sp.dma_start(agg_raw[0:n, t, 0, :], c.table[t][bass.ds(b * BT, n), :]
                                     ).then_inc(table_in, 16)

            norm.load(sp, 0, 0, BT)
            load_tables(0, BT)
            load_unit(0, BT, 0)
            load_v(0, BT, 0)
            load_v(0, BT, 1)

            def body(b, k, n, after):
                subs = len(subtiles(n))
                if after:
                    sp.wait_ge(acc_mm, b * CH + AHEAD)
                    sp.wait_ge(x1_ready, b * CH + AHEAD)
                    norm.load(sp, b + 1, 1 - k, after)
                    sp.wait_ge(agg_step, b * 4 + 4)
                    load_tables(b + 1, after)
                if subs > 2:
                    sp.wait_ge(scored, b * STEPS + 4)
                    load_unit(b, n, 1)
                    for s in (2, 3):
                        sp.wait_ge(mixed, b * STEPS + (AHEAD + last_step(n, s - 2) + 1))
                        load_v(b, n, s)
                if after:
                    sp.wait_ge(scored, b * STEPS + len(steps(n)))
                    sp.sem_inc(c.passed, 1)
                    load_unit(b + 1, after, 0)
                    for s in range(min(2, len(subtiles(after)))):
                        sp.wait_ge(mixed, b * STEPS + (AHEAD + last_step(n, subs - 2 + s) + 1))
                        load_v(b + 1, after, s)

            over_blocks(sp, 2, body)

        @block.tensor
        def _(pe):
            def turn_agg(b, n, use):
                pe.wait_ge(agg_step, b * 4 + 4)
                pe.wait_ge(turn_free, use)
                pe.sem_inc(c.passed, 1)
                for s, r in enumerate(subtiles(n)):
                    mm = pe.transpose(turn_bank[0:EDIM, s * P:s * P + r], agg_sum[0:r, s, 0:EDIM], c.ident[0:r, 0:r])
                mm.then_inc(agg_turned, 1)

            def turn_x1(b, n, s, use):
                r = subtiles(n)[s]
                pe.wait_ge(x1n_ready, b * CH + (s + 1))
                pe.wait_ge(turn_free, use)
                for ch in range(CH):
                    mm = pe.transpose(turn_bank[:, ch * P:ch * P + r], x1n[0:r, ch * P:(ch + 1) * P],
                                      c.ident[0:r, 0:r])
                mm.then_inc(x1n_turned, 1)

            def scores(b, n, step):
                gs = groups(n, step)
                if step % 4 == 0:
                    pe.wait_ge(kt_ready, b * 2 + step // 4 + 1)
                pe.wait_ge(near_ready, b * STEPS + step + 1)
                for j, (sub, t, w) in enumerate(gs):
                    half = slice((sub % 2) * HDIM, (sub % 2 + 1) * HDIM)
                    mm = pe.matmul(s_bank[step % 2][0:w * HEADS, j * P:j * P + w * HEADS],
                                   kt[half, t:t + w, :].rearrange("d t h -> d (t h)"),
                                   qs[half, :, t:t + w].rearrange("d h t -> d t h"), start=True, stop=True)
                mm.then_inc(scored, 1)

            def mix(b, n, step):
                gs = groups(n, step)
                sub = gs[0][0]
                pe.wait_ge(near_ready, b * STEPS + (AHEAD + step + 1))
                if step == last_step(n, sub) - len([s for s in steps(n) if groups(n, s)[0][0] == sub]) + 1:
                    pe.wait_ge(r_ready, b * CH + sub)
                    loads = 2 if n % GT else 1
                    pe.wait_ge(v_in[sub % 2], b * 32 + 16 * (sub // 2) + 16 * loads)
                for j, (_, t, w) in enumerate(gs):
                    g = t // GT
                    rows = w * HEADS
                    view = near[step % 2][0:rows, j, 0:rows].rearrange("p (t h) -> p t h", h=HEADS)
                    for parity in range(2):
                        out = r_bank[parity * HDIM:(parity + 1) * HDIM, :].rearrange("p (c t) -> p t c", c=CH)
                        mm = pe.matmul(out[:, t:t + w, :], v[sub % 2][0:rows, g, :], view[:, :, parity::2],
                                       start=True, stop=True)
                mm.then_inc(mixed, 1)

            def hidden(b, n, j):
                cut = slice(j * P, (j + 1) * P)
                pe.wait_ge(hid_ready, b * JH + j + 1)
                products(pe, h_bank[j % 2][:, 0:n],
                         [(w1_hi[:, ch, cut], w1_lo[:, ch, cut]) for ch in range(CH)]
                         + [(w1_hi[0:EDIM, CH, cut], w1_lo[0:EDIM, CH, cut])],
                         norm.pairs(0, slice(0, n)) + [(agg_hi[:, 0:n], agg_lo[:, 0:n])]).then_inc(h_mm, 1)

            def output(b, n, s):
                r = subtiles(n)[s]
                cut = slice(s * P, s * P + r)
                pe.wait_ge(h_ready, b * JH + JH)
                pe.wait_ge(x1_ready, b * CH + s + 1)
                products(pe, acc[s % 2][0:r, :], [(h_hi[:, j, cut], h_lo[:, j, cut]) for j in range(JH)],
                         [(w2_hi[:, j, :], w2_lo[:, j, :]) for j in range(JH)], last=False)
                pe.wait_ge(r_ready, b * CH + (s + 1))
                products(pe, acc[s % 2][0:r, :], [(r_hi[s % 2][:, ch, 0:r], r_lo[s % 2][:, ch, 0:r]) for ch in range(CH)],
                         [(wo_hi[:, ch, :], wo_lo[:, ch, :]) for ch in range(CH)], first=False).then_inc(acc_mm, 1)

            pe.sem_inc(mixed, AHEAD)
            pe.sem_inc(acc_mm, AHEAD)
            for s in range(CH):
                norm.turn(pe, 0, BT, s, s)
            turn_agg(0, BT, CH)

            def body(b, k, n, after):
                pe.wait_ge(turn_free, turns_before(b))
                use = turns_before(b)
                order = turning(n, after)
                subs = len(subtiles(n))
                early = subs == 1
                if early:
                    for step in steps(n):
                        scores(b, n, step)
                        mix(b, n, step)
                for slot in range(JH + subs):
                    if not early:
                        for step in steps(n):
                            if S_SLOT[step] == slot:
                                scores(b, n, step)
                            if V_SLOT[step] == slot:
                                mix(b, n, step)
                    if slot < JH:
                        hidden(b, n, slot)
                    else:
                        output(b, n, slot - JH)
                    while order and order[0][0] == slot:
                        _, kind, s = order.pop(0)
                        if kind == "x":
                            norm.turn(pe, b + 1, after, s, use)
                        elif kind == "agg":
                            turn_agg(b + 1, after, use)
                        else:
                            turn_x1(b, n, s, use)
                        use = use + 1
                while order:
                    turn_x1(b, n, order.pop(0)[2], use)
                    use = use + 1

            over_blocks(pe, 2, body)

        @block.scalar
        def _(act):
            act.sem_inc(hid_ready, AHEAD)
            norm.deviation(act, 0, BT)
            for s in range(CH):
                norm.split_hi(act, 0, 0, BT, s)
            act.wait_ge(agg_turned, 1)
            act.activation(agg_hi[:, :], turn_bank[0:EDIM, :], ACT.Copy).then_inc(agg_hi_ready, 1)

            def by_token(b, n, u):
                halves = len(subtiles(n)[2 * u:2 * u + 2])
                rows, r = halves * HDIM, subtiles(n)[2 * u]
                act.wait_ge(qk_in, b * 128 + (64 * u + 32 * halves))
                act.activation(kt[0:rows, 0:r, :], ks[0:rows, :, 0:r].rearrange("d h t -> d t h"), ACT.Copy
                               ).then_inc(kt_ready, 1)

            by_token(0, BT, 0)

            def split_r(b, n, s):
                r = subtiles(n)[s]
                act.wait_ge(mixed, b * STEPS + (AHEAD + last_step(n, s) + 1))
                act.wait_ge(acc_mm, b * CH + s + 1)
                bank = r_bank[:, :].rearrange("p (c t) -> p c t", c=CH)[:, :, 0:r]
                act.activation(r_hi[s % 2][:, :, 0:r], bank, ACT.Copy).then_inc(r_hi_ready, 1)

            def deviation1(b, n, s):
                r = subtiles(n)[s]
                act.wait_ge(mv1_ready, b * CH + (s + 1))
                act.activation(std1[0:r, :], mv1[0:r, 1:2], ACT.Sqrt, bias=c.eps[0:r, :]).then_inc(std1_ready, 1)

            def body(b, k, n, after):
                order = turning(n, after)
                subs = len(subtiles(n))
                if subs == 1:
                    split_r(b, n, 0)
                for slot in range(JH + subs):
                    if subs > 1:
                        for s in range(subs):
                            if V_SLOT[last_step(n, s)] == slot:
                                split_r(b, n, s)
                    if slot < JH:
                        act.wait_ge(h_mm, b * JH + slot + 1)
                        act.wait_ge(h_ready, b * JH + slot)
                        act.activation(hid[:, 0:n], h_bank[slot % 2][:, 0:n], ACT.Relu,
                                       bias=b1[:, slot:slot + 1]).then_inc(hid_ready, 1)
                        act.wait_ge(hid_ready, b * JH + (AHEAD + slot + 1))
                        if slot == 0:
                            act.wait_ge(acc_mm, b * CH + AHEAD)
                        act.activation(h_hi[:, slot, 0:n], hid[:, 0:n], ACT.Copy).then_inc(h_hi_ready, 1)
                        if after and slot == 4:
                            norm.deviation(act, b + 1, after)
                        if subs > 2 and slot == 4:
                            act.wait_ge(scored, b * STEPS + 4)
                            by_token(b, n, 1)
                    else:
                        deviation1(b, n, slot - JH)
                    if after and slot == 10:
                        act.wait_ge(scored, b * STEPS + STEPS)
                        by_token(b + 1, after, 0)
                    while order and order[0][0] == slot:
                        act_turned(act, b, k, n, after, order.pop(0), None)
                while order:
                    act_turned(act, b, k, n, after, order.pop(0), None)

            over_blocks(act, 2, body)

        @block.vector
        def _(dve):
            def divide_sums(b, n):
                r, ns = subtiles(n)[-1], len(subtiles(n))
                dve.wait_ge(table_in, b * (16 * TABLES) + 16 * TABLES)
                dve.tensor_reduce(agg_sum[0:r, 0:ns, :], agg_raw[0:r, :, 0:ns, :].rearrange("p t s e -> p s e t"),
                                  AX.X, ALU.add).then_inc(agg_step, 1)
                dve.wait_ge(agg_step, b * 4 + 1)
                dve.tensor_scalar(agg_cnt[0:r, 0:ns], agg_sum[0:r, 0:ns, EDIM], 1.0, None, ALU.max).then_inc(agg_step, 1)
                dve.wait_ge(agg_step, b * 4 + 2)
                dve.reciprocal(agg_inv[0:r, 0:ns], agg_cnt[0:r, 0:ns]).then_inc(agg_step, 1)
                dve.wait_ge(agg_step, b * 4 + 3)
                dve.tensor_tensor(agg_sum[0:r, 0:ns, 0:EDIM], agg_sum[0:r, 0:ns, 0:EDIM],
                                  agg_inv[0:r, 0:ns].unsqueeze(2).to_broadcast([r, ns, EDIM]),
                                  ALU.mult).then_inc(agg_step, 1)

            def split_agg(b, n):
                dve.wait_ge(agg_hi_ready, b + 1)
                dve.tensor_tensor(agg_lo[:, 0:n], turn_bank[0:EDIM, 0:n], agg_hi[:, 0:n].bitcast(F32),
                                  ALU.subtract).then_inc(turn_free, 1)

            def take_factor(b, k):
                dve.tensor_copy(factor[k][:, :], c.factors[:, bass.ds(b, 1)]).then_inc(factor_ready, 1)

            def neighbours(b, k, n, step):
                gs = groups(n, step)
                if step == 0:
                    dve.wait_ge(factor_ready, b + 1)
                dve.wait_ge(scored, b * STEPS + step + 1)
                dve.wait_ge(mixed, b * STEPS + step + 1)
                whole = len([g for g in gs if g[2] == GT])
                if whole:
                    op = dve.scalar_tensor_tensor(
                        out=near[step % 2][:, 0:whole, :],
                        in0=s_bank[step % 2][:, 0:whole * P].rearrange("p (j f) -> p j f", f=P),
                        scalar=factor[k][:, :], in1=c.same_token[:, :].unsqueeze(1).to_broadcast([P, whole, P]),
                        op0=ALU.mult, op1=ALU.mult)
                if whole < len(gs):
                    rows = gs[-1][2] * HEADS
                    op = dve.scalar_tensor_tensor(
                        out=near[step % 2][0:rows, whole, 0:rows], in0=s_bank[step % 2][0:rows, whole * P:whole * P + rows],
                        scalar=factor[k][0:rows, :], in1=c.same_token[0:rows, 0:rows], op0=ALU.mult, op1=ALU.mult)
                op.then_inc(near_ready, 1)

            def split_r(b, n, s):
                r = subtiles(n)[s]
                dve.wait_ge(r_hi_ready, b * CH + (s + 1))
                bank = r_bank[:, :].rearrange("p (c t) -> p c t", c=CH)[:, :, 0:r]
                dve.tensor_tensor(r_lo[s % 2][:, :, 0:r], bank, r_hi[s % 2][:, :, 0:r].bitcast(F32),
                                  ALU.subtract).then_inc(r_ready, 1)

            def finish(b, k, n, s):
                r = subtiles(n)[s]
                at = b * CH + (s + 1)
                dve.wait_ge(acc_mm, at + AHEAD)
                dve.wait_ge(base_ready, at)
                dve.wait_ge(x1_free, b * CH + s + 1)
                dve.tensor_tensor(x1[s % 2][0:r, :], acc[s % 2][0:r, :], norm.x[k][0:r, s, :], ALU.add
                                  ).then_inc(x1_ready, 1)
                dve.wait_ge(x1_ready, at + AHEAD)
                dve.bn_stats(raw1[0:r, :], x1[s % 2][0:r, :]).then_inc(raw1_ready, 1)
                dve.wait_ge(raw1_ready, at)
                dve.sem_inc(c.passed, 1)
                dve.bn_aggr(mv1[0:r, :], raw1[0:r, :]).then_inc(mv1_ready, 1)
                dve.wait_ge(std1_ready, at)
                dve.reciprocal(rstd1[0:r, :], std1[0:r, :]).then_inc(rstd1_ready, 1)
                dve.wait_ge(rstd1_ready, at)
                dve.wait_ge(x1n_turned, b * CH + s)
                dve.tensor_scalar(x1n[0:r, :], x1[s % 2][0:r, :], mv1[0:r, 0:1], rstd1[0:r, :],
                                  ALU.subtract, ALU.mult).then_inc(x1n_ready, 1)

            def add_part(b, n, s, use):
                dve.wait_ge(turn_free, use + 1)
                dve.wait_ge(parts_added, b * CH + (s + 1))
                dve.tensor_tensor(c.token_sum[:, :], c.token_sum[:, :], part[s % 2][:, :], ALU.add
                                  ).then_inc(parts_added, 1)

            dve.sem_inc(near_ready, AHEAD)
            dve.sem_inc(x1_ready, AHEAD)
            dve.memset(c.token_sum[:, :], 0.0).then_inc(parts_added, 1)
            norm.first_on_dve(dve)
            divide_sums(0, BT)
            split_agg(0, BT)
            take_factor(0, 0)

            def body(b, k, n, after):
                order = turning(n, after)
                use = turns_before(b)
                subs = len(subtiles(n))
                if subs == 1:
                    for step in steps(n):
                        neighbours(b, k, n, step)
                    split_r(b, n, 0)
                for slot in range(JH + subs):
                    if subs > 1:
                        for step in steps(n):
                            if S_SLOT[step] == slot:
                                neighbours(b, k, n, step)
                        for s in range(subs):
                            if V_SLOT[last_step(n, s)] == slot:
                                split_r(b, n, s)
                    if slot < JH:
                        dve.wait_ge(h_hi_ready, b * JH + slot + 1)
                        dve.tensor_tensor(h_lo[:, slot, 0:n], hid[:, 0:n], h_hi[:, slot, 0:n].bitcast(F32),
                                          ALU.subtract).then_inc(h_ready, 1)
                    else:
                        finish(b, k, n, slot - JH)
                    if after and slot < len(subtiles(after)):
                        norm.stats(dve, b + 1, 1 - k, after, slot)
                    if after and slot == 4:
                        norm.aggregate(dve, b + 1, 1 - k, after)
                    if after and slot == 5:
                        norm.invert(dve, b + 1, after)
                        take_factor(b + 1, 1 - k)
                        for s in range(min(2, len(subtiles(after)))):
                            norm.normalise(dve, b + 1, 1 - k, after, s)
                    if after and slot == 6:
                        divide_sums(b + 1, after)
                    while order and order[0][0] == slot:
                        _, kind, s = order.pop(0)
                        if kind == "x":
                            norm.split_lo(dve, b + 1, 0, after, s)
                            if s + 2 < len(subtiles(after)):
                                norm.normalise(dve, b + 1, 1 - k, after, s + 2)
                        elif kind == "agg":
                            split_agg(b + 1, after)
                        else:
                            add_part(b, n, s, use)
                        use = use + 1
                while order:
                    add_part(b, n, order.pop(0)[2], use)
                    use = use + 1

            over_blocks(dve, 2, body)

        @block.gpsimd
        def _(pool):
            def bases(b, k, n):
                for s, r in enumerate(subtiles(n)):
                    at = b * CH + (s + 1)
                    pool.wait_ge(norm.xn_ready, at)
                    pool.tensor_tensor(norm.x[k][0:r, s, :], norm.x[k][0:r, s, :], norm.xn[s % 2][0:r, :], ALU.add
                                       ).then_inc(with_xn, 1)
                    pool.wait_ge(with_xn, at)
                    pool.tensor_tensor(norm.x[k][0:r, s, :], norm.x[k][0:r, s, :], bias[0:r, :], ALU.add
                                       ).then_inc(base_ready, 1)

            pool.sem_inc(x1_free, AHEAD)
            bases(0, 0, BT)

            def body(b, k, n, after):
                use = turns_before(b)
                order = turning(n, after)
                store = {s: use + i + 1 for i, (_, kind, s) in enumerate(order) if kind == "x1"}
                if after:
                    bases(b + 1, 1 - k, after)
                for s, r in enumerate(subtiles(n)):
                    at = b * BT + s * P
                    pool.wait_ge(x1_ready, b * CH + (AHEAD + s + 1))
                    pool.dma_start(c.x1[bass.ds(at, r), :], x1[s % 2][0:r, :]).then_inc(x1_stored, 16)
                    pool.wait_ge(turn_free, store[s])
                    pool.dma_start(c.x1n[:, bass.ds(at, r)].rearrange("(c p) t -> p c t", p=P), x1nT[:, :, 0:r]
                                   ).then_inc(x1nT_stored, 16)
                    pool.wait_ge(x1_stored, b * (16 * CH) + 16 * (s + 1))
                    pool.sem_inc(x1_free, 1)
                    pool.wait_ge(x1nT_stored, b * (16 * CH) + 16 * (s + 1))

            over_blocks(pool, 2, body)


def expert_stage(nc, c):
    with ExitStack() as ctx:
        def sb(what, shape, dt=F32):
            return ctx.enter_context(nc.sbuf_tensor(f"ex_{what}", shape, dt))

        def bank(what):
            return ctx.enter_context(nc.psum_tensor(f"ex_{what}", [P, BT], F32))

        def sem(what):
            return ctx.enter_context(nc.semaphore(f"ex_{what}"))

        w_gate = sb("w_gate", [P, CH, EXPERTS])
        b_gate = sb("b_gate", [1, EXPERTS])
        mean = sb("mean", [P, CH])
        logit, prob_e, prob = sb("logit", [1, EXPERTS]), sb("prob_e", [1, EXPERTS]), sb("prob", [1, EXPERTS])
        neg_top, total, total_inv = sb("neg_top", [1, 1]), sb("total", [1, 1]), sb("total_inv", [1, 1])
        other, rank = sb("other", [1, EXPERTS]), sb("rank", [1, EXPERTS])
        pick = sb("pick", [1, 2])
        pick_all = sb("pick_all", [P, 2])
        row_f = sb("row_f", [P, CH])
        row = sb("row", [P, CH], I32)
        expert = sb("expert", [P, 1], I32)
        w_raw = sb("w_raw", [P, CH, DIM])
        w_hi = sb("w_hi", [P, CH, DIM], F32R)
        w_lo = sb("w_lo", [P, CH, DIM], F32R)
        b_raw = sb("b_raw", [P, DIM])
        xT = [sb(f"xT{k}", [P, CH, BT]) for k in range(2)]
        xT_hi = [sb(f"xT_hi{k}", [P, CH, BT], F32R) for k in range(2)]
        xT_lo = [sb(f"xT_lo{k}", [P, CH, BT], F32R) for k in range(2)]
        x1 = [sb(f"x1_{k}", [P, CH, DIM]) for k in range(2)]
        y = [sb(f"y{k}", [P, DIM]) for k in range(2)]
        done = [sb(f"done{k}", [P, CH, DIM]) for k in range(2)]
        small, wide = bank("small"), bank("wide")
        BANKS = 4
        y_bank = [bank(f"y_bank{k}") for k in range(BANKS)]
        gate_in, gate_step, gate_mm, gate_exp = sem("gate_in"), sem("gate_step"), sem("gate_mm"), sem("gate_exp")
        gathered, w_hi_ready, w_ready = sem("gathered"), sem("w_hi_ready"), sem("w_ready")
        x_in, x1_in = [sem(f"x_in{k}") for k in range(2)], [sem(f"x1_in{k}") for k in range(2)]
        xT_hi_ready, xT_ready = sem("xT_hi_ready"), sem("xT_ready")
        y_mm, y_ready, y_done, stored, done_free = sem("y_mm"), sem("y_ready"), sem("y_done"), sem("stored"), sem("done_free")
        block = ctx.enter_context(nc.Block())

        @block.sync
        def _(sp):
            sp.dma_start(w_gate[:, :, :], c.w_gate.rearrange("(c p) e -> p c e", p=P)).then_inc(gate_in, 16)
            sp.dma_start(b_gate[:, :], c.b_gate.rearrange("(a e) -> a e", a=1)).then_inc(gate_in, 16)

            def load(b, k, n):
                sp.dma_start(xT[k][:, :, 0:n], c.x1n[:, cols(b, n)].rearrange("(c p) t -> p c t", p=P)
                             ).then_inc(x_in[k], 16)
                if n == BT:
                    sp.dma_start(x1[k][:, :, :], c.x1[cols(b, n), :].rearrange("(s p) d -> p s d", p=P)
                                 ).then_inc(x1_in[k], 16)
                else:
                    sp.dma_start(x1[k][0:n, 0, :], c.x1[cols(b, n), :]).then_inc(x1_in[k], 16)

            load(0, 0, BT)
            load(1, 1, BT)

            def body(b, k, n, after):
                ns = len(subtiles(n))
                sp.wait_ge(y_done, b * CH + ns)
                if not isinstance(b, int) or b + 2 < NB:
                    load(b + 2, k, TAIL if isinstance(b, int) and b + 2 == FULL else BT)
                sp.wait_ge(stored, b * 16)
                sp.sem_inc(done_free, 1)
                if n == BT:
                    sp.dma_start(c.out[cols(b, n), :].rearrange("(s p) d -> p s d", p=P), done[k][:, :, :]
                                 ).then_inc(stored, 16)
                else:
                    sp.dma_start(c.out[cols(b, n), :], done[k][0:n, 0, :]).then_inc(stored, 16)

            over_blocks(sp, 2, body)
            sp.wait_ge(stored, 16 * NB)

        @block.gpsimd
        def _(pool):
            pool.wait_ge(gate_step, 13)
            for ch in range(CH):
                pool.indirect_dma_start(w_raw[:, ch, :], None, c.w_exp,
                                        bass.IndirectOffsetOnAxis(ap=row[:, ch:ch + 1], axis=0),
                                        bounds_check=EXPERTS * DIM - 1).then_inc(gathered, 16)
            pool.indirect_dma_start(b_raw[:, :], None, c.b_exp,
                                    bass.IndirectOffsetOnAxis(ap=expert[:, :], axis=0),
                                    bounds_check=EXPERTS - 1).then_inc(gathered, 16)

        @block.tensor
        def _(pe):
            pe.wait_ge(gate_in, 32)
            pe.wait_ge(gate_step, 1)
            for ch in range(CH):
                mm = pe.matmul(small[0:1, 0:EXPERTS], mean[:, ch:ch + 1], w_gate[:, ch, :], start=ch == 0,
                               stop=ch == CH - 1)
            mm.then_inc(gate_mm, 1)
            pe.wait_ge(gate_step, 10)
            pe.matmul(wide[:, 0:2], c.ones_row[:, :], pick[:, :], start=True, stop=True).then_inc(gate_mm, 1)
            pe.wait_ge(w_ready, CH)

            def body(b, k, n, after):
                pe.wait_ge(xT_ready, b + 1)
                for s, r in enumerate(subtiles(n)):
                    cut = slice(s * P, s * P + r)
                    pe.wait_ge(y_ready, b * CH + s + 1)
                    products(pe, y_bank[s % BANKS][0:r, :], [(xT_hi[k][:, ch, cut], xT_lo[k][:, ch, cut]) for ch in range(CH)],
                             [(w_hi[:, ch, :], w_lo[:, ch, :]) for ch in range(CH)]).then_inc(y_mm, 1)

            over_blocks(pe, 2, body)

        @block.scalar
        def _(act):
            act.wait_ge(gate_step, 3)
            act.activation(prob_e[:, :], logit[:, :], ACT.Exp, bias=neg_top[:, :], accum_out=total[:, :]
                           ).then_inc(gate_exp, 1)
            for ch in range(CH):
                act.wait_ge(gathered, 16 * (CH + 1))
                act.activation(w_hi[:, ch, :], w_raw[:, ch, :], ACT.Copy).then_inc(w_hi_ready, 1)

            for b in range(2):
                act.wait_ge(x_in[b], 16)
                act.activation(xT_hi[b][:, :, :], xT[b][:, :, :], ACT.Copy).then_inc(xT_hi_ready, 1)

            def ahead(b, k, n, after):
                if isinstance(b, int) and b + 2 >= NB:
                    return
                nn = TAIL if isinstance(b, int) and b + 2 == FULL else BT
                act.wait_ge(x_in[k], landed(b, k, 2) + 16)
                act.wait_ge(y_mm, b * CH + CH)
                act.activation(xT_hi[k][:, :, 0:nn], xT[k][:, :, 0:nn], ACT.Copy).then_inc(xT_hi_ready, 1)

            over_blocks(act, 2, ahead)

        @block.vector
        def _(dve):
            def step(op):
                op.then_inc(gate_step, 1)

            step(dve.tensor_scalar(mean[:, :], c.token_sum[:, :], 1.0 / TOKENS, None, ALU.mult))
            dve.wait_ge(gate_mm, 1)
            step(dve.tensor_tensor(logit[:, :], small[0:1, 0:EXPERTS], b_gate[:, :], ALU.add))
            dve.wait_ge(gate_step, 2)
            step(dve.tensor_reduce(neg_top[:, :], logit[:, :], AX.X, ALU.max, negate=True))
            dve.wait_ge(gate_exp, 1)
            step(dve.reciprocal(total_inv[:, :], total[:, :]))
            dve.wait_ge(gate_step, 4)
            step(dve.tensor_scalar(prob[:, :], prob_e[:, :], total_inv[:, :], None, ALU.mult))
            dve.wait_ge(gate_step, 5)
            step(dve.tensor_reduce(pick[:, 1:2], prob[:, :], AX.X, ALU.max))
            dve.wait_ge(gate_step, 6)
            step(dve.tensor_scalar(other[:, :], prob[:, :], pick[:, 1:2], None, ALU.is_lt))
            dve.wait_ge(gate_step, 7)
            step(dve.scalar_tensor_tensor(out=rank[:, :], in0=other[:, :], scalar=float(EXPERTS),
                                          in1=c.expert_no[:, :], op0=ALU.mult, op1=ALU.add))
            dve.wait_ge(gate_step, 8)
            dve.tensor_reduce(pick[:, 0:1], rank[:, :], AX.X, ALU.min).then_inc(gate_step, 2)
            dve.wait_ge(gate_mm, 2)
            step(dve.tensor_copy(pick_all[:, :], wide[:, 0:2]))
            dve.wait_ge(gate_step, 11)
            dve.tensor_copy(expert[:, :], pick_all[:, 0:1])
            step(dve.scalar_tensor_tensor(out=row_f[:, :], in0=pick_all[:, 0:1].to_broadcast([P, CH]),
                                          scalar=float(DIM), in1=c.feat[:, :], op0=ALU.mult, op1=ALU.add))
            dve.wait_ge(gate_step, 12)
            step(dve.tensor_copy(row[:, :], row_f[:, :]))
            for ch in range(CH):
                dve.wait_ge(w_hi_ready, ch + 1)
                dve.tensor_tensor(w_lo[:, ch, :], w_raw[:, ch, :], w_hi[:, ch, :].bitcast(F32), ALU.subtract
                                  ).then_inc(w_ready, 1)

            def split(b, k, n):
                dve.wait_ge(xT_hi_ready, b + 1)
                dve.tensor_tensor(xT_lo[k][:, :, 0:n], xT[k][:, :, 0:n], xT_hi[k][:, :, 0:n].bitcast(F32),
                                  ALU.subtract).then_inc(xT_ready, 1)

            dve.sem_inc(y_ready, BANKS)
            split(0, 0, BT)

            def body(b, k, n, after):
                if after:
                    split(b + 1, 1 - k, after)
                dve.wait_ge(x1_in[k], landed(b, k, 2))
                for s, r in enumerate(subtiles(n)):
                    at = b * CH + (s + 1)
                    dve.wait_ge(y_mm, at)
                    dve.tensor_tensor(y[s % 2][0:r, :], y_bank[s % BANKS][0:r, :], b_raw[0:r, :], ALU.add).then_inc(y_ready, 1)
                    dve.wait_ge(y_ready, at + BANKS)
                    if s == 0:
                        dve.wait_ge(done_free, b)
                    dve.scalar_tensor_tensor(out=done[k][0:r, s, :], in0=y[s % 2][0:r, :], scalar=pick_all[0:r, 1:2],
                                             in1=x1[k][0:r, s, :], op0=ALU.mult, op1=ALU.add).then_inc(y_done, 1)

            over_blocks(dve, 2, body)

def kernel_body(nc, c):
    with ExitStack() as ctx:
        def sb(what, shape, dt=F32):
            return ctx.enter_context(nc.sbuf_tensor(what, shape, dt))

        c.scattered = [ctx.enter_context(nc.semaphore(f"scattered{t}")) for t in range(TABLES)]
        c.passed = ctx.enter_context(nc.semaphore("passed"))
        c.ident = sb("ident", [P, P])
        c.same_token = sb("same_token", [P, P])
        c.eps = sb("eps", [P, 1])
        c.ones_row = sb("ones_row", [1, P])
        c.feat = sb("feat", [P, CH])
        c.expert_no = sb("expert_no", [1, EXPERTS])
        c.factors = sb("factors", [P, NB])
        c.token_sum = sb("token_sum", [P, CH])
        with ExitStack() as early:
            def sb2(what, shape, dt=F32):
                return early.enter_context(nc.sbuf_tensor(what, shape, dt))

            c.ident_r = sb2("ident_r", [P, P], F32R)
            c.upper = sb2("upper", [P, P])
            c.sel = sb2("sel", [2 * HEADS, QK * P], F32R)
            c.row_sel = sb2("row_sel", [HEADS, P])
            c.spare = sb2("spare", [P, 1])
            c.bias_v = sb2("bias_v", [P, DIM])
            c.bias_qk = sb2("bias_qk", [P, QK])
            c.sums = sb2("sums", [P, QK])
            c.shares = sb2("shares", [P, QK])
            c.heads = sb2("heads", [P, QK, 2 * HEADS])
            constants_stage(nc, c)
            edges = project_stage(nc, c)
            with nc.sbuf_tensor("inverse", [2 * HEADS, TOKENS], F32) as c.inverse:
                edges = norms_stage(nc, c, edges)
                edges = scale_stage(nc, c, edges)
        mix_stage(nc, c)
        expert_stage(nc, c)


def _layouts(inp):
    import numpy as np
    arr = {n: np.asarray(a) for n, a in inp.items()}
    w = arr["L0_mix_W_qkv"].reshape(HEADS, 3, HDIM, DIM).transpose(1, 0, 2, 3).reshape(3 * DIM, DIM)
    bq = arr["L0_mix_b_qkv"].reshape(HEADS, 3, HDIM).transpose(1, 0, 2).reshape(3 * DIM)
    out = {
        "x": arr["x"], "dst": arr["dst"], "edge_attr": arr["edge_attr_64"],
        "w_qkv": w.T, "b_qk": bq[:2 * DIM].reshape(QK, P).T, "b_v": bq[2 * DIM:],
        "w1": arr["L0_gnn_W1"], "b1": arr["L0_gnn_b1"].reshape(JH, P).T, "w2": arr["L0_gnn_W2"], "b2": arr["L0_gnn_b2"],
        "w_out": arr["L0_mix_W_out"].T, "b_out": arr["L0_mix_b_out"],
        "w_gate": arr["L0_ffn_Wg"], "b_gate": arr["L0_ffn_bg"],
        "w_exp": arr["L0_ffn_We"].reshape(EXPERTS * DIM, DIM), "b_exp": arr["L0_ffn_be"],
    }
    return {n: np.ascontiguousarray(a) for n, a in out.items()}


def build(nc, shapes):
    c = Shared()

    def given(name):
        shape, dtype = shapes[name]
        return nc.dram_tensor(f"in_{name}", shape, dtype, kind="ExternalInput").ap()

    c.x, c.dst, c.edge_attr = given("x"), given("dst"), given("edge_attr")
    c.w_qkv, c.b_qk, c.b_v = given("w_qkv"), given("b_qk"), given("b_v")
    c.w1, c.b1, c.w2, c.b2 = given("w1"), given("b1"), given("w2"), given("b2")
    c.w_out, c.b_out = given("w_out"), given("b_out")
    c.w_gate, c.b_gate = given("w_gate"), given("b_gate")
    c.w_exp, c.b_exp = given("w_exp"), given("b_exp")
    c.out = nc.dram_tensor("out", (TOKENS, DIM), F32, kind="ExternalOutput").ap()
    c.v = nc.dram_tensor("v_rows", [TOKENS, DIM], F32, kind="Internal").ap()
    c.qk = nc.dram_tensor("qk_T", [2 * DIM, TOKENS], F32, kind="Internal").ap()
    c.qk_scaled = nc.dram_tensor("qk_scaled_T", [2 * DIM, TOKENS], F32, kind="Internal").ap()
    c.x1 = nc.dram_tensor("x1_rows", [TOKENS, DIM], F32, kind="Internal").ap()
    c.x1n = nc.dram_tensor("x1n_T", [DIM, TOKENS], F32, kind="Internal").ap()
    c.table = [nc.dram_tensor(f"table{t}", [TROWS, ECOLS], F32, kind="Internal").ap() for t in range(TABLES)]
    kernel_body(nc, c)


def kernel(**inputs):
    import numpy as _np
    import concourse.bacc as _bacc
    from concourse.bass_utils import run_bass_kernel_spmd as _run

    arrays = _layouts(inputs)
    nc = _bacc.Bacc("TRN2", target_bir_lowering=False, num_devices=1)
    build(nc, {n: (a.shape, mybir.dt.from_np(a.dtype)) for n, a in arrays.items()})
    r = _run(nc, [{f"in_{n}": a for n, a in arrays.items()}], core_ids=[0])
    return r.results[0]["out"]
```

```python
from contextlib import ExitStack

import concourse.bass as bass
from concourse import mybir

ALU = mybir.AluOpType
ACT = mybir.ActivationFunctionType
AX = mybir.AxisListType
F32 = mybir.dt.float32
F32R = mybir.dt.float32r
I32 = mybir.dt.int32

P = 128
TOKENS = 6250
DIM = 512
HEADS = 8
HDIM = DIM // HEADS
EDGES = 106250
EDIM = 64
HID = 1024
EXPERTS = 16
CH = DIM // P
QK = 2 * CH
JH = HID // P
BT = 512
FULL = TOKENS // BT
TAIL = TOKENS - FULL * BT
NB = FULL + 1
GT = P // HEADS
EPS = 1e-5
MID = TOKENS // 2
TABLES = 4
TROWS = 6400
ECOLS = EDIM + 1


def subtiles(n):
    return [min(P, n - s) for s in range(0, n, P)]


def over_blocks(eng, unroll, body):
    looped = (FULL - 1) // unroll
    with eng.Fori(0, looped) as i:
        for k in range(unroll):
            body(i * unroll + k, k, BT, BT)
    for b in range(looped * unroll, NB):
        sizes = [BT] * FULL + [TAIL, 0]
        body(b, b % unroll, sizes[b], sizes[b + 1])


def landed(b, k, unroll, dmas=1):
    return (b - k) * (16 * dmas // unroll) + 16 * dmas


def later_size(b, by):
    sizes = [BT] * FULL + [TAIL] + [0] * by
    return sizes[b + by] if isinstance(b, int) else BT


def cols(b, n):
    return bass.ds(b * BT, n)


class Edges:

    def __init__(self, ctx, nc, c, name, first_edge, tiles, tail_tiles, tail_rows, unroll, scattered, psum):
        self.c, self.first, self.tiles, self.unroll = c, first_edge, tiles, unroll
        self.tail_tiles, self.tail_rows = tail_tiles, tail_rows
        self.quads = tiles // 4
        self.scattered = dict(scattered)
        self.last_edge = first_edge + FULL * tiles * P + tail_tiles * tail_rows

        def sb(what, shape, dt=F32):
            return ctx.enter_context(nc.sbuf_tensor(f"{name}_{what}", shape, dt))

        def sem(what):
            return ctx.enter_context(nc.semaphore(f"{name}_{what}"))

        self.attr = [sb(f"attr{k}", [P, tiles, ECOLS]) for k in range(unroll)]
        self.dst = [sb(f"dst{k}", [P, tiles], I32) for k in range(unroll)]
        self.dst_f = [sb(f"dst_f{k}", [P, tiles]) for k in range(unroll)]
        self.dst_r = [sb(f"dst_r{k}", [P, tiles], F32R) for k in range(unroll)]
        self.later = [sb(f"later{k}", [P, tiles]) for k in range(unroll)]
        self.row_a = [sb(f"row_a{k}", [P, tiles]) for k in range(unroll)]
        self.row_b = [sb(f"row_b{k}", [P, tiles]) for k in range(unroll)]
        self.row = [sb(f"row{k}", [P, tiles], I32) for k in range(unroll)]
        self.sums = [sb(f"sums{k}", [P, tiles, ECOLS]) for k in range(unroll)]
        self.sel = [sb(f"sel{k}", [P, 4, P]) for k in range(2)]
        self.p_dst, self.p_sum = psum
        self.spare_banks = len(self.p_dst) - 1

        self.edges_in = [sem(f"edges_in{k}") for k in range(unroll)]
        self.ones_set = sem("ones_set")
        self.dst_ready = sem("dst_ready")
        self.spread = sem("spread")
        self.selected = sem("selected")
        self.summed = sem("summed")
        self.kept = sem("kept")
        self.dst_step = sem("dst_step")
        self.row_step = sem("row_step")
        self.rows_ready = sem("rows_ready")
        self.sums_free = sem("sums_free")

    def shape(self, n):
        return (self.tiles, P) if n == BT else (self.tail_tiles, self.tail_rows)

    def quads_of(self, n):
        m = self.shape(n)[0]
        return [(q, min(4, m - q)) for q in range(0, m, 4)]

    def load(self, sp, b, k, n, guard):
        m, rows = self.shape(n)
        if guard is not None:
            sp.wait_ge(self.summed, guard)
        at = self.first + b * (self.tiles * P)
        sp.dma_start(self.dst[k][0:rows, 0:m],
                     self.c.dst[bass.ds(at, m * rows)].rearrange("(p m) -> p m", m=m)).then_inc(self.edges_in[k], 16)
        sp.dma_start(self.attr[k][0:rows, 0:m, 0:EDIM],
                     self.c.edge_attr[bass.ds(at, m * rows), :].rearrange("(p m) d -> p m d", m=m)
                     ).then_inc(self.edges_in[k], 16)

    def load_first(self, sp):
        sp.wait_ge(self.ones_set, self.unroll)
        self.load(sp, 0, 0, BT, None)

    def load_next(self, sp, b, k, after):
        if after:
            self.load(sp, b + 1, (k + 1) % self.unroll, after, self.quads * b)

    def begin_dve(self, dve):
        for k in range(self.unroll):
            dve.memset(self.attr[k][:, :, EDIM:ECOLS], 1.0).then_inc(self.ones_set, 1)
        if self.spare_banks:
            dve.sem_inc(self.selected, self.spare_banks)

    def begin_act(self, act):
        if self.spare_banks:
            act.sem_inc(self.kept, self.spare_banks)

    def prepare(self, dve, b, k, n):
        m, rows = self.shape(n)
        dve.wait_ge(self.edges_in[k], landed(b, k, self.unroll, 2))
        dve.tensor_scalar(self.dst_f[k][0:rows, 0:m], self.dst[k][0:rows, 0:m], float(-MID), None,
                          ALU.add).then_inc(self.dst_step, 1)
        dve.wait_ge(self.dst_step, b + 1)
        dve.tensor_copy(self.dst_r[k][0:rows, 0:m], self.dst_f[k][0:rows, 0:m]).then_inc(self.dst_ready, 1)

    def spread_dst(self, pe, b, k, n, q):
        rows = self.shape(n)[1]
        if q == 0:
            pe.wait_ge(self.dst_ready, b + 1)
        pe.wait_ge(self.selected, b * self.quads + q)
        j0, w = self.quads_of(n)[q]
        for j in range(w):
            mm = pe.matmul(self.p_dst[q % len(self.p_dst)][0:rows, j * P:j * P + rows],
                           self.dst_r[k][0:rows, j0 + j:j0 + j + 1].to_broadcast([rows, rows]),
                           self.c.ident_r[0:rows, 0:rows], start=True, stop=True)
        mm.then_inc(self.spread, 1)

    def select(self, dve, b, k, n, q):
        rows = self.shape(n)[1]
        dve.wait_ge(self.spread, b * self.quads + q + 1)
        j0, w = self.quads_of(n)[q]
        for j in range(w):
            t = j0 + j
            op = dve.scalar_tensor_tensor(
                out=self.sel[q % 2][0:rows, j, 0:rows], in0=self.p_dst[q % len(self.p_dst)][0:rows, j * P:j * P + rows],
                scalar=self.dst_f[k][0:rows, t:t + 1], in1=self.c.upper[0:rows, 0:rows],
                op0=ALU.is_equal, op1=ALU.mult, accum_out=self.later[k][0:rows, t:t + 1])
        op.then_inc(self.selected, 1)

    def sum_tile(self, pe, b, k, n, q):
        rows = self.shape(n)[1]
        pe.wait_ge(self.selected, b * self.quads + (self.spare_banks + q + 1))
        pe.wait_ge(self.kept, b * self.quads + q)
        j0, w = self.quads_of(n)[q]
        for j in range(w):
            mm = pe.matmul(self.p_sum[q % len(self.p_sum)][0:rows, j * ECOLS:(j + 1) * ECOLS], self.sel[q % 2][0:rows, j, 0:rows],
                           self.attr[k][0:rows, j0 + j, :], start=True, stop=True)
        mm.then_inc(self.summed, 1)

    def keep(self, act, b, k, n, q):
        rows = self.shape(n)[1]
        act.wait_ge(self.summed, b * self.quads + q + 1)
        if q == 0:
            act.wait_ge(self.sums_free, b + 1)
        j0, w = self.quads_of(n)[q]
        act.activation(self.sums[k][0:rows, j0:j0 + w, :], self.p_sum[q % len(self.p_sum)][0:rows, 0:w * ECOLS]
                       .rearrange("p (w c) -> p w c", w=w), ACT.Copy).then_inc(self.kept, 1)

    def rows(self, dve, b, k, n):
        m, rows = self.shape(n)
        dve.wait_ge(self.selected, b * self.quads + (self.spare_banks + len(self.quads_of(n))))
        dve.wait_ge(self.sums_free, b + 1)
        dve.tensor_scalar(self.row_a[k][0:rows, 0:m], self.dst_f[k][0:rows, 0:m], self.c.spare[0:rows, :],
                          None, ALU.subtract).then_inc(self.row_step, 1)
        dve.wait_ge(self.row_step, b * 2 + 1)
        dve.scalar_tensor_tensor(out=self.row_b[k][0:rows, 0:m], in0=self.later[k][0:rows, 0:m], scalar=1.0,
                                 in1=self.row_a[k][0:rows, 0:m], op0=ALU.is_equal,
                                 op1=ALU.mult).then_inc(self.row_step, 1)
        dve.wait_ge(self.row_step, b * 2 + 2)
        dve.tensor_scalar(self.row[k][0:rows, 0:m], self.row_b[k][0:rows, 0:m], self.c.spare[0:rows, :],
                          float(MID), ALU.add, ALU.add).then_inc(self.rows_ready, 1)

    def begin_pool(self, pool):
        pool.sem_inc(self.sums_free, self.unroll - 1)

    def scatter(self, pool, b, k, n):
        m, rows = self.shape(n)
        pool.wait_ge(self.rows_ready, b + 1)
        pool.wait_ge(self.kept, b * self.quads + (self.spare_banks + len(self.quads_of(n))))
        each = self.tiles // TABLES
        for j in range(m):
            t = j % TABLES
            pool.wait_ge(self.c.scattered[t], (b * each + (j // TABLES + self.scattered[t])) * 16)
            pool.sem_inc(self.c.passed, 1)
            pool.indirect_dma_start(
                self.c.table[t], bass.IndirectOffsetOnAxis(ap=self.row[k][0:rows, j:j + 1], axis=0),
                self.sums[k][0:rows, j, :], None, compute_op=ALU.add).then_inc(self.c.scattered[t], 16)
            if j == TABLES - 1:
                pool.sem_inc(self.sums_free, 1)

    def finish_pool(self, pool):
        for t, count in self.total().items():
            pool.wait_ge(self.c.scattered[t], 16 * count)

    def total(self):
        return {t: self.scattered[t] + FULL * (self.tiles // TABLES)
                + len([j for j in range(self.tail_tiles) if j % TABLES == t]) for t in range(TABLES)}


class Weights:

    def __init__(self, ctx, nc, name, items, width):
        self.items = items
        self.raw = [ctx.enter_context(nc.sbuf_tensor(f"{name}_raw{k}", [P, width], F32)) for k in range(2)]
        self.loaded = [ctx.enter_context(nc.semaphore(f"{name}_loaded{k}")) for k in range(2)]
        self.hi_ready = ctx.enter_context(nc.semaphore(f"{name}_hi_ready"))
        self.lo_ready = ctx.enter_context(nc.semaphore(f"{name}_lo_ready"))

    def load(self, sp):
        for i, (src, hi, lo) in enumerate(self.items):
            if i >= 2:
                sp.wait_ge(self.lo_ready, i - 1)
            sp.dma_start(self.raw[i % 2][0:src.shape[0], 0:src.shape[1]], src).then_inc(self.loaded[i % 2], 16)

    def split_hi(self, act):
        for i, (src, hi, lo) in enumerate(self.items):
            act.wait_ge(self.loaded[i % 2], 16 * (i // 2 + 1))
            act.activation(hi, self.raw[i % 2][0:src.shape[0], 0:src.shape[1]], ACT.Copy).then_inc(self.hi_ready, 1)

    def split_lo(self, dve):
        for i, (src, hi, lo) in enumerate(self.items):
            dve.wait_ge(self.hi_ready, i + 1)
            dve.tensor_tensor(lo, self.raw[i % 2][0:src.shape[0], 0:src.shape[1]], hi.bitcast(F32),
                              ALU.subtract).then_inc(self.lo_ready, 1)

    def wait(self, pe):
        pe.wait_ge(self.lo_ready, len(self.items))


def products(pe, out, left, right, first=True, last=True):
    n = 3 * len(left)
    i = 0
    for (lh, ll), (rh, rl) in zip(left, right):
        for a, c in ((lh, rh), (ll, rh), (lh, rl)):
            mm = pe.matmul(out, a, c, start=first and i == 0, stop=last and i == n - 1)
            i += 1
    return mm


class Norm:

    def __init__(self, ctx, nc, c, name, banks, copies, bank_free=None, xn_used=None):
        def sb(what, shape, dt=F32):
            return ctx.enter_context(nc.sbuf_tensor(f"{name}_{what}", shape, dt))

        def sem(what):
            return ctx.enter_context(nc.semaphore(f"{name}_{what}"))

        self.c, self.banks = c, banks
        self.x = [sb(f"x{k}", [P, CH, DIM]) for k in range(2)]
        self.xn = [sb(f"xn{k}", [P, DIM]) for k in range(2)]
        self.hi = [sb(f"xT_hi{k}", [P, CH, BT], F32R) for k in range(copies)]
        self.lo = [sb(f"xT_lo{k}", [P, CH, BT], F32R) for k in range(copies)]
        self.raw = sb("raw", [P, CH, 6])
        self.mv = sb("mv", [P, CH, 2])
        self.std = sb("std", [P, CH])
        self.rstd = sb("rstd", [P, CH])
        self.x_in = [sem(f"x_in{k}") for k in range(2)]
        self.raw_ready = sem("raw_ready")
        self.mv_ready = sem("mv_ready")
        self.std_ready = sem("std_ready")
        self.rstd_ready = sem("rstd_ready")
        self.xn_ready = sem("xn_ready")
        self.turned = sem("turned")
        self.hi_ready = sem("hi_ready")
        self.split = bank_free or [sem("split")]
        self.xn_used = xn_used

    def load(self, sp, b, k, n):
        if n == BT:
            sp.dma_start(self.x[k][:, :, :], self.c.x[bass.ds(b * BT, n), :].rearrange("(s p) d -> p s d", p=P)
                         ).then_inc(self.x_in[k], 16)
        else:
            sp.dma_start(self.x[k][0:n, 0, :], self.c.x[bass.ds(b * BT, n), :]).then_inc(self.x_in[k], 16)

    def stats(self, dve, b, k, n, s):
        if s == 0:
            dve.wait_ge(self.x_in[k], landed(b, k, 2))
        r = subtiles(n)[s]
        dve.bn_stats(self.raw[0:r, s, :], self.x[k][0:r, s, :]).then_inc(self.raw_ready, 1)

    def aggregate(self, dve, b, k, n):
        dve.wait_ge(self.raw_ready, b * CH + len(subtiles(n)))
        dve.sem_inc(self.c.passed, 1)
        for s, r in enumerate(subtiles(n)):
            op = dve.bn_aggr(self.mv[0:r, s, :], self.raw[0:r, s, :])
        op.then_inc(self.mv_ready, 1)

    def deviation(self, act, b, n):
        r, ns = subtiles(n)[-1], len(subtiles(n))
        act.wait_ge(self.mv_ready, b + 1)
        act.activation(self.std[0:r, 0:ns], self.mv[0:r, 0:ns, 1], ACT.Sqrt,
                       bias=self.c.eps[0:r, :]).then_inc(self.std_ready, 1)

    def invert(self, dve, b, n):
        r, ns = subtiles(n)[-1], len(subtiles(n))
        dve.wait_ge(self.std_ready, b + 1)
        dve.reciprocal(self.rstd[0:r, 0:ns], self.std[0:r, 0:ns]).then_inc(self.rstd_ready, 1)

    def normalise(self, dve, b, k, n, s):
        r = subtiles(n)[s]
        if s == 0:
            dve.wait_ge(self.rstd_ready, b + 1)
        if not isinstance(b, int) or b * CH + s >= 2:
            dve.wait_ge(self.turned, b * CH + (s - 1))
            if self.xn_used is not None:
                dve.wait_ge(self.xn_used, b * CH + (s - 1))
        dve.tensor_scalar(self.xn[s % 2][0:r, :], self.x[k][0:r, s, :], self.mv[0:r, s, 0:1],
                          self.rstd[0:r, s:s + 1], ALU.subtract, ALU.mult).then_inc(self.xn_ready, 1)

    def turn(self, pe, b, n, s, bank_uses):
        r = subtiles(n)[s]
        bank = self.banks[s % len(self.banks)]
        pe.wait_ge(self.xn_ready, b * CH + (s + 1))
        if bank_uses is not None:
            pe.wait_ge(self.split[s % len(self.split)], bank_uses)
        for ch in range(CH):
            mm = pe.transpose(bank[:, ch * P:ch * P + r], self.xn[s % 2][0:r, ch * P:(ch + 1) * P],
                              self.c.ident[0:r, 0:r])
        mm.then_inc(self.turned, 1)

    def views(self, k, n, s):
        r = subtiles(n)[s]
        bank = self.banks[s % len(self.banks)][:, :].rearrange("p (c t) -> p c t", c=CH)[:, :, 0:r]
        return bank, self.hi[k][:, :, s * P:s * P + r], self.lo[k][:, :, s * P:s * P + r]

    def split_hi(self, act, b, k, n, s):
        act.wait_ge(self.turned, b * CH + (s + 1))
        bank, hi, lo = self.views(k, n, s)
        act.activation(hi, bank, ACT.Copy).then_inc(self.hi_ready, 1)

    def split_lo(self, dve, b, k, n, s):
        dve.wait_ge(self.hi_ready, b * CH + (s + 1))
        bank, hi, lo = self.views(k, n, s)
        dve.tensor_tensor(lo, bank, hi.bitcast(F32), ALU.subtract
                          ).then_inc(self.split[s % len(self.split)], 1)

    def pairs(self, k, cut):
        return [(self.hi[k][:, c, cut], self.lo[k][:, c, cut]) for c in range(CH)]

    def first_on_dve(self, dve):
        for s in range(CH):
            self.stats(dve, 0, 0, BT, s)
        self.aggregate(dve, 0, 0, BT)
        self.invert(dve, 0, BT)
        for s in range(CH):
            self.normalise(dve, 0, 0, BT, s)
            if s >= 1:
                self.split_lo(dve, 0, 0, BT, s - 1)
        self.split_lo(dve, 0, 0, BT, CH - 1)


class Shared:
    pass


def constants_stage(nc, c):
    with ExitStack() as ctx:
        zero = ctx.enter_context(nc.sbuf_tensor("zero", [P, TROWS // P * ECOLS], F32))
        sel_f = ctx.enter_context(nc.sbuf_tensor("sel_f", [2 * HEADS, QK * P], F32))
        spare_i = ctx.enter_context(nc.sbuf_tensor("spare_i", [P, 1], I32))
        feat_i = ctx.enter_context(nc.sbuf_tensor("feat_i", [P, CH], I32))
        expert_i = ctx.enter_context(nc.sbuf_tensor("expert_i", [1, EXPERTS], I32))
        zero_set, filled, shaped, converted, tables_zero = c.finished = [
            ctx.enter_context(nc.semaphore(name))
            for name in ("zero_set", "filled", "shaped", "converted", "tables_zero")]
        block = ctx.enter_context(nc.Block())

        @block.sync
        def _(sp):
            sp.wait_ge(zero_set, 1)
            for t in range(TABLES):
                sp.dma_start(c.table[t].rearrange("(p a) c -> p (a c)", p=P), zero[:, :]).then_inc(tables_zero, 16)
            sp.dma_start(c.bias_v[:, :], c.b_v.partition_broadcast(P)).then_inc(tables_zero, 16)
            sp.dma_start(c.bias_qk[:, :], c.b_qk).then_inc(tables_zero, 16)
            sp.wait_ge(tables_zero, 16 * (TABLES + 2))

        @block.gpsimd
        def _(pool):
            pool.memset(c.ident[:, :], 0.0)
            pool.memset(sel_f[:, :], 0.0)
            pool.memset(c.row_sel[:, :], 0.0)
            pool.memset(c.upper[:, :], 1.0)
            pool.memset(c.same_token[:, :], 1.0).then_inc(filled, 1)
            pool.wait_ge(filled, 1)
            pool.affine_select(out=c.ident[:, :], in_=c.ident[:, :], compare_op=ALU.not_equal, fill=1.0, base=0,
                               pattern=[[-1, P]], channel_multiplier=1)
            pool.affine_select(out=sel_f[:, :], in_=sel_f[:, :], compare_op=ALU.not_equal, fill=1.0, base=0,
                               pattern=[[-HEADS, 2], [-2, CH], [-1, 2], [0, HDIM]], channel_multiplier=1)
            pool.affine_select(out=c.row_sel[:, :], in_=c.row_sel[:, :], compare_op=ALU.not_equal, fill=1.0,
                               base=0, pattern=[[0, GT], [-1, HEADS]], channel_multiplier=1)
            pool.affine_select(out=c.upper[:, :], in_=c.upper[:, :], compare_op=ALU.is_ge, fill=0.0, base=0,
                               pattern=[[1, P]], channel_multiplier=-1)
            pool.affine_select(out=c.same_token[:, :], in_=c.same_token[:, :], compare_op=ALU.is_ge, fill=0.0,
                               base=0, pattern=[[-HEADS, GT], [0, HEADS]], channel_multiplier=1).then_inc(filled, 1)
            pool.wait_ge(filled, 2)
            pool.affine_select(out=c.same_token[:, :], in_=c.same_token[:, :], compare_op=ALU.is_ge, fill=0.0,
                               base=HEADS - 1, pattern=[[HEADS, GT], [0, HEADS]], channel_multiplier=-1)
            pool.iota(spare_i[:, :], [[0, 1]], base=TOKENS - MID, channel_multiplier=1)
            pool.iota(feat_i[:, :], [[P, CH]], base=0, channel_multiplier=1)
            pool.iota(expert_i[:, :], [[1, EXPERTS]], base=0, channel_multiplier=0).then_inc(shaped, 1)

        @block.vector
        def _(dve):
            dve.memset(zero[:, :], 0.0).then_inc(zero_set, 1)
            dve.memset(c.eps[:, :], EPS)
            dve.memset(c.ones_row[:, :], 1.0)
            dve.wait_ge(shaped, 1)
            dve.tensor_copy(c.ident_r[:, :], c.ident[:, :])
            dve.tensor_copy(c.sel[:, :], sel_f[:, :])
            dve.tensor_copy(c.spare[:, :], spare_i[:, :])
            dve.tensor_copy(c.feat[:, :], feat_i[:, :])
            dve.tensor_copy(c.expert_no[:, :], expert_i[:, :]).then_inc(converted, 1)
            dve.wait_ge(converted, 1)


def project_stage(nc, c):
    with ExitStack() as ctx:
        def sb(what, shape, dt=F32):
            return ctx.enter_context(nc.sbuf_tensor(f"pr_{what}", shape, dt))

        def bank(what):
            return ctx.enter_context(nc.psum_tensor(f"pr_{what}", [P, BT], F32))

        def sem(what):
            return ctx.enter_context(nc.semaphore(f"pr_{what}"))

        W3 = 3 * DIM
        w_hi = sb("w_hi", [P, CH, W3], F32R)
        w_lo = sb("w_lo", [P, CH, W3], F32R)
        qk = [sb(f"qk{k}", [P, QK, BT]) for k in range(2)]
        v = sb("v", [P, CH, DIM])
        part = [sb(f"part{k}", [P, QK]) for k in range(2)]
        turn_banks = [bank(f"turn{k}") for k in range(2)]
        v_bank = [bank(f"v_bank{k}") for k in range(2)]
        qk_bank = [bank(f"qk_bank{k}") for k in range(2)]
        weights = Weights(ctx, nc, "pr_w", [
            (c.w_qkv[i * P:(i + 1) * P, a:a + W3 // 2], w_hi[:, i, a:a + W3 // 2], w_lo[:, i, a:a + W3 // 2])
            for i in range(CH) for a in (0, W3 // 2)], W3 // 2)
        norm = Norm(ctx, nc, c, "pr_norm", turn_banks, 2)
        edges = Edges(ctx, nc, c, "pr_edge", 0, 36, 12, P, 2, {t: 0 for t in range(TABLES)},
                      ([bank("dst")], [bank("sum")]))
        v_mm, v_bank_free = sem("v_mm"), sem("v_bank_free")
        qk_mm, qk_bank_free = sem("qk_mm"), sem("qk_bank_free")
        v_stored, v_free = sem("v_stored"), sem("v_free")
        qk_stored, qk_free = sem("qk_stored"), sem("qk_free")
        added = sem("added")
        c.finished += [v_mm, v_bank_free, qk_mm, qk_bank_free, v_stored, v_free, qk_stored, qk_free, added]
        block = ctx.enter_context(nc.Block())

        def groups(n):
            return [("v", s) for s in range(len(subtiles(n)))] + [("qk", o) for o in range(QK)]

        def slots(n):
            return range(max(len(groups(n)), len(edges.quads_of(n))))

        @block.sync
        def _(sp):
            norm.load(sp, 0, 0, BT)
            norm.load(sp, 1, 1, BT)
            weights.load(sp)
            sp.sem_inc(v_free, 1)
            sp.sem_inc(qk_free, 2)
            edges.load_first(sp)

            def body(b, k, n, after):
                edges.load_next(sp, b, k, after)
                if after and not (isinstance(b, int) and b + 2 >= NB):
                    nn = TAIL if isinstance(b, int) and b + 2 == FULL else BT
                    sp.wait_ge(norm.xn_ready, (b + 1) * CH)
                    norm.load(sp, b + 2, k, nn)
                sp.wait_ge(v_bank_free, b * CH + (2 + len(subtiles(n))))
                if n == BT:
                    sp.dma_start(c.v[cols(b, n), :].rearrange("(s p) d -> p s d", p=P), v[:, :, :]
                                 ).then_inc(v_stored, 16)
                else:
                    sp.dma_start(c.v[cols(b, n), :], v[0:n, 0, :]).then_inc(v_stored, 16)
                sp.wait_ge(v_stored, b * 16 + 16)
                sp.sem_inc(v_free, 1)
                sp.wait_ge(qk_bank_free, b * QK + (2 + QK))
                sp.sem_inc(c.passed, 1)
                sp.dma_start(c.qk[:, cols(b, n)].rearrange("(o p) t -> p o t", p=P), qk[k][:, :, 0:n]
                             ).then_inc(qk_stored, 16)
                sp.wait_ge(qk_stored, b * 16 + 16)
                sp.sem_inc(qk_free, 1)

            over_blocks(sp, 2, body)

        @block.tensor
        def _(pe):
            for s in range(CH):
                norm.turn(pe, 0, BT, s, s - 1 if s >= 2 else None)
            weights.wait(pe)

            def body(b, k, n, after):
                pe.wait_ge(norm.split[0], b * CH + len(subtiles(n)))
                todo = groups(n)
                quads = edges.quads_of(n)
                for g in slots(n):
                    if g < len(quads):
                        edges.spread_dst(pe, b, k, n, g)
                    if g < len(todo):
                        kind, i = todo[g]
                        if kind == "v":
                            r = subtiles(n)[i]
                            pe.wait_ge(v_bank_free, b * CH + i + 1)
                            products(pe, v_bank[i % 2][0:r, :], norm.pairs(k, slice(i * P, i * P + r)),
                                     [(w_hi[:, ch, 2 * DIM:W3], w_lo[:, ch, 2 * DIM:W3]) for ch in range(CH)]
                                     ).then_inc(v_mm, 1)
                        else:
                            pe.wait_ge(qk_bank_free, b * QK + i + 1)
                            cut = slice(i * P, (i + 1) * P)
                            products(pe, qk_bank[i % 2][:, 0:n],
                                     [(w_hi[:, ch, cut], w_lo[:, ch, cut]) for ch in range(CH)],
                                     norm.pairs(k, slice(0, n))).then_inc(qk_mm, 1)
                    if g < len(quads):
                        edges.sum_tile(pe, b, k, n, g)
                    if after and 7 <= g < 7 + len(subtiles(after)):
                        norm.turn(pe, b + 1, after, g - 7, b * CH + (CH + g - 7 - 1))

            over_blocks(pe, 2, body)

        @block.scalar
        def _(act):
            norm.deviation(act, 0, BT)
            for s in range(CH):
                norm.split_hi(act, 0, 0, BT, s)
            weights.split_hi(act)
            edges.begin_act(act)
            act.sem_inc(qk_bank_free, 2)

            def body(b, k, n, after):
                todo = groups(n)
                for g in slots(n):
                    if g < len(todo) and todo[g][0] == "qk":
                        o = todo[g][1]
                        act.wait_ge(qk_mm, b * QK + o + 1)
                        if o == 0:
                            act.wait_ge(qk_free, b + 1)
                            act.wait_ge(added, b)
                        act.activation(qk[k][:, o, 0:n], qk_bank[o % 2][:, 0:n], ACT.Sigmoid,
                                       bias=c.bias_qk[:, o:o + 1], accum_out=part[k][:, o:o + 1]
                                       ).then_inc(qk_bank_free, 1)
                    if g < len(edges.quads_of(n)):
                        edges.keep(act, b, k, n, g)
                    if after and g == 4:
                        norm.deviation(act, b + 1, after)
                    if after and 7 <= g < 7 + len(subtiles(after)):
                        if g == 7:
                            act.wait_ge(qk_mm, b * QK)
                        norm.split_hi(act, b + 1, 1 - k, after, g - 7)

            over_blocks(act, 2, body)

        @block.vector
        def _(dve):
            edges.begin_dve(dve)
            norm.first_on_dve(dve)
            dve.sem_inc(v_bank_free, 2)
            dve.memset(c.sums[:, :], 0.0).then_inc(added, 1)
            weights.split_lo(dve)

            edges.prepare(dve, 0, 0, BT)

            def body(b, k, n, after):
                todo = groups(n)
                for g in slots(n):
                    if g < len(edges.quads_of(n)):
                        edges.select(dve, b, k, n, g)
                    if g < len(todo) and todo[g][0] == "v":
                        s = todo[g][1]
                        r = subtiles(n)[s]
                        if s == 0:
                            dve.wait_ge(v_free, b + 1)
                        dve.wait_ge(v_mm, b * CH + s + 1)
                        dve.tensor_tensor(v[0:r, s, :], v_bank[s % 2][0:r, :], c.bias_v[0:r, :],
                                          ALU.add).then_inc(v_bank_free, 1)
                    if after and g < len(subtiles(after)):
                        norm.stats(dve, b + 1, 1 - k, after, g)
                    if after and g == 4:
                        norm.aggregate(dve, b + 1, 1 - k, after)
                    if after and g == 5:
                        norm.invert(dve, b + 1, after)
                    if after and g == 6:
                        edges.prepare(dve, b + 1, 1 - k, after)
                    if after and 6 <= g < 6 + len(subtiles(after)):
                        norm.normalise(dve, b + 1, 1 - k, after, g - 6)
                    if after and 7 <= g < 7 + len(subtiles(after)):
                        norm.split_lo(dve, b + 1, 1 - k, after, g - 7)
                edges.rows(dve, b, k, n)
                dve.wait_ge(qk_bank_free, b * QK + (2 + QK))
                dve.wait_ge(added, b + 1)
                dve.tensor_tensor(c.sums[:, :], c.sums[:, :], part[k][:, :], ALU.add).then_inc(added, 1)

            over_blocks(dve, 2, body)

        @block.gpsimd
        def _(pool):
            edges.begin_pool(pool)
            over_blocks(pool, 2, lambda b, k, n, after: edges.scatter(pool, b, k, n))
            edges.finish_pool(pool)

    return edges


def head_matrix(dve, c, src, built):
    dve.memset(c.heads[:, :, :], 0.0).then_inc(built, 1)
    dve.wait_ge(built, 1)
    flat = c.heads[:, :, :].rearrange("p o r -> p (o r)")
    step = 2 * HEADS + 2
    for parity in range(2):
        rows = slice(parity * HDIM, (parity + 1) * HDIM)
        for side, at in ((0, 0), (1, CH * 2 * HEADS + HEADS)):
            a = at + parity
            op = dve.tensor_copy(flat[rows, a:a + (CH - 1) * step + 1:step],
                                 src[rows, (1 - side) * CH:(2 - side) * CH])
    op.then_inc(built, 1)
    return 2


def norms_stage(nc, c, before):
    with ExitStack() as ctx:
        def sb(what, shape, dt=F32):
            return ctx.enter_context(nc.sbuf_tensor(f"nm_{what}", shape, dt))

        def bank(what):
            return ctx.enter_context(nc.psum_tensor(f"nm_{what}", [P, BT], F32))

        def sem(what):
            return ctx.enter_context(nc.semaphore(f"nm_{what}"))

        U = 4
        R = 2 * HEADS
        qk = [sb(f"qk{k}", [P, QK, BT]) for k in range(U)]
        r_hi = [sb(f"r_hi{k}", [R, BT], F32R) for k in range(U)]
        r_lo = [sb(f"r_lo{k}", [R, BT], F32R) for k in range(U)]
        part = [sb(f"part{k}", [P, QK]) for k in range(U)]
        io_bank = [bank(f"io{k}") for k in range(2)]
        wide = [bank(f"wide{k}") for k in range(2)]
        edges = Edges(ctx, nc, c, "nm_edge", before.last_edge, 16, 2, P, U, before.total(),
                      ([bank(f"dst{k}") for k in range(2)], [bank(f"sum{k}") for k in range(2)]))
        built, qk_in = sem("built"), [sem(f"qk_in{k}") for k in range(U)]
        io_mm, r_step, r_ready = sem("io_mm"), sem("r_step"), sem("r_ready")
        wide_mm, wide_free, added = sem("wide_mm"), sem("wide_free"), sem("added")
        block = ctx.enter_context(nc.Block())

        @block.sync
        def _(sp):
            def load(b, k, n):
                sp.dma_start(qk[k][:, :, 0:n], c.qk[:, cols(b, n)].rearrange("(o p) t -> p o t", p=P)
                             ).then_inc(qk_in[k], 16)

            for b in range(3):
                load(b, b, BT)
            edges.load_first(sp)

            def body(b, k, n, after):
                edges.load_next(sp, b, k, after)
                if later_size(b, 3):
                    sp.wait_ge(wide_free, b * QK + 2)
                    load(b + 3, (k + 3) % U, later_size(b, 3))

            over_blocks(sp, U, body)

        @block.tensor
        def _(pe):
            def io(b, k, n, o):
                if o == 0:
                    pe.wait_ge(qk_in[k], landed(b, k, U))
                mm = pe.matmul(io_bank[k % 2][0:R, 0:n], c.heads[:, o, :], qk[k][:, o, 0:n],
                               start=o == 0, stop=o == QK - 1)
                if o == QK - 1:
                    mm.then_inc(io_mm, 1)

            pe.wait_ge(built, 2)
            for b in range(2):
                for o in range(QK):
                    io(b, b, BT, o)

            def widen(b, k, n, o):
                if o == 0:
                    pe.wait_ge(r_ready, b + 1)
                pe.wait_ge(wide_free, b * QK + o + 1)
                for i, r in enumerate((r_hi[k], r_lo[k])):
                    mm = pe.matmul(wide[o % 2][:, 0:n], c.sel[:, o * P:(o + 1) * P], r[:, 0:n],
                                   start=i == 0, stop=i == 1)
                mm.then_inc(wide_mm, 1)

            def body(b, k, n, after):
                ahead = later_size(b, 2)
                quads = len(edges.quads_of(n))
                for half in range(2):
                    for q in (2 * half, 2 * half + 1):
                        if q < quads:
                            edges.spread_dst(pe, b, k, n, q)
                    for o in range(half * CH, (half + 1) * CH):
                        widen(b, k, n, o)
                        if ahead:
                            if o == 0:
                                pe.wait_ge(r_step, b * 3 + 2)
                            io(b + 2, (k + 2) % U, ahead, o)
                    for q in (2 * half, 2 * half + 1):
                        if q < quads:
                            edges.sum_tile(pe, b, k, n, q)

            over_blocks(pe, U, body)

        @block.scalar
        def _(act):
            edges.begin_act(act)

            def body(b, k, n, after):
                for q in range(len(edges.quads_of(n))):
                    edges.keep(act, b, k, n, q)

            over_blocks(act, U, body)

        @block.vector
        def _(dve):
            edges.begin_dve(dve)
            head_matrix(dve, c, c.sums, built)
            dve.memset(c.shares[:, :], 0.0).then_inc(added, 1)
            dve.sem_inc(wide_free, 2)

            def invert(b, k, n, half):
                w = (n + 1) // 2
                a, z = half * w, min(n, (half + 1) * w)
                dve.wait_ge(io_mm, b + 1)
                dve.reciprocal(c.inverse[:, bass.ds(b * BT + a, z - a)], io_bank[k % 2][0:R, a:z]).then_inc(r_step, 1)

            def split(b, k, n):
                dve.wait_ge(r_step, b * 3 + 2)
                dve.sem_inc(c.passed, 1)
                dve.tensor_copy(r_hi[k][:, 0:n], c.inverse[:, cols(b, n)]).then_inc(r_step, 1)
                dve.wait_ge(r_step, b * 3 + 3)
                dve.tensor_tensor(r_lo[k][:, 0:n], c.inverse[:, cols(b, n)], r_hi[k][:, 0:n].bitcast(F32),
                                  ALU.subtract).then_inc(r_ready, 1)

            for half in range(2):
                invert(0, 0, BT, half)
            split(0, 0, BT)
            edges.prepare(dve, 0, 0, BT)

            def body(b, k, n, after):
                quads = len(edges.quads_of(n))
                for o in range(QK):
                    if o % CH < 2 and 2 * (o // CH) + o % CH < quads:
                        edges.select(dve, b, k, n, 2 * (o // CH) + o % CH)
                    dve.wait_ge(wide_mm, b * QK + o + 1)
                    dve.tensor_tensor_reduce(wide[o % 2][:, 0:n], qk[k][:, o, 0:n], wide[o % 2][:, 0:n], 1.0, 0.0,
                                             ALU.mult, ALU.add, part[k][:, o:o + 1]).then_inc(wide_free, 1)
                    if after and o % CH == 1:
                        invert(b + 1, (k + 1) % U, after, o // CH)
                    if after and o == 2:
                        edges.prepare(dve, b + 1, (k + 1) % U, after)
                    if after and o == 6:
                        split(b + 1, (k + 1) % U, after)
                edges.rows(dve, b, k, n)
                dve.wait_ge(wide_free, b * QK + (2 + QK))
                dve.wait_ge(added, b + 1)
                dve.tensor_tensor(c.shares[:, :], c.shares[:, :], part[k][:, :], ALU.add).then_inc(added, 1)

            over_blocks(dve, U, body)

        @block.gpsimd
        def _(pool):
            edges.begin_pool(pool)
            over_blocks(pool, U, lambda b, k, n, after: edges.scatter(pool, b, k, n))
            edges.finish_pool(pool)

    return edges


def scale_stage(nc, c, before):
    with ExitStack() as ctx:
        def sb(what, shape, dt=F32):
            return ctx.enter_context(nc.sbuf_tensor(f"sc_{what}", shape, dt))

        def bank(what):
            return ctx.enter_context(nc.psum_tensor(f"sc_{what}", [P, BT], F32))

        def sem(what):
            return ctx.enter_context(nc.semaphore(f"sc_{what}"))

        U = 4
        H = HEADS
        qk = [sb(f"qk{k}", [P, QK, BT]) for k in range(U)]
        gate = [sb(f"gate{k}", [H, BT]) for k in range(U)]
        ce = [sb(f"ce{k}", [H, 2, BT]) for k in range(U)]
        ce_hi = [sb(f"ce_hi{k}", [H, 2, BT], F32R) for k in range(U)]
        ce_lo = [sb(f"ce_lo{k}", [H, 2, BT], F32R) for k in range(U)]
        neg_max = [sb(f"neg_max{k}", [H, 1]) for k in range(U)]
        exp_sum = [sb(f"exp_sum{k}", [H, 1]) for k in range(U)]
        neg_maxs = sb("neg_maxs", [H, NB])
        exp_sums = sb("exp_sums", [H, NB])
        top = sb("top", [H, 1])
        rescale = sb("rescale", [H, NB])
        weighted = sb("weighted", [H, NB])
        total = sb("total", [H, 1])
        total_inv = sb("total_inv", [H, 1])
        factor = sb("factor", [H, NB])
        i_bank, o_bank = bank("i_bank"), bank("o_bank")
        wide = [bank(f"wide{k}") for k in range(2)]
        edges = Edges(ctx, nc, c, "sc_edge", before.last_edge, 16, 1, EDGES % P % 16, U, before.total(),
                      ([bank(f"dst{k}") for k in range(2)], [bank(f"sum{k}") for k in range(2)]))
        assert edges.last_edge == EDGES
        built, qk_stored = sem("built"), sem("qk_stored")
        qk_in = [sem(f"qk_in{k}") for k in range(U)]
        io_mm, gated, max_ready, exp_ready = sem("io_mm"), sem("gated"), sem("max_ready"), sem("exp_ready")
        c_ready, hi_ready, ce_ready, noted = sem("c_ready"), sem("hi_ready"), sem("ce_ready"), sem("noted")
        wide_mm, wide_free = sem("wide_mm"), sem("wide_free")
        end_step, end_exp, end_mm = sem("end_step"), sem("end_exp"), sem("end_mm")
        block = ctx.enter_context(nc.Block())

        @block.sync
        def _(sp):
            def load(b, k, n):
                sp.dma_start(qk[k][:, :, 0:n], c.qk[:, cols(b, n)].rearrange("(o p) t -> p o t", p=P)
                             ).then_inc(qk_in[k], 16)

            for b in range(3):
                load(b, b, BT)
            edges.load_first(sp)

            def body(b, k, n, after):
                edges.load_next(sp, b, k, after)
                sp.wait_ge(qk_stored, b * 16)
                if later_size(b, 3):
                    load(b + 3, (k + 3) % U, later_size(b, 3))
                sp.wait_ge(wide_free, b * QK + (2 + QK))
                sp.dma_start(c.qk_scaled[:, cols(b, n)].rearrange("(o p) t -> p o t", p=P), qk[k][:, :, 0:n]
                             ).then_inc(qk_stored, 16)

            over_blocks(sp, U, body)
            sp.wait_ge(qk_stored, NB * 16)

        @block.tensor
        def _(pe):
            def io(b, k, n, o):
                if o == 0:
                    pe.wait_ge(qk_in[k], landed(b, k, U))
                out, row = (i_bank, 0) if o < CH else (o_bank, H)
                mm = pe.matmul(out[0:H, 0:n], c.heads[:, o, row:row + H], qk[k][:, o, 0:n],
                               start=o % CH == 0, stop=o % CH == CH - 1)
                if o % CH == CH - 1:
                    mm.then_inc(io_mm, 1)

            pe.wait_ge(built, 2)
            def banks_free(b, o):
                if o == 0:
                    pe.wait_ge(gated, b)
                if o == CH:
                    pe.wait_ge(exp_ready, b)
                    pe.wait_ge(max_ready, b)

            for b in range(2):
                for o in range(QK):
                    if b:
                        banks_free(b, o)
                    io(b, b, BT, o)

            def widen(b, k, n, o):
                if o == 0:
                    pe.wait_ge(ce_ready, b + 1)
                pe.wait_ge(wide_free, b * QK + o + 1)
                for i, r in enumerate((ce_hi[k], ce_lo[k])):
                    mm = pe.matmul(wide[o % 2][:, 0:n], c.sel[0:H, (o % CH) * P:(o % CH + 1) * P],
                                   r[:, o // CH, 0:n], start=i == 0, stop=i == 1)
                mm.then_inc(wide_mm, 1)

            def body(b, k, n, after):
                ahead = later_size(b, 2)
                quads = len(edges.quads_of(n))
                for half in range(2):
                    for q in (2 * half, 2 * half + 1):
                        if q < quads:
                            edges.spread_dst(pe, b, k, n, q)
                    for o in range(half * CH, (half + 1) * CH):
                        widen(b, k, n, o)
                        if ahead:
                            banks_free(b + 2, o)
                            io(b + 2, (k + 2) % U, ahead, o)
                    for q in (2 * half, 2 * half + 1):
                        if q < quads:
                            edges.sum_tile(pe, b, k, n, q)

            over_blocks(pe, U, body)
            pe.wait_ge(end_step, 7)
            pe.matmul(i_bank[:, 0:NB], c.row_sel[:, :], factor[:, :], start=True, stop=True).then_inc(end_mm, 1)

        @block.scalar
        def _(act):
            def gates(b, k, n):
                act.wait_ge(io_mm, b * 2 + 1)
                act.activation(gate[k][:, 0:n], i_bank[0:H, 0:n], ACT.Sigmoid).then_inc(gated, 1)

            def exponentials(b, k, n):
                act.wait_ge(max_ready, b + 1)
                act.activation(ce[k][:, 1, 0:n], o_bank[0:H, 0:n], ACT.Exp, bias=neg_max[k][:, :],
                               accum_out=exp_sum[k][:, :]).then_inc(exp_ready, 1)

            edges.begin_act(act)
            gates(0, 0, BT)
            exponentials(0, 0, BT)
            gates(1, 1, BT)

            def body(b, k, n, after):
                quads = len(edges.quads_of(n))
                if after:
                    exponentials(b + 1, (k + 1) % U, after)
                for q in range(quads):
                    edges.keep(act, b, k, n, q)
                    if q == 1 and later_size(b, 2):
                        gates(b + 2, (k + 2) % U, later_size(b, 2))

            over_blocks(act, U, body)
            act.wait_ge(end_step, 2)
            act.activation(rescale[:, :], neg_maxs[:, :], ACT.Exp, bias=top[:, :], scale=-1.0).then_inc(end_exp, 1)

        @block.vector
        def _(dve):
            edges.begin_dve(dve)
            head_matrix(dve, c, c.shares, built)
            dve.sem_inc(wide_free, 2)

            def maximum(b, k, n):
                dve.wait_ge(io_mm, b * 2 + 2)
                dve.tensor_reduce(neg_max[k][:, :], o_bank[0:H, 0:n], AX.X, ALU.max, negate=True
                                  ).then_inc(max_ready, 1)

            def scale_q(b, k, n):
                dve.wait_ge(gated, b + 1)
                dve.tensor_tensor(ce[k][:, 0, 0:n], gate[k][:, 0:n], c.inverse[0:H, cols(b, n)], ALU.mult
                                  ).then_inc(c_ready, 1)

            def scales_hi(b, k, n):
                dve.wait_ge(c_ready, b + 1)
                dve.wait_ge(exp_ready, b + 1)
                dve.tensor_copy(ce_hi[k][:, :, 0:n], ce[k][:, :, 0:n]).then_inc(hi_ready, 1)

            def scales_lo(b, k, n):
                dve.wait_ge(hi_ready, b + 1)
                dve.tensor_tensor(ce_lo[k][:, :, 0:n], ce[k][:, :, 0:n], ce_hi[k][:, :, 0:n].bitcast(F32),
                                  ALU.subtract).then_inc(ce_ready, 1)
                dve.wait_ge(max_ready, b + 1)
                dve.tensor_copy(neg_maxs[:, bass.ds(b, 1)], neg_max[k][:, :])
                dve.tensor_copy(exp_sums[:, bass.ds(b, 1)], exp_sum[k][:, :]).then_inc(noted, 1)

            maximum(0, 0, BT)
            scale_q(0, 0, BT)
            scales_hi(0, 0, BT)
            scales_lo(0, 0, BT)
            edges.prepare(dve, 0, 0, BT)

            def body(b, k, n, after):
                quads = len(edges.quads_of(n))
                if after:
                    maximum(b + 1, (k + 1) % U, after)
                for o in range(QK):
                    if o % CH < 2 and 2 * (o // CH) + o % CH < quads:
                        edges.select(dve, b, k, n, 2 * (o // CH) + o % CH)
                    dve.wait_ge(wide_mm, b * QK + o + 1)
                    dve.tensor_tensor(qk[k][:, o, 0:n], qk[k][:, o, 0:n], wide[o % 2][:, 0:n], ALU.mult
                                      ).then_inc(wide_free, 1)
                    if after:
                        if o == 2:
                            scale_q(b + 1, (k + 1) % U, after)
                            edges.prepare(dve, b + 1, (k + 1) % U, after)
                        if o == 4:
                            scales_hi(b + 1, (k + 1) % U, after)
                        if o == 6:
                            scales_lo(b + 1, (k + 1) % U, after)
                edges.rows(dve, b, k, n)

            over_blocks(dve, U, body)
            dve.wait_ge(noted, NB)
            dve.tensor_reduce(top[:, :], neg_maxs[:, :], AX.X, ALU.min).then_inc(end_step, 2)
            dve.wait_ge(end_exp, 1)
            dve.tensor_tensor(weighted[:, :], rescale[:, :], exp_sums[:, :], ALU.mult).then_inc(end_step, 1)
            dve.wait_ge(end_step, 3)
            dve.tensor_reduce(total[:, :], weighted[:, :], AX.X, ALU.add).then_inc(end_step, 1)
            dve.wait_ge(end_step, 4)
            dve.reciprocal(total_inv[:, :], total[:, :]).then_inc(end_step, 1)
            dve.wait_ge(end_step, 5)
            dve.tensor_scalar(factor[:, :], rescale[:, :], total_inv[:, :], None, ALU.mult).then_inc(end_step, 2)
            dve.wait_ge(end_mm, 1)
            dve.tensor_copy(c.factors[:, :], i_bank[:, 0:NB]).then_inc(end_step, 1)
            dve.wait_ge(end_step, 8)

        @block.gpsimd
        def _(pool):
            edges.begin_pool(pool)
            over_blocks(pool, U, lambda b, k, n, after: edges.scatter(pool, b, k, n))
            edges.finish_pool(pool)

    return edges


def mix_stage(nc, c):
    with ExitStack() as ctx:
        def sb(what, shape, dt=F32):
            return ctx.enter_context(nc.sbuf_tensor(f"mx_{what}", shape, dt))

        def bank(what):
            return ctx.enter_context(nc.psum_tensor(f"mx_{what}", [P, BT], F32))

        def sem(what):
            return ctx.enter_context(nc.semaphore(f"mx_{what}"))

        w1_hi = sb("w1_hi", [P, CH + 1, HID], F32R)
        w1_lo = sb("w1_lo", [P, CH + 1, HID], F32R)
        w2_hi = sb("w2_hi", [P, JH, DIM], F32R)
        w2_lo = sb("w2_lo", [P, JH, DIM], F32R)
        wo_hi = sb("wo_hi", [P, CH, DIM], F32R)
        wo_lo = sb("wo_lo", [P, CH, DIM], F32R)
        b1 = sb("b1", [P, JH])
        bias = sb("bias", [P, DIM])
        with ExitStack() as head:
            bias2 = head.enter_context(nc.sbuf_tensor("mx_bias2", [P, DIM], F32))
            bias_o = head.enter_context(nc.sbuf_tensor("mx_bias_o", [P, DIM], F32))
            bias_in = head.enter_context(nc.semaphore("mx_bias_in"))
            items = [(c.w1[i * P:min((i + 1) * P, DIM + EDIM), :], i, w1_hi, w1_lo) for i in range(CH + 1)]
            items += [(c.w2[i * P:(i + 1) * P, :], i, w2_hi, w2_lo) for i in range(JH)]
            items += [(c.w_out[i * P:(i + 1) * P, :], i, wo_hi, wo_lo) for i in range(CH)]
            weights = Weights(head, nc, "mx_w", [(src, hi[0:src.shape[0], i, :], lo[0:src.shape[0], i, :])
                                                 for src, i, hi, lo in items], HID)
            block = head.enter_context(nc.Block())

            @block.sync
            def _(sp):
                sp.dma_start(b1[:, :], c.b1).then_inc(bias_in, 16)
                sp.dma_start(bias2[:, :], c.b2.partition_broadcast(P)).then_inc(bias_in, 16)
                sp.dma_start(bias_o[:, :], c.b_out.partition_broadcast(P)).then_inc(bias_in, 16)
                weights.load(sp)

            @block.gpsimd
            def _(pool):
                for done in c.finished:
                    pool.sem_clear(done)

            @block.scalar
            def _(act):
                weights.split_hi(act)

            @block.vector
            def _(dve):
                weights.split_lo(dve)
                dve.wait_ge(bias_in, 48)
                dve.tensor_tensor(bias[:, :], bias2[:, :], bias_o[:, :], ALU.add)

        GROUPS = P // GT
        agg_raw = sb("agg_raw", [P, TABLES, CH, ECOLS])
        agg_sum = sb("agg_sum", [P, CH, ECOLS])
        agg_cnt = sb("agg_cnt", [P, CH])
        agg_inv = sb("agg_inv", [P, CH])
        agg_hi = sb("agg_hi", [EDIM, BT], F32R)
        agg_lo = sb("agg_lo", [EDIM, BT], F32R)
        qs = sb("qs", [P, HEADS, P])
        ks = sb("ks", [P, HEADS, P])
        kt = sb("kt", [P, P, HEADS])
        v = [sb(f"v{k}", [P, GROUPS, HDIM]) for k in range(2)]
        near = [sb(f"near{k}", [P, 4, P]) for k in range(2)]
        factor = [sb(f"factor{k}", [P, 1]) for k in range(2)]
        r_hi = [sb(f"r_hi{k}", [P, CH, P], F32R) for k in range(2)]
        r_lo = [sb(f"r_lo{k}", [P, CH, P], F32R) for k in range(2)]
        hid = sb("hid", [P, BT])
        h_hi = sb("h_hi", [P, JH, BT], F32R)
        h_lo = sb("h_lo", [P, JH, BT], F32R)
        x1 = [sb(f"x1_{k}", [P, DIM]) for k in range(2)]
        raw1, mv1, std1, rstd1 = sb("raw1", [P, 6]), sb("mv1", [P, 2]), sb("std1", [P, 1]), sb("rstd1", [P, 1])
        x1n = sb("x1n", [P, DIM])
        x1nT = sb("x1nT", [P, CH, P])
        part = [sb(f"part{k}", [P, CH]) for k in range(2)]
        turn_bank = [bank(f"turn{k}") for k in range(2)]
        r_bank, s_bank = bank("r"), bank("s")
        h_bank = [bank(f"h{k}") for k in range(2)]
        acc = [bank(f"acc{k}") for k in range(2)]
        turn_free = [sem(f"turn_free{k}") for k in range(2)]
        with_xn, base_ready = sem("with_xn"), sem("base_ready")
        norm = Norm(ctx, nc, c, "mx_norm", turn_bank, 1, turn_free, with_xn)

        table_in, agg_step, agg_turned, agg_hi_ready = sem("table_in"), sem("agg_step"), sem("agg_turned"), sem("agg_hi_ready")
        qk_in, v_in = sem("qk_in"), [sem(f"v_in{k}") for k in range(2)]
        factor_ready = sem("factor_ready")
        kt_ready = sem("kt_ready")
        scored, near_ready, mixed = sem("scored"), sem("near_ready"), sem("mixed")
        r_hi_ready, r_ready = sem("r_hi_ready"), sem("r_ready")
        h_mm, hid_ready, h_hi_ready, h_ready = sem("h_mm"), sem("hid_ready"), sem("h_hi_ready"), sem("h_ready")
        acc_mm, x1_ready, x1_stored, x1_free = sem("acc_mm"), sem("x1_ready"), sem("x1_stored"), sem("x1_free")
        raw1_ready, mv1_ready, std1_ready, rstd1_ready = sem("raw1_ready"), sem("mv1_ready"), sem("std1_ready"), sem("rstd1_ready")
        x1n_ready, x1n_turned, x1nT_ready, x1nT_stored = sem("x1n_ready"), sem("x1n_turned"), sem("x1nT_ready"), sem("x1nT_stored")
        parts_added = sem("parts_added")
        block = ctx.enter_context(nc.Block())

        AHEAD = 2
        STEPS = BT // (4 * GT)
        SLOTS = JH + CH
        S_SLOT = (0, 1, 2, 3, 7, 8, 9, 10)
        V_SLOT = (1, 2, 3, 4, 8, 9, 10, 11)

        def groups(n, step):
            t0 = step * 4 * GT
            return [(t // P, t % P, min(GT, n - t)) for t in range(t0, min(t0 + 4 * GT, n), GT)]

        def steps(n):
            return [s for s in range(STEPS) if groups(n, s)]

        def last_step(n, sub):
            return max(s for s in steps(n) if groups(n, s)[0][0] == sub)

        def turning(n, after):
            subs = len(subtiles(n))
            order = [(JH - 1 + s // 2, s % 2, "x", s) for s in range(len(subtiles(after)))]
            order += [(JH + 1, 0, "x1", 0)] if subs > 1 else []
            order += [(JH + 1, 1, "agg", 0)] if after else []
            order += [(JH + 2, 0, "x1", 1), (JH + 3, 1, "x1", 2), (SLOTS, 0, "x1", 3)] if subs > 1 else []
            return order if subs > 1 else [(JH, 0, "x1", 0)]

        def turns(n, after, which):
            return len([t for t in turning(n, after) if t[1] == which])

        def turns_before(b, which):
            first = 2 + which
            if isinstance(b, int) and b == NB - 1:
                return first + (FULL - 1) * turns(BT, BT, which) + turns(BT, TAIL, which)
            return b * turns(BT, BT, which) + first

        def numbered(b, n, after):
            use = [turns_before(b, which) for which in range(2)]
            out = []
            for at, which, kind, s in turning(n, after):
                out.append((at, which, use[which], kind, s))
                use[which] = use[which] + 1
            return out

        def act_turned(act, b, n, after, item):
            _, which, _, kind, s = item
            if kind == "x":
                norm.split_hi(act, b + 1, 0, after, s)
            elif kind == "agg":
                act.wait_ge(agg_turned, b + 2)
                act.activation(agg_hi[:, 0:after], turn_bank[1][0:EDIM, 0:after], ACT.Copy).then_inc(agg_hi_ready, 1)
            else:
                r = subtiles(n)[s]
                act.wait_ge(x1n_turned, b * CH + (s + 1))
                act.wait_ge(x1nT_stored, b * (16 * CH) + 16 * s)
                act.wait_ge(parts_added, b * CH + s)
                for ch in range(CH):
                    op = act.activation(x1nT[:, ch, 0:r], turn_bank[which][:, ch * P:ch * P + r], ACT.Copy,
                                        accum_out=part[s % 2][:, ch:ch + 1])
                op.then_inc(turn_free[which], 1)

        @block.sync
        def _(sp):
            def load_unit(b, n, u):
                pieces = subtiles(n)[2 * u:2 * u + 2]
                for half, r in enumerate(pieces):
                    at = b * BT + (2 * u + half) * P
                    for dst, row in ((qs, 0), (ks, DIM)):
                        sp.dma_start(dst[half * HDIM:(half + 1) * HDIM, :, 0:r],
                                     c.qk_scaled[row:row + DIM, bass.ds(at, r)].rearrange("(h d) t -> d h t", d=HDIM)
                                     ).then_inc(qk_in, 16)

            def load_v(b, n, s):
                r = subtiles(n)[s]
                rows = c.v.rearrange("t (h e) -> (t h) e", h=HEADS)
                at = b * (BT * HEADS) + s * P * HEADS
                full = r // GT
                sp.dma_start(v[s % 2][:, 0:full, :],
                             rows[bass.ds(at, full * P), :].rearrange("(g p) e -> p g e", p=P)
                             ).then_inc(v_in[s % 2], 16)
                if r % GT:
                    left = (r % GT) * HEADS
                    sp.dma_start(v[s % 2][0:left, full, :], rows[bass.ds(at + full * P, left), :]
                                 ).then_inc(v_in[s % 2], 16)

            def load_tables(b, n):
                for t in range(TABLES):
                    if n == BT:
                        sp.dma_start(agg_raw[:, t, :, :], c.table[t][bass.ds(b * BT, n), :]
                                     .rearrange("(s p) e -> p s e", p=P)).then_inc(table_in, 16)
                    else:
                        sp.dma_start(agg_raw[0:n, t, 0, :], c.table[t][bass.ds(b * BT, n), :]
                                     ).then_inc(table_in, 16)

            norm.load(sp, 0, 0, BT)
            load_tables(0, BT)
            load_unit(0, BT, 0)
            load_v(0, BT, 0)
            load_v(0, BT, 1)

            def body(b, k, n, after):
                subs = len(subtiles(n))
                if after:
                    sp.wait_ge(acc_mm, b * CH + AHEAD)
                    sp.wait_ge(x1_ready, b * CH + AHEAD)
                    norm.load(sp, b + 1, 1 - k, after)
                    sp.wait_ge(agg_step, b * 4 + 4)
                    load_tables(b + 1, after)
                if subs > 2:
                    sp.wait_ge(scored, b * STEPS + 4)
                    load_unit(b, n, 1)
                    for s in (2, 3):
                        sp.wait_ge(mixed, b * STEPS + (AHEAD + last_step(n, s - 2) + 1))
                        load_v(b, n, s)
                if after:
                    sp.wait_ge(scored, b * STEPS + len(steps(n)))
                    sp.sem_inc(c.passed, 1)
                    load_unit(b + 1, after, 0)
                    for s in range(min(2, len(subtiles(after)))):
                        sp.wait_ge(mixed, b * STEPS + (AHEAD + last_step(n, subs - 2 + s) + 1))
                        load_v(b + 1, after, s)

            over_blocks(sp, 2, body)

        @block.tensor
        def _(pe):
            def turn_agg(b, n, use):
                pe.wait_ge(agg_step, b * 4 + 4)
                pe.wait_ge(turn_free[1], use)
                pe.sem_inc(c.passed, 1)
                for s, r in enumerate(subtiles(n)):
                    mm = pe.transpose(turn_bank[1][0:EDIM, s * P:s * P + r], agg_sum[0:r, s, 0:EDIM], c.ident[0:r, 0:r])
                mm.then_inc(agg_turned, 1)

            def turn_x1(b, n, s, which, use):
                r = subtiles(n)[s]
                pe.wait_ge(x1n_ready, b * CH + (s + 1))
                pe.wait_ge(turn_free[which], use)
                for ch in range(CH):
                    mm = pe.transpose(turn_bank[which][:, ch * P:ch * P + r], x1n[0:r, ch * P:(ch + 1) * P],
                                      c.ident[0:r, 0:r])
                mm.then_inc(x1n_turned, 1)

            def scores(b, n, step):
                gs = groups(n, step)
                if step % 4 == 0:
                    pe.wait_ge(kt_ready, b * 2 + step // 4 + 1)
                pe.wait_ge(near_ready, b * STEPS + (AHEAD + step))
                for j, (sub, t, w) in enumerate(gs):
                    half = slice((sub % 2) * HDIM, (sub % 2 + 1) * HDIM)
                    mm = pe.matmul(s_bank[0:w * HEADS, j * P:j * P + w * HEADS],
                                   kt[half, t:t + w, :].rearrange("d t h -> d (t h)"),
                                   qs[half, :, t:t + w].rearrange("d h t -> d t h"), start=True, stop=True)
                mm.then_inc(scored, 1)

            def mix(b, n, step):
                gs = groups(n, step)
                sub = gs[0][0]
                pe.wait_ge(near_ready, b * STEPS + (AHEAD + step + 1))
                if step == last_step(n, sub) - len([s for s in steps(n) if groups(n, s)[0][0] == sub]) + 1:
                    pe.wait_ge(r_ready, b * CH + sub)
                    loads = 2 if n % GT else 1
                    pe.wait_ge(v_in[sub % 2], b * 32 + 16 * (sub // 2) + 16 * loads)
                for j, (_, t, w) in enumerate(gs):
                    g = t // GT
                    rows = w * HEADS
                    view = near[step % 2][0:rows, j, 0:rows].rearrange("p (t h) -> p t h", h=HEADS)
                    for parity in range(2):
                        out = r_bank[parity * HDIM:(parity + 1) * HDIM, :].rearrange("p (c t) -> p t c", c=CH)
                        mm = pe.matmul(out[:, t:t + w, :], v[sub % 2][0:rows, g, :], view[:, :, parity::2],
                                       start=True, stop=True)
                mm.then_inc(mixed, 1)

            def hidden(b, n, j):
                cut = slice(j * P, (j + 1) * P)
                pe.wait_ge(hid_ready, b * JH + j + 1)
                products(pe, h_bank[j % 2][:, 0:n],
                         [(w1_hi[:, ch, cut], w1_lo[:, ch, cut]) for ch in range(CH)]
                         + [(w1_hi[0:EDIM, CH, cut], w1_lo[0:EDIM, CH, cut])],
                         norm.pairs(0, slice(0, n)) + [(agg_hi[:, 0:n], agg_lo[:, 0:n])]).then_inc(h_mm, 1)

            def output(b, n, s):
                r = subtiles(n)[s]
                cut = slice(s * P, s * P + r)
                pe.wait_ge(h_ready, b * JH + JH)
                pe.wait_ge(x1_ready, b * CH + s + 1)
                products(pe, acc[s % 2][0:r, :], [(h_hi[:, j, cut], h_lo[:, j, cut]) for j in range(JH)],
                         [(w2_hi[:, j, :], w2_lo[:, j, :]) for j in range(JH)], last=False)
                pe.wait_ge(r_ready, b * CH + (s + 1))
                products(pe, acc[s % 2][0:r, :], [(r_hi[s % 2][:, ch, 0:r], r_lo[s % 2][:, ch, 0:r]) for ch in range(CH)],
                         [(wo_hi[:, ch, :], wo_lo[:, ch, :]) for ch in range(CH)], first=False).then_inc(acc_mm, 1)

            pe.sem_inc(mixed, AHEAD)
            pe.sem_inc(acc_mm, AHEAD)
            for s in range(CH):
                norm.turn(pe, 0, BT, s, s // 2)
            turn_agg(0, BT, 2)

            def early(b, n, step_free):
                for which in range(2):
                    pe.wait_ge(turn_free[which], step_free[which])
                scores(b, n, 0)
                hidden(b, n, 0)

            early(0, BT, [turns_before(0, which) for which in range(2)])

            def body(b, k, n, after):
                order = numbered(b, n, after)
                ready = [t[2] + 1 for which in range(2)
                         for t in [[u for u in order if u[1] == which and u[3] != "x1"][-1]]] if after else None
                subs = len(subtiles(n))
                if subs == 1:
                    mix(b, n, 0)
                    for step in steps(n)[1:]:
                        scores(b, n, step)
                        mix(b, n, step)
                for slot in range(1, JH + subs + 1):
                    if slot == JH + subs:
                        if after:
                            early(b + 1, after, ready)
                    elif subs > 1:
                        for step in steps(n):
                            if S_SLOT[step] == slot:
                                scores(b, n, step)
                            if V_SLOT[step] == slot:
                                mix(b, n, step)
                    if slot < JH:
                        hidden(b, n, slot)
                    elif slot < JH + subs:
                        output(b, n, slot - JH)
                    while order and order[0][0] == slot:
                        _, which, use, kind, s = order.pop(0)
                        if kind == "x":
                            norm.turn(pe, b + 1, after, s, use)
                        elif kind == "agg":
                            turn_agg(b + 1, after, use)
                        else:
                            turn_x1(b, n, s, which, use)

            over_blocks(pe, 2, body)

        @block.scalar
        def _(act):
            act.sem_inc(hid_ready, AHEAD)
            norm.deviation(act, 0, BT)
            for s in range(CH):
                norm.split_hi(act, 0, 0, BT, s)
            act.wait_ge(agg_turned, 1)
            act.activation(agg_hi[:, :], turn_bank[1][0:EDIM, :], ACT.Copy).then_inc(agg_hi_ready, 1)

            def by_token(b, n, u):
                halves = len(subtiles(n)[2 * u:2 * u + 2])
                rows, r = halves * HDIM, subtiles(n)[2 * u]
                act.wait_ge(qk_in, b * 128 + (64 * u + 32 * halves))
                act.activation(kt[0:rows, 0:r, :], ks[0:rows, :, 0:r].rearrange("d h t -> d t h"), ACT.Copy
                               ).then_inc(kt_ready, 1)

            by_token(0, BT, 0)

            def split_r(b, n, s):
                r = subtiles(n)[s]
                act.wait_ge(mixed, b * STEPS + (AHEAD + last_step(n, s) + 1))
                act.wait_ge(acc_mm, b * CH + s + 1)
                bank = r_bank[:, :].rearrange("p (c t) -> p c t", c=CH)[:, :, 0:r]
                act.activation(r_hi[s % 2][:, :, 0:r], bank, ACT.Copy).then_inc(r_hi_ready, 1)

            def deviation1(b, n, s):
                r = subtiles(n)[s]
                act.wait_ge(mv1_ready, b * CH + (s + 1))
                act.activation(std1[0:r, :], mv1[0:r, 1:2], ACT.Sqrt, bias=c.eps[0:r, :]).then_inc(std1_ready, 1)

            def rectify(b, n, j):
                act.wait_ge(h_mm, b * JH + j + 1)
                act.wait_ge(h_ready, b * JH + j)
                act.activation(hid[:, 0:n], h_bank[j % 2][:, 0:n], ACT.Relu,
                               bias=b1[:, j:j + 1]).then_inc(hid_ready, 1)
                act.wait_ge(hid_ready, b * JH + (AHEAD + j + 1))
                if j == 0:
                    act.wait_ge(acc_mm, b * CH + AHEAD)
                act.activation(h_hi[:, j, 0:n], hid[:, 0:n], ACT.Copy).then_inc(h_hi_ready, 1)

            rectify(0, BT, 0)

            def body(b, k, n, after):
                order = numbered(b, n, after)
                subs = len(subtiles(n))
                if subs == 1:
                    split_r(b, n, 0)
                for slot in range(1, JH + subs + 1):
                    if subs > 1:
                        for s in range(subs):
                            if V_SLOT[last_step(n, s)] == slot:
                                split_r(b, n, s)
                    if slot < JH:
                        rectify(b, n, slot)
                        if after and slot == 5:
                            norm.deviation(act, b + 1, after)
                        if subs > 2 and slot == 4:
                            act.wait_ge(scored, b * STEPS + 4)
                            by_token(b, n, 1)
                    elif slot < JH + subs:
                        deviation1(b, n, slot - JH)
                        if after and slot == 10:
                            act.wait_ge(scored, b * STEPS + STEPS)
                            by_token(b + 1, after, 0)
                    elif after:
                        rectify(b + 1, after, 0)
                    while order and order[0][0] == slot:
                        act_turned(act, b, n, after, order.pop(0))

            over_blocks(act, 2, body)

        @block.vector
        def _(dve):
            def divide_sums(b, n):
                r, ns = subtiles(n)[-1], len(subtiles(n))
                dve.wait_ge(table_in, b * (16 * TABLES) + 16 * TABLES)
                dve.tensor_reduce(agg_sum[0:r, 0:ns, :], agg_raw[0:r, :, 0:ns, :].rearrange("p t s e -> p s e t"),
                                  AX.X, ALU.add).then_inc(agg_step, 1)
                dve.wait_ge(agg_step, b * 4 + 1)
                dve.tensor_scalar(agg_cnt[0:r, 0:ns], agg_sum[0:r, 0:ns, EDIM], 1.0, None, ALU.max).then_inc(agg_step, 1)
                dve.wait_ge(agg_step, b * 4 + 2)
                dve.reciprocal(agg_inv[0:r, 0:ns], agg_cnt[0:r, 0:ns]).then_inc(agg_step, 1)
                dve.wait_ge(agg_step, b * 4 + 3)
                dve.tensor_tensor(agg_sum[0:r, 0:ns, 0:EDIM], agg_sum[0:r, 0:ns, 0:EDIM],
                                  agg_inv[0:r, 0:ns].unsqueeze(2).to_broadcast([r, ns, EDIM]),
                                  ALU.mult).then_inc(agg_step, 1)

            def split_agg(b, n):
                dve.wait_ge(agg_hi_ready, b + 1)
                dve.tensor_tensor(agg_lo[:, 0:n], turn_bank[1][0:EDIM, 0:n], agg_hi[:, 0:n].bitcast(F32),
                                  ALU.subtract).then_inc(turn_free[1], 1)

            def take_factor(b, k):
                dve.tensor_copy(factor[k][:, :], c.factors[:, bass.ds(b, 1)]).then_inc(factor_ready, 1)

            def neighbours(b, k, n, step):
                gs = groups(n, step)
                if step == 0:
                    dve.wait_ge(factor_ready, b + 1)
                dve.wait_ge(scored, b * STEPS + step + 1)
                dve.wait_ge(mixed, b * STEPS + step + 1)
                whole = len([g for g in gs if g[2] == GT])
                if whole:
                    op = dve.scalar_tensor_tensor(
                        out=near[step % 2][:, 0:whole, :],
                        in0=s_bank[:, 0:whole * P].rearrange("p (j f) -> p j f", f=P),
                        scalar=factor[k][:, :], in1=c.same_token[:, :].unsqueeze(1).to_broadcast([P, whole, P]),
                        op0=ALU.mult, op1=ALU.mult)
                if whole < len(gs):
                    rows = gs[-1][2] * HEADS
                    op = dve.scalar_tensor_tensor(
                        out=near[step % 2][0:rows, whole, 0:rows], in0=s_bank[0:rows, whole * P:whole * P + rows],
                        scalar=factor[k][0:rows, :], in1=c.same_token[0:rows, 0:rows], op0=ALU.mult, op1=ALU.mult)
                op.then_inc(near_ready, 1)

            def split_r(b, n, s):
                r = subtiles(n)[s]
                dve.wait_ge(r_hi_ready, b * CH + (s + 1))
                bank = r_bank[:, :].rearrange("p (c t) -> p c t", c=CH)[:, :, 0:r]
                dve.tensor_tensor(r_lo[s % 2][:, :, 0:r], bank, r_hi[s % 2][:, :, 0:r].bitcast(F32),
                                  ALU.subtract).then_inc(r_ready, 1)

            def finish(b, k, n, s):
                r = subtiles(n)[s]
                at = b * CH + (s + 1)
                dve.wait_ge(acc_mm, at + AHEAD)
                dve.wait_ge(base_ready, at)
                dve.wait_ge(x1_free, b * CH + s + 1)
                dve.tensor_tensor(x1[s % 2][0:r, :], acc[s % 2][0:r, :], norm.x[k][0:r, s, :], ALU.add
                                  ).then_inc(x1_ready, 1)
                dve.wait_ge(x1_ready, at + AHEAD)
                dve.bn_stats(raw1[0:r, :], x1[s % 2][0:r, :]).then_inc(raw1_ready, 1)
                dve.wait_ge(raw1_ready, at)
                dve.sem_inc(c.passed, 1)
                dve.bn_aggr(mv1[0:r, :], raw1[0:r, :]).then_inc(mv1_ready, 1)
                dve.wait_ge(std1_ready, at)
                dve.reciprocal(rstd1[0:r, :], std1[0:r, :]).then_inc(rstd1_ready, 1)
                dve.wait_ge(rstd1_ready, at)
                dve.wait_ge(x1n_turned, b * CH + s)
                dve.tensor_scalar(x1n[0:r, :], x1[s % 2][0:r, :], mv1[0:r, 0:1], rstd1[0:r, :],
                                  ALU.subtract, ALU.mult).then_inc(x1n_ready, 1)

            def add_part(b, s, which, use):
                dve.wait_ge(turn_free[which], use + 1)
                dve.wait_ge(parts_added, b * CH + (s + 1))
                dve.tensor_tensor(c.token_sum[:, :], c.token_sum[:, :], part[s % 2][:, :], ALU.add
                                  ).then_inc(parts_added, 1)

            dve.sem_inc(near_ready, AHEAD)
            dve.sem_inc(x1_ready, AHEAD)
            dve.memset(c.token_sum[:, :], 0.0).then_inc(parts_added, 1)
            norm.first_on_dve(dve)
            divide_sums(0, BT)
            split_agg(0, BT)
            take_factor(0, 0)

            def low(b, n, j):
                dve.wait_ge(h_hi_ready, b * JH + j + 1)
                dve.tensor_tensor(h_lo[:, j, 0:n], hid[:, 0:n], h_hi[:, j, 0:n].bitcast(F32),
                                  ALU.subtract).then_inc(h_ready, 1)

            neighbours(0, 0, BT, 0)
            low(0, BT, 0)

            def body(b, k, n, after):
                order = numbered(b, n, after)
                subs = len(subtiles(n))
                if subs == 1:
                    for step in steps(n)[1:]:
                        neighbours(b, k, n, step)
                    split_r(b, n, 0)
                for slot in range(1, JH + subs + 1):
                    if slot == JH + subs:
                        if after:
                            neighbours(b + 1, 1 - k, after, 0)
                            low(b + 1, after, 0)
                    elif subs > 1:
                        for step in steps(n):
                            if S_SLOT[step] == slot:
                                neighbours(b, k, n, step)
                        for s in range(subs):
                            if V_SLOT[last_step(n, s)] == slot:
                                split_r(b, n, s)
                    if slot < JH:
                        low(b, n, slot)
                    elif slot < JH + subs:
                        finish(b, k, n, slot - JH)
                    if after and slot <= len(subtiles(after)):
                        norm.stats(dve, b + 1, 1 - k, after, slot - 1)
                    if after and slot == 5:
                        norm.aggregate(dve, b + 1, 1 - k, after)
                    if after and slot == 6:
                        norm.invert(dve, b + 1, after)
                        take_factor(b + 1, 1 - k)
                        for s in range(min(2, len(subtiles(after)))):
                            norm.normalise(dve, b + 1, 1 - k, after, s)
                    if after and slot == 7:
                        divide_sums(b + 1, after)
                    while order and order[0][0] == slot:
                        _, which, use, kind, s = order.pop(0)
                        if kind == "x":
                            norm.split_lo(dve, b + 1, 0, after, s)
                            if s + 2 < len(subtiles(after)):
                                norm.normalise(dve, b + 1, 1 - k, after, s + 2)
                        elif kind == "agg":
                            split_agg(b + 1, after)
                        else:
                            add_part(b, s, which, use)

            over_blocks(dve, 2, body)

        @block.gpsimd
        def _(pool):
            def bases(b, k, n):
                for s, r in enumerate(subtiles(n)):
                    at = b * CH + (s + 1)
                    pool.wait_ge(norm.xn_ready, at)
                    pool.tensor_tensor(norm.x[k][0:r, s, :], norm.x[k][0:r, s, :], norm.xn[s % 2][0:r, :], ALU.add
                                       ).then_inc(with_xn, 1)
                    pool.wait_ge(with_xn, at)
                    pool.tensor_tensor(norm.x[k][0:r, s, :], norm.x[k][0:r, s, :], bias[0:r, :], ALU.add
                                       ).then_inc(base_ready, 1)

            pool.sem_inc(x1_free, AHEAD)
            bases(0, 0, BT)

            def body(b, k, n, after):
                turned = {s: (turn_free[which], use + 1) for _, which, use, kind, s in numbered(b, n, after)
                          if kind == "x1"}
                if after:
                    bases(b + 1, 1 - k, after)
                for s, r in enumerate(subtiles(n)):
                    at = b * BT + s * P
                    pool.wait_ge(x1_ready, b * CH + (AHEAD + s + 1))
                    pool.dma_start(c.x1[bass.ds(at, r), :], x1[s % 2][0:r, :]).then_inc(x1_stored, 16)
                    pool.wait_ge(*turned[s])
                    pool.dma_start(c.x1n[:, bass.ds(at, r)].rearrange("(c p) t -> p c t", p=P), x1nT[:, :, 0:r]
                                   ).then_inc(x1nT_stored, 16)
                    pool.wait_ge(x1_stored, b * (16 * CH) + 16 * (s + 1))
                    pool.sem_inc(x1_free, 1)
                    pool.wait_ge(x1nT_stored, b * (16 * CH) + 16 * (s + 1))

            over_blocks(pool, 2, body)


def expert_stage(nc, c):
    with ExitStack() as ctx:
        def sb(what, shape, dt=F32):
            return ctx.enter_context(nc.sbuf_tensor(f"ex_{what}", shape, dt))

        def bank(what):
            return ctx.enter_context(nc.psum_tensor(f"ex_{what}", [P, BT], F32))

        def sem(what):
            return ctx.enter_context(nc.semaphore(f"ex_{what}"))

        w_gate = sb("w_gate", [P, CH, EXPERTS])
        b_gate = sb("b_gate", [1, EXPERTS])
        mean = sb("mean", [P, CH])
        logit, prob_e, prob = sb("logit", [1, EXPERTS]), sb("prob_e", [1, EXPERTS]), sb("prob", [1, EXPERTS])
        neg_top, total, total_inv = sb("neg_top", [1, 1]), sb("total", [1, 1]), sb("total_inv", [1, 1])
        other, rank = sb("other", [1, EXPERTS]), sb("rank", [1, EXPERTS])
        pick = sb("pick", [1, 2])
        pick_all = sb("pick_all", [P, 2])
        row_f = sb("row_f", [P, CH])
        row = sb("row", [P, CH], I32)
        expert = sb("expert", [P, 1], I32)
        w_raw = sb("w_raw", [P, CH, DIM])
        w_hi = sb("w_hi", [P, CH, DIM], F32R)
        w_lo = sb("w_lo", [P, CH, DIM], F32R)
        b_raw = sb("b_raw", [P, DIM])
        xT = [sb(f"xT{k}", [P, CH, BT]) for k in range(2)]
        xT_hi = [sb(f"xT_hi{k}", [P, CH, BT], F32R) for k in range(2)]
        xT_lo = [sb(f"xT_lo{k}", [P, CH, BT], F32R) for k in range(2)]
        x1 = [sb(f"x1_{k}", [P, CH, DIM]) for k in range(2)]
        y = [sb(f"y{k}", [P, DIM]) for k in range(2)]
        done = [sb(f"done{k}", [P, CH, DIM]) for k in range(2)]
        small, wide = bank("small"), bank("wide")
        BANKS = 4
        y_bank = [bank(f"y_bank{k}") for k in range(BANKS)]
        gate_in, gate_step, gate_mm, gate_exp = sem("gate_in"), sem("gate_step"), sem("gate_mm"), sem("gate_exp")
        gathered, w_hi_ready, w_ready = sem("gathered"), sem("w_hi_ready"), sem("w_ready")
        x_in, x1_in = [sem(f"x_in{k}") for k in range(2)], [sem(f"x1_in{k}") for k in range(2)]
        xT_hi_ready, xT_ready = sem("xT_hi_ready"), sem("xT_ready")
        y_mm, y_ready, y_done, stored, done_free = sem("y_mm"), sem("y_ready"), sem("y_done"), sem("stored"), sem("done_free")
        block = ctx.enter_context(nc.Block())

        @block.sync
        def _(sp):
            sp.dma_start(w_gate[:, :, :], c.w_gate.rearrange("(c p) e -> p c e", p=P)).then_inc(gate_in, 16)
            sp.dma_start(b_gate[:, :], c.b_gate.rearrange("(a e) -> a e", a=1)).then_inc(gate_in, 16)

            def load(b, k, n):
                sp.dma_start(xT[k][:, :, 0:n], c.x1n[:, cols(b, n)].rearrange("(c p) t -> p c t", p=P)
                             ).then_inc(x_in[k], 16)
                if n == BT:
                    sp.dma_start(x1[k][:, :, :], c.x1[cols(b, n), :].rearrange("(s p) d -> p s d", p=P)
                                 ).then_inc(x1_in[k], 16)
                else:
                    sp.dma_start(x1[k][0:n, 0, :], c.x1[cols(b, n), :]).then_inc(x1_in[k], 16)

            load(0, 0, BT)
            load(1, 1, BT)

            def body(b, k, n, after):
                ns = len(subtiles(n))
                sp.wait_ge(y_done, b * CH + ns)
                if not isinstance(b, int) or b + 2 < NB:
                    load(b + 2, k, TAIL if isinstance(b, int) and b + 2 == FULL else BT)
                sp.wait_ge(stored, b * 16)
                sp.sem_inc(done_free, 1)
                if n == BT:
                    sp.dma_start(c.out[cols(b, n), :].rearrange("(s p) d -> p s d", p=P), done[k][:, :, :]
                                 ).then_inc(stored, 16)
                else:
                    sp.dma_start(c.out[cols(b, n), :], done[k][0:n, 0, :]).then_inc(stored, 16)

            over_blocks(sp, 2, body)
            sp.wait_ge(stored, 16 * NB)

        @block.gpsimd
        def _(pool):
            pool.wait_ge(gate_step, 13)
            for ch in range(CH):
                pool.indirect_dma_start(w_raw[:, ch, :], None, c.w_exp,
                                        bass.IndirectOffsetOnAxis(ap=row[:, ch:ch + 1], axis=0),
                                        bounds_check=EXPERTS * DIM - 1).then_inc(gathered, 16)
            pool.indirect_dma_start(b_raw[:, :], None, c.b_exp,
                                    bass.IndirectOffsetOnAxis(ap=expert[:, :], axis=0),
                                    bounds_check=EXPERTS - 1).then_inc(gathered, 16)

        @block.tensor
        def _(pe):
            pe.wait_ge(gate_in, 32)
            pe.wait_ge(gate_step, 1)
            for ch in range(CH):
                mm = pe.matmul(small[0:1, 0:EXPERTS], mean[:, ch:ch + 1], w_gate[:, ch, :], start=ch == 0,
                               stop=ch == CH - 1)
            mm.then_inc(gate_mm, 1)
            pe.wait_ge(gate_step, 10)
            pe.matmul(wide[:, 0:2], c.ones_row[:, :], pick[:, :], start=True, stop=True).then_inc(gate_mm, 1)
            pe.wait_ge(w_ready, CH)

            def body(b, k, n, after):
                pe.wait_ge(xT_ready, b + 1)
                for s, r in enumerate(subtiles(n)):
                    cut = slice(s * P, s * P + r)
                    pe.wait_ge(y_ready, b * CH + s + 1)
                    products(pe, y_bank[s % BANKS][0:r, :], [(xT_hi[k][:, ch, cut], xT_lo[k][:, ch, cut]) for ch in range(CH)],
                             [(w_hi[:, ch, :], w_lo[:, ch, :]) for ch in range(CH)]).then_inc(y_mm, 1)

            over_blocks(pe, 2, body)

        @block.scalar
        def _(act):
            act.wait_ge(gate_step, 3)
            act.activation(prob_e[:, :], logit[:, :], ACT.Exp, bias=neg_top[:, :], accum_out=total[:, :]
                           ).then_inc(gate_exp, 1)
            for ch in range(CH):
                act.wait_ge(gathered, 16 * (CH + 1))
                act.activation(w_hi[:, ch, :], w_raw[:, ch, :], ACT.Copy).then_inc(w_hi_ready, 1)

            for b in range(2):
                act.wait_ge(x_in[b], 16)
                act.activation(xT_hi[b][:, :, :], xT[b][:, :, :], ACT.Copy).then_inc(xT_hi_ready, 1)

            def ahead(b, k, n, after):
                if isinstance(b, int) and b + 2 >= NB:
                    return
                nn = TAIL if isinstance(b, int) and b + 2 == FULL else BT
                act.wait_ge(x_in[k], landed(b, k, 2) + 16)
                act.wait_ge(y_mm, b * CH + CH)
                act.activation(xT_hi[k][:, :, 0:nn], xT[k][:, :, 0:nn], ACT.Copy).then_inc(xT_hi_ready, 1)

            over_blocks(act, 2, ahead)

        @block.vector
        def _(dve):
            def step(op):
                op.then_inc(gate_step, 1)

            step(dve.tensor_scalar(mean[:, :], c.token_sum[:, :], 1.0 / TOKENS, None, ALU.mult))
            dve.wait_ge(gate_mm, 1)
            step(dve.tensor_tensor(logit[:, :], small[0:1, 0:EXPERTS], b_gate[:, :], ALU.add))
            dve.wait_ge(gate_step, 2)
            step(dve.tensor_reduce(neg_top[:, :], logit[:, :], AX.X, ALU.max, negate=True))
            dve.wait_ge(gate_exp, 1)
            step(dve.reciprocal(total_inv[:, :], total[:, :]))
            dve.wait_ge(gate_step, 4)
            step(dve.tensor_scalar(prob[:, :], prob_e[:, :], total_inv[:, :], None, ALU.mult))
            dve.wait_ge(gate_step, 5)
            step(dve.tensor_reduce(pick[:, 1:2], prob[:, :], AX.X, ALU.max))
            dve.wait_ge(gate_step, 6)
            step(dve.tensor_scalar(other[:, :], prob[:, :], pick[:, 1:2], None, ALU.is_lt))
            dve.wait_ge(gate_step, 7)
            step(dve.scalar_tensor_tensor(out=rank[:, :], in0=other[:, :], scalar=float(EXPERTS),
                                          in1=c.expert_no[:, :], op0=ALU.mult, op1=ALU.add))
            dve.wait_ge(gate_step, 8)
            dve.tensor_reduce(pick[:, 0:1], rank[:, :], AX.X, ALU.min).then_inc(gate_step, 2)
            dve.wait_ge(gate_mm, 2)
            step(dve.tensor_copy(pick_all[:, :], wide[:, 0:2]))
            dve.wait_ge(gate_step, 11)
            dve.tensor_copy(expert[:, :], pick_all[:, 0:1])
            step(dve.scalar_tensor_tensor(out=row_f[:, :], in0=pick_all[:, 0:1].to_broadcast([P, CH]),
                                          scalar=float(DIM), in1=c.feat[:, :], op0=ALU.mult, op1=ALU.add))
            dve.wait_ge(gate_step, 12)
            step(dve.tensor_copy(row[:, :], row_f[:, :]))
            for ch in range(CH):
                dve.wait_ge(w_hi_ready, ch + 1)
                dve.tensor_tensor(w_lo[:, ch, :], w_raw[:, ch, :], w_hi[:, ch, :].bitcast(F32), ALU.subtract
                                  ).then_inc(w_ready, 1)

            def split(b, k, n):
                dve.wait_ge(xT_hi_ready, b + 1)
                dve.tensor_tensor(xT_lo[k][:, :, 0:n], xT[k][:, :, 0:n], xT_hi[k][:, :, 0:n].bitcast(F32),
                                  ALU.subtract).then_inc(xT_ready, 1)

            dve.sem_inc(y_ready, BANKS)
            split(0, 0, BT)

            def body(b, k, n, after):
                if after:
                    split(b + 1, 1 - k, after)
                dve.wait_ge(x1_in[k], landed(b, k, 2))
                for s, r in enumerate(subtiles(n)):
                    at = b * CH + (s + 1)
                    dve.wait_ge(y_mm, at)
                    dve.tensor_tensor(y[s % 2][0:r, :], y_bank[s % BANKS][0:r, :], b_raw[0:r, :], ALU.add).then_inc(y_ready, 1)
                    dve.wait_ge(y_ready, at + BANKS)
                    if s == 0:
                        dve.wait_ge(done_free, b)
                    dve.scalar_tensor_tensor(out=done[k][0:r, s, :], in0=y[s % 2][0:r, :], scalar=pick_all[0:r, 1:2],
                                             in1=x1[k][0:r, s, :], op0=ALU.mult, op1=ALU.add).then_inc(y_done, 1)

            over_blocks(dve, 2, body)

def kernel_body(nc, c):
    with ExitStack() as ctx:
        def sb(what, shape, dt=F32):
            return ctx.enter_context(nc.sbuf_tensor(what, shape, dt))

        c.scattered = [ctx.enter_context(nc.semaphore(f"scattered{t}")) for t in range(TABLES)]
        c.passed = ctx.enter_context(nc.semaphore("passed"))
        c.ident = sb("ident", [P, P])
        c.same_token = sb("same_token", [P, P])
        c.eps = sb("eps", [P, 1])
        c.ones_row = sb("ones_row", [1, P])
        c.feat = sb("feat", [P, CH])
        c.expert_no = sb("expert_no", [1, EXPERTS])
        c.factors = sb("factors", [P, NB])
        c.token_sum = sb("token_sum", [P, CH])
        with ExitStack() as early:
            def sb2(what, shape, dt=F32):
                return early.enter_context(nc.sbuf_tensor(what, shape, dt))

            c.ident_r = sb2("ident_r", [P, P], F32R)
            c.upper = sb2("upper", [P, P])
            c.sel = sb2("sel", [2 * HEADS, QK * P], F32R)
            c.row_sel = sb2("row_sel", [HEADS, P])
            c.spare = sb2("spare", [P, 1])
            c.bias_v = sb2("bias_v", [P, DIM])
            c.bias_qk = sb2("bias_qk", [P, QK])
            c.sums = sb2("sums", [P, QK])
            c.shares = sb2("shares", [P, QK])
            c.heads = sb2("heads", [P, QK, 2 * HEADS])
            constants_stage(nc, c)
            edges = project_stage(nc, c)
            with nc.sbuf_tensor("inverse", [2 * HEADS, TOKENS], F32) as c.inverse:
                edges = norms_stage(nc, c, edges)
                edges = scale_stage(nc, c, edges)
        mix_stage(nc, c)
        expert_stage(nc, c)


def _layouts(inp):
    import numpy as np
    arr = {n: np.asarray(a) for n, a in inp.items()}
    w = arr["L0_mix_W_qkv"].reshape(HEADS, 3, HDIM, DIM).transpose(1, 0, 2, 3).reshape(3 * DIM, DIM)
    bq = arr["L0_mix_b_qkv"].reshape(HEADS, 3, HDIM).transpose(1, 0, 2).reshape(3 * DIM)
    out = {
        "x": arr["x"], "dst": arr["dst"], "edge_attr": arr["edge_attr_64"],
        "w_qkv": w.T, "b_qk": bq[:2 * DIM].reshape(QK, P).T, "b_v": bq[2 * DIM:],
        "w1": arr["L0_gnn_W1"], "b1": arr["L0_gnn_b1"].reshape(JH, P).T, "w2": arr["L0_gnn_W2"], "b2": arr["L0_gnn_b2"],
        "w_out": arr["L0_mix_W_out"].T, "b_out": arr["L0_mix_b_out"],
        "w_gate": arr["L0_ffn_Wg"], "b_gate": arr["L0_ffn_bg"],
        "w_exp": arr["L0_ffn_We"].reshape(EXPERTS * DIM, DIM), "b_exp": arr["L0_ffn_be"],
    }
    return {n: np.ascontiguousarray(a) for n, a in out.items()}


def build(nc, shapes):
    c = Shared()

    def given(name):
        shape, dtype = shapes[name]
        return nc.dram_tensor(f"in_{name}", shape, dtype, kind="ExternalInput").ap()

    c.x, c.dst, c.edge_attr = given("x"), given("dst"), given("edge_attr")
    c.w_qkv, c.b_qk, c.b_v = given("w_qkv"), given("b_qk"), given("b_v")
    c.w1, c.b1, c.w2, c.b2 = given("w1"), given("b1"), given("w2"), given("b2")
    c.w_out, c.b_out = given("w_out"), given("b_out")
    c.w_gate, c.b_gate = given("w_gate"), given("b_gate")
    c.w_exp, c.b_exp = given("w_exp"), given("b_exp")
    c.out = nc.dram_tensor("out", (TOKENS, DIM), F32, kind="ExternalOutput").ap()
    c.v = nc.dram_tensor("v_rows", [TOKENS, DIM], F32, kind="Internal").ap()
    c.qk = nc.dram_tensor("qk_T", [2 * DIM, TOKENS], F32, kind="Internal").ap()
    c.qk_scaled = nc.dram_tensor("qk_scaled_T", [2 * DIM, TOKENS], F32, kind="Internal").ap()
    c.x1 = nc.dram_tensor("x1_rows", [TOKENS, DIM], F32, kind="Internal").ap()
    c.x1n = nc.dram_tensor("x1n_T", [DIM, TOKENS], F32, kind="Internal").ap()
    c.table = [nc.dram_tensor(f"table{t}", [TROWS, ECOLS], F32, kind="Internal").ap() for t in range(TABLES)]
    kernel_body(nc, c)


def kernel(**inputs):
    import numpy as _np
    import concourse.bacc as _bacc
    from concourse.bass_utils import run_bass_kernel_spmd as _run

    arrays = _layouts(inputs)
    nc = _bacc.Bacc("TRN2", target_bir_lowering=False, num_devices=1)
    build(nc, {n: (a.shape, mybir.dt.from_np(a.dtype)) for n, a in arrays.items()})
    r = _run(nc, [{f"in_{n}": a for n, a in arrays.items()}], core_ids=[0])
    return r.results[0]["out"]
```

```python
from contextlib import ExitStack

import concourse.bass as bass
from concourse import mybir

ALU = mybir.AluOpType
ACT = mybir.ActivationFunctionType
AX = mybir.AxisListType
F32 = mybir.dt.float32
F32R = mybir.dt.float32r
I32 = mybir.dt.int32

P = 128
TOKENS = 6250
DIM = 512
HEADS = 8
HDIM = DIM // HEADS
EDGES = 106250
EDIM = 64
HID = 1024
EXPERTS = 16
CH = DIM // P
QK = 2 * CH
JH = HID // P
BT = 512
FULL = TOKENS // BT
TAIL = TOKENS - FULL * BT
NB = FULL + 1
GT = P // HEADS
EPS = 1e-5
MID = TOKENS // 2
TABLES = 4
TROWS = 6400
ECOLS = EDIM + 1


def subtiles(n):
    return [min(P, n - s) for s in range(0, n, P)]


def over_blocks(eng, unroll, body):
    looped = (FULL - 1) // unroll
    with eng.Fori(0, looped) as i:
        for k in range(unroll):
            body(i * unroll + k, k, BT, BT)
    for b in range(looped * unroll, NB):
        sizes = [BT] * FULL + [TAIL, 0]
        body(b, b % unroll, sizes[b], sizes[b + 1])


def landed(b, k, unroll, dmas=1):
    return (b - k) * (16 * dmas // unroll) + 16 * dmas


def later_size(b, by):
    sizes = [BT] * FULL + [TAIL] + [0] * by
    return sizes[b + by] if isinstance(b, int) else BT


def cols(b, n):
    return bass.ds(b * BT, n)


class Edges:

    def __init__(self, ctx, nc, c, name, first_edge, tiles, tail_tiles, tail_rows, unroll, scattered, psum,
                 pieces=1):
        self.c, self.first, self.tiles, self.unroll = c, first_edge, tiles, unroll
        self.tail_tiles, self.tail_rows = tail_tiles, tail_rows
        self.quads = tiles // 4
        self.scattered = dict(scattered)
        self.pieces = pieces
        self.last_edge = first_edge + FULL * tiles * P + tail_tiles * tail_rows

        def sb(what, shape, dt=F32):
            return ctx.enter_context(nc.sbuf_tensor(f"{name}_{what}", shape, dt))

        self.sems = []

        def sem(what):
            self.sems.append(ctx.enter_context(nc.semaphore(f"{name}_{what}")))
            return self.sems[-1]

        self.attr = [sb(f"attr{k}", [P, tiles, ECOLS]) for k in range(unroll)]
        self.dst = [sb(f"dst{k}", [P, tiles], I32) for k in range(unroll)]
        self.dst_f = [sb(f"dst_f{k}", [P, tiles]) for k in range(unroll)]
        self.dst_r = [sb(f"dst_r{k}", [P, tiles], F32R) for k in range(unroll)]
        self.later = [sb(f"later{k}", [P, tiles]) for k in range(unroll)]
        self.row_a = [sb(f"row_a{k}", [P, tiles]) for k in range(unroll)]
        self.row_b = [sb(f"row_b{k}", [P, tiles]) for k in range(unroll)]
        self.row = [sb(f"row{k}", [P, tiles], I32) for k in range(unroll)]
        self.sums = [sb(f"sums{k}", [P, tiles, ECOLS]) for k in range(unroll)]
        self.sel = [sb(f"sel{k}", [P, 4, P]) for k in range(2)]
        self.p_dst, self.p_sum = psum
        self.spare_banks = len(self.p_dst) - 1

        self.edges_in = [sem(f"edges_in{k}") for k in range(unroll)]
        self.ones_set = sem("ones_set")
        self.dst_ready = sem("dst_ready")
        self.spread = sem("spread")
        self.selected = sem("selected")
        self.summed = sem("summed")
        self.kept = sem("kept")
        self.dst_step = sem("dst_step")
        self.row_step = sem("row_step")
        self.rows_ready = sem("rows_ready")
        self.sums_free = sem("sums_free")

    def shape(self, n):
        return (self.tiles, P) if n == BT else (self.tail_tiles, self.tail_rows)

    def quads_of(self, n):
        m = self.shape(n)[0]
        return [(q, min(4, m - q)) for q in range(0, m, 4)]

    def load(self, sp, b, k, n, guard):
        m, rows = self.shape(n)
        if guard is not None:
            sp.wait_ge(self.summed, guard)
        at = self.first + b * (self.tiles * P)
        sp.dma_start(self.dst[k][0:rows, 0:m],
                     self.c.dst[bass.ds(at, m * rows)].rearrange("(p m) -> p m", m=m)).then_inc(self.edges_in[k], 16)
        self.load_piece(sp, b, k, n, 0)

    def load_piece(self, sp, b, k, n, i):
        m, rows = self.shape(n)
        at = self.first + b * (self.tiles * P)
        cut = slice(m * i // self.pieces, m * (i + 1) // self.pieces)
        sp.dma_start(self.attr[k][0:rows, cut, 0:EDIM],
                     self.c.edge_attr[bass.ds(at, m * rows), :].rearrange("(p m) d -> p m d", m=m)[:, cut, :]
                     ).then_inc(self.edges_in[k], 16)

    def load_first(self, sp):
        sp.wait_ge(self.ones_set, self.unroll)
        self.load(sp, 0, 0, BT, None)
        for i in range(1, self.pieces):
            self.load_piece(sp, 0, 0, BT, i)

    def load_next(self, sp, b, k, after):
        if after:
            self.load(sp, b + 1, (k + 1) % self.unroll, after, self.quads * b)

    def load_more(self, sp, b, k, after, i):
        if after:
            self.load_piece(sp, b + 1, (k + 1) % self.unroll, after, i)

    def begin_dve(self, dve):
        for k in range(self.unroll):
            dve.memset(self.attr[k][:, :, EDIM:ECOLS], 1.0).then_inc(self.ones_set, 1)
        if self.spare_banks:
            dve.sem_inc(self.selected, self.spare_banks)

    def begin_act(self, act):
        if self.spare_banks:
            act.sem_inc(self.kept, self.spare_banks)

    def prepare(self, dve, b, k, n):
        m, rows = self.shape(n)
        dve.wait_ge(self.edges_in[k], landed(b, k, self.unroll, 1 + self.pieces))
        dve.tensor_scalar(self.dst_f[k][0:rows, 0:m], self.dst[k][0:rows, 0:m], float(-MID), None,
                          ALU.add).then_inc(self.dst_step, 1)
        dve.wait_ge(self.dst_step, b + 1)
        dve.tensor_scalar(self.row_a[k][0:rows, 0:m], self.dst_f[k][0:rows, 0:m], self.c.spare[0:rows, :],
                          None, ALU.subtract)
        dve.tensor_copy(self.dst_r[k][0:rows, 0:m], self.dst_f[k][0:rows, 0:m]).then_inc(self.dst_ready, 1)

    def spread_dst(self, pe, b, k, n, q):
        rows = self.shape(n)[1]
        if q == 0:
            pe.wait_ge(self.dst_ready, b + 1)
        pe.wait_ge(self.selected, b * self.quads + q)
        j0, w = self.quads_of(n)[q]
        for j in range(w):
            mm = pe.matmul(self.p_dst[(k * self.quads + q) % len(self.p_dst)][0:rows, j * P:j * P + rows],
                           self.dst_r[k][0:rows, j0 + j:j0 + j + 1].to_broadcast([rows, rows]),
                           self.c.ident_r[0:rows, 0:rows], start=True, stop=True)
        mm.then_inc(self.spread, 1)

    def select(self, dve, b, k, n, q):
        rows = self.shape(n)[1]
        dve.wait_ge(self.spread, b * self.quads + q + 1)
        j0, w = self.quads_of(n)[q]
        for j in range(w):
            t = j0 + j
            op = dve.scalar_tensor_tensor(
                out=self.sel[(k * self.quads + q) % 2][0:rows, j, 0:rows], in0=self.p_dst[(k * self.quads + q) % len(self.p_dst)][0:rows, j * P:j * P + rows],
                scalar=self.dst_f[k][0:rows, t:t + 1], in1=self.c.upper[0:rows, 0:rows],
                op0=ALU.is_equal, op1=ALU.mult, accum_out=self.later[k][0:rows, t:t + 1])
        op.then_inc(self.selected, 1)

    def sum_tile(self, pe, b, k, n, q):
        rows = self.shape(n)[1]
        pe.wait_ge(self.selected, b * self.quads + (self.spare_banks + q + 1))
        pe.wait_ge(self.kept, b * self.quads + q)
        j0, w = self.quads_of(n)[q]
        for j in range(w):
            mm = pe.matmul(self.p_sum[(k * self.quads + q) % len(self.p_sum)][0:rows, j * ECOLS:(j + 1) * ECOLS], self.sel[(k * self.quads + q) % 2][0:rows, j, 0:rows],
                           self.attr[k][0:rows, j0 + j, :], start=True, stop=True)
        mm.then_inc(self.summed, 1)

    def keep(self, act, b, k, n, q):
        rows = self.shape(n)[1]
        act.wait_ge(self.summed, b * self.quads + q + 1)
        if q == 0:
            act.wait_ge(self.sums_free, b + 1)
        j0, w = self.quads_of(n)[q]
        act.activation(self.sums[k][0:rows, j0:j0 + w, :], self.p_sum[(k * self.quads + q) % len(self.p_sum)][0:rows, 0:w * ECOLS]
                       .rearrange("p (w c) -> p w c", w=w), ACT.Copy).then_inc(self.kept, 1)

    def rows(self, dve, b, k, n, q):
        rows = self.shape(n)[1]
        at = b * self.quads + q + 1
        j0, w = self.quads_of(n)[q]
        cut = slice(j0, j0 + w)
        dve.wait_ge(self.selected, at + self.spare_banks)
        dve.wait_ge(self.dst_ready, b + 1)
        if q == 0:
            dve.wait_ge(self.sums_free, b + 1)
        dve.scalar_tensor_tensor(out=self.row_b[k][0:rows, cut], in0=self.later[k][0:rows, cut], scalar=1.0,
                                 in1=self.row_a[k][0:rows, cut], op0=ALU.is_equal,
                                 op1=ALU.mult).then_inc(self.row_step, 1)
        dve.wait_ge(self.row_step, at)
        dve.tensor_scalar(self.row[k][0:rows, cut], self.row_b[k][0:rows, cut], self.c.spare[0:rows, :],
                          float(MID), ALU.add, ALU.add).then_inc(self.rows_ready, 1)

    def begin_pool(self, pool):
        pool.sem_inc(self.sums_free, self.unroll - 1)

    def scatter(self, pool, b, k, n):
        m, rows = self.shape(n)
        each = self.tiles // TABLES
        for j in range(m):
            t = j % TABLES
            if j % 4 == 0:
                at = b * self.quads + j // 4 + 1
                pool.wait_ge(self.rows_ready, at)
                pool.wait_ge(self.kept, at + self.spare_banks)
            pool.wait_ge(self.c.scattered[t], (b * each + (j // TABLES + self.scattered[t])) * 16)
            pool.sem_inc(self.c.passed, 1)
            pool.indirect_dma_start(
                self.c.table[t], bass.IndirectOffsetOnAxis(ap=self.row[k][0:rows, j:j + 1], axis=0),
                self.sums[k][0:rows, j, :], None, compute_op=ALU.add).then_inc(self.c.scattered[t], 16)
            if j == TABLES - 1:
                pool.sem_inc(self.sums_free, 1)

    def finish_pool(self, pool):
        for t, count in self.total().items():
            pool.wait_ge(self.c.scattered[t], 16 * count)

    def total(self):
        return {t: self.scattered[t] + FULL * (self.tiles // TABLES)
                + len([j for j in range(self.tail_tiles) if j % TABLES == t]) for t in range(TABLES)}


class Weights:

    def __init__(self, ctx, nc, name, items):
        self.items = items
        self.loaded = [ctx.enter_context(nc.semaphore(f"{name}_loaded{i}")) for i in range(len(items))]
        self.hi_ready = ctx.enter_context(nc.semaphore(f"{name}_hi_ready"))
        self.lo_ready = ctx.enter_context(nc.semaphore(f"{name}_lo_ready"))

    def load(self, sp):
        for (src, raw, hi, lo), loaded in zip(self.items, self.loaded):
            sp.dma_start(raw, src).then_inc(loaded, 16)

    def split_hi(self, act):
        for (src, raw, hi, lo), loaded in zip(self.items, self.loaded):
            act.wait_ge(loaded, 16)
            act.activation(hi, raw, ACT.Copy).then_inc(self.hi_ready, 1)

    def split_lo(self, dve):
        for i, (src, raw, hi, lo) in enumerate(self.items):
            dve.wait_ge(self.hi_ready, i + 1)
            dve.tensor_tensor(lo, raw, hi.bitcast(F32), ALU.subtract).then_inc(self.lo_ready, 1)

    def wait(self, pe):
        pe.wait_ge(self.lo_ready, len(self.items))


def products(pe, out, left, right, first=True, last=True):
    n = 3 * len(left)
    i = 0
    for (lh, ll), (rh, rl) in zip(left, right):
        for a, c in ((lh, rh), (ll, rh), (lh, rl)):
            mm = pe.matmul(out, a, c, start=first and i == 0, stop=last and i == n - 1)
            i += 1
    return mm


class Norm:

    def __init__(self, ctx, nc, c, name, banks, copies, bank_free=None, xn_used=None):
        def sb(what, shape, dt=F32):
            return ctx.enter_context(nc.sbuf_tensor(f"{name}_{what}", shape, dt))

        self.sems = []

        def sem(what):
            self.sems.append(ctx.enter_context(nc.semaphore(f"{name}_{what}")))
            return self.sems[-1]

        self.c, self.banks = c, banks
        self.x = [sb(f"x{k}", [P, CH, DIM]) for k in range(2)]
        self.xn = [sb(f"xn{k}", [P, DIM]) for k in range(2)]
        self.hi = [sb(f"xT_hi{k}", [P, CH, BT], F32R) for k in range(copies)]
        self.lo = [sb(f"xT_lo{k}", [P, CH, BT], F32R) for k in range(copies)]
        self.raw = sb("raw", [P, CH, 6])
        self.mv = sb("mv", [P, CH, 2])
        self.std = sb("std", [P, CH])
        self.rstd = sb("rstd", [P, CH])
        self.x_in = [sem(f"x_in{k}") for k in range(2)]
        self.raw_ready = sem("raw_ready")
        self.mv_ready = sem("mv_ready")
        self.std_ready = sem("std_ready")
        self.rstd_ready = sem("rstd_ready")
        self.xn_ready = sem("xn_ready")
        self.turned = sem("turned")
        self.hi_ready = sem("hi_ready")
        self.split = bank_free or [sem("split")]
        self.xn_used = xn_used

    def load(self, sp, b, k, n):
        if n == BT:
            sp.dma_start(self.x[k][:, :, :], self.c.x[bass.ds(b * BT, n), :].rearrange("(s p) d -> p s d", p=P)
                         ).then_inc(self.x_in[k], 16)
        else:
            sp.dma_start(self.x[k][0:n, 0, :], self.c.x[bass.ds(b * BT, n), :]).then_inc(self.x_in[k], 16)

    def stats(self, dve, b, k, n, s):
        if s == 0:
            dve.wait_ge(self.x_in[k], landed(b, k, 2))
        r = subtiles(n)[s]
        dve.bn_stats(self.raw[0:r, s, :], self.x[k][0:r, s, :]).then_inc(self.raw_ready, 1)

    def aggregate(self, dve, b, k, n):
        dve.wait_ge(self.raw_ready, b * CH + len(subtiles(n)))
        dve.sem_inc(self.c.passed, 1)
        for s, r in enumerate(subtiles(n)):
            op = dve.bn_aggr(self.mv[0:r, s, :], self.raw[0:r, s, :])
        op.then_inc(self.mv_ready, 1)

    def deviation(self, act, b, n):
        r, ns = subtiles(n)[-1], len(subtiles(n))
        act.wait_ge(self.mv_ready, b + 1)
        act.activation(self.std[0:r, 0:ns], self.mv[0:r, 0:ns, 1], ACT.Sqrt,
                       bias=self.c.eps[0:r, :]).then_inc(self.std_ready, 1)

    def invert(self, dve, b, n):
        r, ns = subtiles(n)[-1], len(subtiles(n))
        dve.wait_ge(self.std_ready, b + 1)
        dve.reciprocal(self.rstd[0:r, 0:ns], self.std[0:r, 0:ns]).then_inc(self.rstd_ready, 1)

    def normalise(self, dve, b, k, n, s):
        r = subtiles(n)[s]
        if s == 0:
            dve.wait_ge(self.rstd_ready, b + 1)
        if not isinstance(b, int) or b * CH + s >= 2:
            dve.wait_ge(self.turned, b * CH + (s - 1))
            if self.xn_used is not None:
                dve.wait_ge(self.xn_used, b * CH + (s - 1))
        dve.tensor_scalar(self.xn[s % 2][0:r, :], self.x[k][0:r, s, :], self.mv[0:r, s, 0:1],
                          self.rstd[0:r, s:s + 1], ALU.subtract, ALU.mult).then_inc(self.xn_ready, 1)

    def turn(self, pe, b, n, s, bank_uses):
        r = subtiles(n)[s]
        bank = self.banks[s % len(self.banks)]
        pe.wait_ge(self.xn_ready, b * CH + (s + 1))
        if bank_uses is not None:
            pe.wait_ge(self.split[s % len(self.split)], bank_uses)
        for ch in range(CH):
            mm = pe.transpose(bank[:, ch * P:ch * P + r], self.xn[s % 2][0:r, ch * P:(ch + 1) * P],
                              self.c.ident[0:r, 0:r])
        mm.then_inc(self.turned, 1)

    def views(self, k, n, s):
        r = subtiles(n)[s]
        bank = self.banks[s % len(self.banks)][:, :].rearrange("p (c t) -> p c t", c=CH)[:, :, 0:r]
        return bank, self.hi[k][:, :, s * P:s * P + r], self.lo[k][:, :, s * P:s * P + r]

    def split_hi(self, act, b, k, n, s):
        act.wait_ge(self.turned, b * CH + (s + 1))
        bank, hi, lo = self.views(k, n, s)
        act.activation(hi, bank, ACT.Copy).then_inc(self.hi_ready, 1)

    def split_lo(self, dve, b, k, n, s):
        dve.wait_ge(self.hi_ready, b * CH + (s + 1))
        bank, hi, lo = self.views(k, n, s)
        dve.tensor_tensor(lo, bank, hi.bitcast(F32), ALU.subtract
                          ).then_inc(self.split[s % len(self.split)], 1)

    def pairs(self, k, cut):
        return [(self.hi[k][:, c, cut], self.lo[k][:, c, cut]) for c in range(CH)]

    def first_on_dve(self, dve):
        for s in range(CH):
            self.stats(dve, 0, 0, BT, s)
        self.aggregate(dve, 0, 0, BT)
        self.invert(dve, 0, BT)
        for s in range(CH):
            self.normalise(dve, 0, 0, BT, s)
            if s >= 1:
                self.split_lo(dve, 0, 0, BT, s - 1)
        self.split_lo(dve, 0, 0, BT, CH - 1)


class Shared:
    pass


def constants_stage(nc, c):
    with ExitStack() as ctx:
        sel_f = ctx.enter_context(nc.sbuf_tensor("sel_f", [2 * HEADS, QK * P], F32))
        spare_i = ctx.enter_context(nc.sbuf_tensor("spare_i", [P, 1], I32))
        feat_i = ctx.enter_context(nc.sbuf_tensor("feat_i", [P, CH], I32))
        expert_i = ctx.enter_context(nc.sbuf_tensor("expert_i", [1, EXPERTS], I32))
        filled, shaped, converted, biases_in = c.finished = [
            ctx.enter_context(nc.semaphore(name)) for name in ("filled", "shaped", "converted", "biases_in")]
        block = ctx.enter_context(nc.Block())

        @block.sync
        def _(sp):
            sp.dma_start(c.bias_v[:, :], c.b_v.partition_broadcast(P)).then_inc(biases_in, 16)
            sp.dma_start(c.bias_qk[:, :], c.b_qk).then_inc(biases_in, 16)
            sp.wait_ge(biases_in, 32)

        @block.gpsimd
        def _(pool):
            pool.memset(c.ident[:, :], 0.0)
            pool.memset(sel_f[:, :], 0.0)
            pool.memset(c.row_sel[:, :], 0.0)
            pool.memset(c.upper[:, :], 1.0)
            pool.memset(c.same_token[:, :], 1.0).then_inc(filled, 1)
            pool.wait_ge(filled, 1)
            pool.affine_select(out=c.ident[:, :], in_=c.ident[:, :], compare_op=ALU.not_equal, fill=1.0, base=0,
                               pattern=[[-1, P]], channel_multiplier=1)
            pool.affine_select(out=sel_f[:, :], in_=sel_f[:, :], compare_op=ALU.not_equal, fill=1.0, base=0,
                               pattern=[[-HEADS, 2], [-2, CH], [-1, 2], [0, HDIM]], channel_multiplier=1)
            pool.affine_select(out=c.row_sel[:, :], in_=c.row_sel[:, :], compare_op=ALU.not_equal, fill=1.0,
                               base=0, pattern=[[0, GT], [-1, HEADS]], channel_multiplier=1)
            pool.affine_select(out=c.upper[:, :], in_=c.upper[:, :], compare_op=ALU.is_ge, fill=0.0, base=0,
                               pattern=[[1, P]], channel_multiplier=-1)
            pool.affine_select(out=c.same_token[:, :], in_=c.same_token[:, :], compare_op=ALU.is_ge, fill=0.0,
                               base=0, pattern=[[-HEADS, GT], [0, HEADS]], channel_multiplier=1).then_inc(filled, 1)
            pool.wait_ge(filled, 2)
            pool.affine_select(out=c.same_token[:, :], in_=c.same_token[:, :], compare_op=ALU.is_ge, fill=0.0,
                               base=HEADS - 1, pattern=[[HEADS, GT], [0, HEADS]], channel_multiplier=-1)
            pool.iota(spare_i[:, :], [[0, 1]], base=TOKENS - MID, channel_multiplier=1)
            pool.iota(feat_i[:, :], [[P, CH]], base=0, channel_multiplier=1)
            pool.iota(expert_i[:, :], [[1, EXPERTS]], base=0, channel_multiplier=0).then_inc(shaped, 1)

        @block.vector
        def _(dve):
            dve.memset(c.zero[:, :], 0.0)
            dve.memset(c.eps[:, :], EPS)
            dve.memset(c.ones_row[:, :], 1.0)
            dve.wait_ge(shaped, 1)
            dve.tensor_copy(c.ident_r[:, :], c.ident[:, :])
            dve.tensor_copy(c.sel[:, :], sel_f[:, :])
            dve.tensor_copy(c.spare[:, :], spare_i[:, :])
            dve.tensor_copy(c.feat[:, :], feat_i[:, :])
            dve.tensor_copy(c.expert_no[:, :], expert_i[:, :]).then_inc(converted, 1)
            dve.wait_ge(converted, 1)


def project_stage(nc, c):
    with ExitStack() as ctx:
        def sb(what, shape, dt=F32):
            return ctx.enter_context(nc.sbuf_tensor(f"pr_{what}", shape, dt))

        def bank(what):
            return ctx.enter_context(nc.psum_tensor(f"pr_{what}", [P, BT], F32))

        def sem(what):
            return ctx.enter_context(nc.semaphore(f"pr_{what}"))

        W3 = 3 * DIM
        w_hi = sb("w_hi", [P, CH, W3], F32R)
        w_lo = sb("w_lo", [P, CH, W3], F32R)
        qk = [sb(f"qk{k}", [P, QK, BT]) for k in range(2)]
        v = sb("v", [P, CH, DIM])
        part = [sb(f"part{k}", [P, QK]) for k in range(2)]
        turn_banks = [bank(f"turn{k}") for k in range(2)]
        v_bank = [bank(f"v_bank{k}") for k in range(2)]
        qk_bank = [bank(f"qk_bank{k}") for k in range(2)]
        raw = [qk[i // 2][:, :, :].rearrange("p o t -> p (o t)")[:, i % 2 * W3:(i % 2 + 1) * W3] for i in range(CH)]
        weights = Weights(ctx, nc, "pr_w", [(c.w_qkv[i * P:(i + 1) * P, :], raw[i], w_hi[:, i, :], w_lo[:, i, :])
                                            for i in range(CH)])
        norm = Norm(ctx, nc, c, "pr_norm", turn_banks, 2)
        edges = Edges(ctx, nc, c, "pr_edge", 0, 40, 12, P, 2, {t: 0 for t in range(TABLES)},
                      ([bank("dst")], [bank("sum")]), pieces=4)
        v_mm, v_bank_free = sem("v_mm"), sem("v_bank_free")
        qk_mm, qk_bank_free = sem("qk_mm"), sem("qk_bank_free")
        v_stored, v_free = sem("v_stored"), sem("v_free")
        qk_stored, qk_free = sem("qk_stored"), sem("qk_free")
        added, tables_zero = sem("added"), sem("tables_zero")
        c.finished += norm.sems + edges.sems + [tables_zero, v_mm, v_bank_free, qk_mm, qk_bank_free, v_stored, v_free, qk_stored, qk_free, added]
        block = ctx.enter_context(nc.Block())

        def groups(n):
            return [("v", s) for s in range(len(subtiles(n)))] + [("qk", o) for o in range(QK)]

        def slots(n):
            return range(max(len(groups(n)), len(edges.quads_of(n))))

        @block.sync
        def _(sp):
            norm.load(sp, 0, 0, BT)
            weights.load(sp)
            sp.sem_inc(v_free, 1)
            sp.sem_inc(qk_free, 1)
            edges.load_first(sp)
            norm.load(sp, 1, 1, BT)
            for t in range(TABLES):
                sp.dma_start(c.table[t].rearrange("(p b a) c -> p b (a c)", p=P, b=5),
                             c.zero[:, :].unsqueeze(1).to_broadcast([P, 5, TROWS // P * ECOLS // 5])
                             ).then_inc(tables_zero, 16)

            def body(b, k, n, after):
                edges.load_next(sp, b, k, after)
                sp.wait_ge(qk_stored, b * 64)
                sp.sem_inc(qk_free, 1)
                if later_size(b, 2):
                    sp.wait_ge(norm.xn_ready, (b + 1) * CH)
                    norm.load(sp, b + 2, k, later_size(b, 2))
                sp.wait_ge(v_bank_free, b * CH + (2 + len(subtiles(n))))
                if n == BT:
                    sp.dma_start(c.v[cols(b, n), :].rearrange("(s p) d -> p s d", p=P), v[:, :, :]
                                 ).then_inc(v_stored, 16)
                else:
                    sp.dma_start(c.v[cols(b, n), :], v[0:n, 0, :]).then_inc(v_stored, 16)
                sp.wait_ge(v_stored, b * 16 + 16)
                sp.sem_inc(v_free, 1)
                for i in range(4):
                    if i < 3:
                        edges.load_more(sp, b, k, after, i + 1)
                    sp.wait_ge(qk_bank_free, b * QK + (2 + 2 * i + 2))
                    sp.sem_inc(c.passed, 1)
                    sp.dma_start(c.qk[2 * i * P:(2 * i + 2) * P, cols(b, n)].rearrange("(o p) t -> p o t", p=P),
                                 qk[k][:, 2 * i:2 * i + 2, 0:n]).then_inc(qk_stored, 16)

            over_blocks(sp, 2, body)
            sp.wait_ge(qk_stored, NB * 64)

        @block.tensor
        def _(pe):
            for s in range(CH):
                norm.turn(pe, 0, BT, s, s - 1 if s >= 2 else None)
            weights.wait(pe)

            def body(b, k, n, after):
                pe.wait_ge(norm.split[0], b * CH + len(subtiles(n)))
                todo = groups(n)
                quads = edges.quads_of(n)
                for g in slots(n):
                    if g < len(quads):
                        edges.spread_dst(pe, b, k, n, g)
                    if g < len(todo):
                        kind, i = todo[g]
                        if kind == "v":
                            r = subtiles(n)[i]
                            pe.wait_ge(v_bank_free, b * CH + i + 1)
                            products(pe, v_bank[i % 2][0:r, :], norm.pairs(k, slice(i * P, i * P + r)),
                                     [(w_hi[:, ch, 2 * DIM:W3], w_lo[:, ch, 2 * DIM:W3]) for ch in range(CH)]
                                     ).then_inc(v_mm, 1)
                        else:
                            pe.wait_ge(qk_bank_free, b * QK + i + 1)
                            cut = slice(i * P, (i + 1) * P)
                            products(pe, qk_bank[i % 2][:, 0:n],
                                     [(w_hi[:, ch, cut], w_lo[:, ch, cut]) for ch in range(CH)],
                                     norm.pairs(k, slice(0, n))).then_inc(qk_mm, 1)
                    if g < len(quads):
                        edges.sum_tile(pe, b, k, n, g)
                    if after and 7 <= g < 7 + len(subtiles(after)):
                        norm.turn(pe, b + 1, after, g - 7, b * CH + (CH + g - 7 - 1))

            over_blocks(pe, 2, body)

        @block.scalar
        def _(act):
            norm.deviation(act, 0, BT)
            for s in range(CH):
                norm.split_hi(act, 0, 0, BT, s)
            weights.split_hi(act)
            edges.begin_act(act)
            act.sem_inc(qk_bank_free, 2)

            def body(b, k, n, after):
                todo = groups(n)
                for g in slots(n):
                    if g < len(todo) and todo[g][0] == "qk":
                        o = todo[g][1]
                        act.wait_ge(qk_mm, b * QK + o + 1)
                        if o == 0:
                            act.wait_ge(qk_free, b + 1)
                            act.wait_ge(added, b)
                        act.activation(qk[k][:, o, 0:n], qk_bank[o % 2][:, 0:n], ACT.Sigmoid,
                                       bias=c.bias_qk[:, o:o + 1], accum_out=part[k][:, o:o + 1]
                                       ).then_inc(qk_bank_free, 1)
                    if g < len(edges.quads_of(n)):
                        edges.keep(act, b, k, n, g)
                    if after and g == 4:
                        norm.deviation(act, b + 1, after)
                    if after and 7 <= g < 7 + len(subtiles(after)):
                        if g == 7:
                            act.wait_ge(qk_mm, b * QK)
                        norm.split_hi(act, b + 1, 1 - k, after, g - 7)

            over_blocks(act, 2, body)

        @block.vector
        def _(dve):
            edges.begin_dve(dve)
            norm.first_on_dve(dve)
            dve.sem_inc(v_bank_free, 2)
            dve.memset(c.sums[:, :], 0.0).then_inc(added, 1)
            weights.split_lo(dve)

            edges.prepare(dve, 0, 0, BT)

            def body(b, k, n, after):
                todo = groups(n)
                for g in slots(n):
                    if g < len(edges.quads_of(n)):
                        edges.select(dve, b, k, n, g)
                    if g < len(todo) and todo[g][0] == "v":
                        s = todo[g][1]
                        r = subtiles(n)[s]
                        if s == 0:
                            dve.wait_ge(v_free, b + 1)
                        dve.wait_ge(v_mm, b * CH + s + 1)
                        dve.tensor_tensor(v[0:r, s, :], v_bank[s % 2][0:r, :], c.bias_v[0:r, :],
                                          ALU.add).then_inc(v_bank_free, 1)
                    if after and g < len(subtiles(after)):
                        norm.stats(dve, b + 1, 1 - k, after, g)
                    if after and g == 4:
                        norm.aggregate(dve, b + 1, 1 - k, after)
                    if after and g == 5:
                        norm.invert(dve, b + 1, after)
                    if after and g == len(todo) - 1:
                        edges.prepare(dve, b + 1, 1 - k, after)
                    if after and 6 <= g < 6 + len(subtiles(after)):
                        norm.normalise(dve, b + 1, 1 - k, after, g - 6)
                    if after and 7 <= g < 7 + len(subtiles(after)):
                        norm.split_lo(dve, b + 1, 1 - k, after, g - 7)
                    if g < len(edges.quads_of(n)):
                        edges.rows(dve, b, k, n, g)
                dve.wait_ge(qk_bank_free, b * QK + (2 + QK))
                dve.wait_ge(added, b + 1)
                dve.tensor_tensor(c.sums[:, :], c.sums[:, :], part[k][:, :], ALU.add).then_inc(added, 1)

            over_blocks(dve, 2, body)

        @block.gpsimd
        def _(pool):
            edges.begin_pool(pool)
            pool.wait_ge(tables_zero, 16 * TABLES)
            over_blocks(pool, 2, lambda b, k, n, after: edges.scatter(pool, b, k, n))
            edges.finish_pool(pool)

    return edges


def head_matrix(dve, c, src, built):
    dve.memset(c.heads[:, :, :], 0.0).then_inc(built, 1)
    dve.wait_ge(built, 1)
    flat = c.heads[:, :, :].rearrange("p o r -> p (o r)")
    step = 2 * HEADS + 2
    for parity in range(2):
        rows = slice(parity * HDIM, (parity + 1) * HDIM)
        for side, at in ((0, 0), (1, CH * 2 * HEADS + HEADS)):
            a = at + parity
            op = dve.tensor_copy(flat[rows, a:a + (CH - 1) * step + 1:step],
                                 src[rows, (1 - side) * CH:(2 - side) * CH])
    op.then_inc(built, 1)
    return 2


def norms_stage(nc, c, before):
    with ExitStack() as ctx:
        def sb(what, shape, dt=F32):
            return ctx.enter_context(nc.sbuf_tensor(f"nm_{what}", shape, dt))

        def bank(what):
            return ctx.enter_context(nc.psum_tensor(f"nm_{what}", [P, BT], F32))

        def sem(what):
            return ctx.enter_context(nc.semaphore(f"nm_{what}"))

        U = 4
        R = 2 * HEADS
        qk = [sb(f"qk{k}", [P, QK, BT]) for k in range(U)]
        r_hi = [sb(f"r_hi{k}", [R, BT], F32R) for k in range(U)]
        r_lo = [sb(f"r_lo{k}", [R, BT], F32R) for k in range(U)]
        part = [sb(f"part{k}", [P, QK]) for k in range(U)]
        io_bank = [bank(f"io{k}") for k in range(2)]
        wide = [bank(f"wide{k}") for k in range(2)]
        edges = Edges(ctx, nc, c, "nm_edge", before.last_edge, 16, 2, P, U, before.total(),
                      ([bank(f"dst{k}") for k in range(2)], [bank(f"sum{k}") for k in range(2)]))
        built, qk_in = sem("built"), [sem(f"qk_in{k}") for k in range(U)]
        io_mm, r_step, r_ready = sem("io_mm"), sem("r_step"), sem("r_ready")
        wide_mm, wide_free, added = sem("wide_mm"), sem("wide_free"), sem("added")
        block = ctx.enter_context(nc.Block())

        @block.sync
        def _(sp):
            def load(b, k, n, half):
                sp.dma_start(qk[k][:, half * CH:(half + 1) * CH, 0:n],
                             c.qk[half * DIM:(half + 1) * DIM, cols(b, n)].rearrange("(o p) t -> p o t", p=P)
                             ).then_inc(qk_in[k], 16)

            for b in range(3):
                for half in range(2):
                    load(b, b, BT, half)
                if b == 0:
                    edges.load_first(sp)

            def body(b, k, n, after):
                edges.load_next(sp, b, k, after)
                for half in range(2):
                    if later_size(b, 3):
                        sp.wait_ge(wide_free, b * QK + (2 + half * CH))
                        sp.sem_inc(c.passed, 1)
                        load(b + 3, (k + 3) % U, later_size(b, 3), half)

            over_blocks(sp, U, body)

        @block.tensor
        def _(pe):
            def io(b, k, n, o):
                if o == 0:
                    pe.wait_ge(qk_in[k], landed(b, k, U, 2))
                mm = pe.matmul(io_bank[k % 2][0:R, 0:n], c.heads[:, o, :], qk[k][:, o, 0:n],
                               start=o == 0, stop=o == QK - 1)
                if o == QK - 1:
                    mm.then_inc(io_mm, 1)

            pe.wait_ge(built, 2)
            for b in range(2):
                for o in range(QK):
                    io(b, b, BT, o)

            def widen(b, k, n, o):
                if o == 0:
                    pe.wait_ge(r_ready, b + 1)
                pe.wait_ge(wide_free, b * QK + o + 1)
                for i, r in enumerate((r_hi[k], r_lo[k])):
                    mm = pe.matmul(wide[o % 2][:, 0:n], c.sel[:, o * P:(o + 1) * P], r[:, 0:n],
                                   start=i == 0, stop=i == 1)
                mm.then_inc(wide_mm, 1)

            def body(b, k, n, after):
                ahead = later_size(b, 2)
                quads = len(edges.quads_of(n))
                for half in range(2):
                    for q in (2 * half, 2 * half + 1):
                        if q < quads:
                            edges.spread_dst(pe, b, k, n, q)
                    for o in range(half * CH, (half + 1) * CH):
                        widen(b, k, n, o)
                        if ahead:
                            if o == 0:
                                pe.wait_ge(r_step, b * 3 + 2)
                            io(b + 2, (k + 2) % U, ahead, o)
                    for q in (2 * half, 2 * half + 1):
                        if q < quads:
                            edges.sum_tile(pe, b, k, n, q)

            over_blocks(pe, U, body)

        @block.scalar
        def _(act):
            edges.begin_act(act)

            def body(b, k, n, after):
                for q in range(len(edges.quads_of(n))):
                    edges.keep(act, b, k, n, q)

            over_blocks(act, U, body)

        @block.vector
        def _(dve):
            edges.begin_dve(dve)
            head_matrix(dve, c, c.sums, built)
            dve.memset(c.shares[:, :], 0.0).then_inc(added, 1)
            dve.sem_inc(wide_free, 2)

            def invert(b, k, n, half):
                w = (n + 1) // 2
                a, z = half * w, min(n, (half + 1) * w)
                dve.wait_ge(io_mm, b + 1)
                dve.reciprocal(c.inverse[:, bass.ds(b * BT + a, z - a)], io_bank[k % 2][0:R, a:z]).then_inc(r_step, 1)

            def split(b, k, n):
                dve.wait_ge(r_step, b * 3 + 2)
                dve.sem_inc(c.passed, 1)
                dve.tensor_copy(r_hi[k][:, 0:n], c.inverse[:, cols(b, n)]).then_inc(r_step, 1)
                dve.wait_ge(r_step, b * 3 + 3)
                dve.tensor_tensor(r_lo[k][:, 0:n], c.inverse[:, cols(b, n)], r_hi[k][:, 0:n].bitcast(F32),
                                  ALU.subtract).then_inc(r_ready, 1)

            for half in range(2):
                invert(0, 0, BT, half)
            split(0, 0, BT)
            edges.prepare(dve, 0, 0, BT)

            def body(b, k, n, after):
                quads = len(edges.quads_of(n))
                for o in range(QK):
                    if o % CH < 2 and 2 * (o // CH) + o % CH < quads:
                        edges.select(dve, b, k, n, 2 * (o // CH) + o % CH)
                    dve.wait_ge(wide_mm, b * QK + o + 1)
                    dve.tensor_tensor_reduce(wide[o % 2][:, 0:n], qk[k][:, o, 0:n], wide[o % 2][:, 0:n], 1.0, 0.0,
                                             ALU.mult, ALU.add, part[k][:, o:o + 1]).then_inc(wide_free, 1)
                    if o in (1, 2, 5, 6):
                        q = 2 * (o // CH) + (o - 1) % CH
                        if q < quads:
                            edges.rows(dve, b, k, n, q)
                    if after and o % CH == 1:
                        invert(b + 1, (k + 1) % U, after, o // CH)
                    if after and o == 2:
                        edges.prepare(dve, b + 1, (k + 1) % U, after)
                    if after and o == 6:
                        split(b + 1, (k + 1) % U, after)
                dve.wait_ge(wide_free, b * QK + (2 + QK))
                dve.wait_ge(added, b + 1)
                dve.tensor_tensor(c.shares[:, :], c.shares[:, :], part[k][:, :], ALU.add).then_inc(added, 1)

            over_blocks(dve, U, body)

        @block.gpsimd
        def _(pool):
            edges.begin_pool(pool)
            over_blocks(pool, U, lambda b, k, n, after: edges.scatter(pool, b, k, n))
            edges.finish_pool(pool)

    return edges


def scale_stage(nc, c, before):
    with ExitStack() as ctx:
        def sb(what, shape, dt=F32):
            return ctx.enter_context(nc.sbuf_tensor(f"sc_{what}", shape, dt))

        def bank(what):
            return ctx.enter_context(nc.psum_tensor(f"sc_{what}", [P, BT], F32))

        def sem(what):
            return ctx.enter_context(nc.semaphore(f"sc_{what}"))

        U = 4
        H = HEADS
        qk = [sb(f"qk{k}", [P, QK, BT]) for k in range(U)]
        gate = [sb(f"gate{k}", [H, BT]) for k in range(U)]
        ce = [sb(f"ce{k}", [H, 2, BT]) for k in range(U)]
        ce_hi = [sb(f"ce_hi{k}", [H, 2, BT], F32R) for k in range(U)]
        ce_lo = [sb(f"ce_lo{k}", [H, 2, BT], F32R) for k in range(U)]
        neg_max = [sb(f"neg_max{k}", [H, 1]) for k in range(U)]
        exp_sum = [sb(f"exp_sum{k}", [H, 1]) for k in range(U)]
        neg_maxs = sb("neg_maxs", [H, NB])
        exp_sums = sb("exp_sums", [H, NB])
        top = sb("top", [H, 1])
        rescale = sb("rescale", [H, NB])
        weighted = sb("weighted", [H, NB])
        total = sb("total", [H, 1])
        total_inv = sb("total_inv", [H, 1])
        factor = sb("factor", [H, NB])
        i_bank, o_bank = bank("i_bank"), bank("o_bank")
        wide = [bank(f"wide{k}") for k in range(2)]
        edges = Edges(ctx, nc, c, "sc_edge", before.last_edge, 12, 1, EDGES % P, U, before.total(),
                      ([bank(f"dst{k}") for k in range(2)], [bank(f"sum{k}") for k in range(2)]))
        assert edges.last_edge == EDGES
        built, qk_stored = sem("built"), sem("qk_stored")
        qk_in = [sem(f"qk_in{k}") for k in range(U)]
        io_mm, gated, max_ready, exp_ready = sem("io_mm"), sem("gated"), sem("max_ready"), sem("exp_ready")
        c_ready, hi_ready, ce_ready, noted = sem("c_ready"), sem("hi_ready"), sem("ce_ready"), sem("noted")
        wide_mm, wide_free = sem("wide_mm"), sem("wide_free")
        end_step, end_exp, end_mm = sem("end_step"), sem("end_exp"), sem("end_mm")
        block = ctx.enter_context(nc.Block())

        @block.sync
        def _(sp):
            def load(b, k, n, half):
                sp.dma_start(qk[k][:, half * CH:(half + 1) * CH, 0:n],
                             c.qk[half * DIM:(half + 1) * DIM, cols(b, n)].rearrange("(o p) t -> p o t", p=P)
                             ).then_inc(qk_in[k], 16)

            for b in range(3):
                for half in range(2):
                    load(b, b, BT, half)
                if b == 0:
                    edges.load_first(sp)

            def body(b, k, n, after):
                edges.load_next(sp, b, k, after)
                sp.wait_ge(qk_stored, b * 32)
                for half in range(2):
                    if later_size(b, 3):
                        load(b + 3, (k + 3) % U, later_size(b, 3), half)
                    sp.wait_ge(wide_free, b * QK + (2 + (half + 1) * CH))
                    sp.sem_inc(c.passed, 1)
                    sp.dma_start(c.qk_scaled[half * DIM:(half + 1) * DIM, cols(b, n)]
                                 .rearrange("(o p) t -> p o t", p=P), qk[k][:, half * CH:(half + 1) * CH, 0:n]
                                 ).then_inc(qk_stored, 16)

            over_blocks(sp, U, body)
            sp.wait_ge(qk_stored, NB * 32)

        @block.tensor
        def _(pe):
            def io(b, k, n, o):
                if o == 0:
                    pe.wait_ge(qk_in[k], landed(b, k, U, 2))
                out, row = (i_bank, 0) if o < CH else (o_bank, H)
                mm = pe.matmul(out[0:H, 0:n], c.heads[:, o, row:row + H], qk[k][:, o, 0:n],
                               start=o % CH == 0, stop=o % CH == CH - 1)
                if o % CH == CH - 1:
                    mm.then_inc(io_mm, 1)

            pe.wait_ge(built, 2)
            def banks_free(b, o):
                if o == 0:
                    pe.wait_ge(gated, b)
                if o == CH:
                    pe.wait_ge(exp_ready, b)
                    pe.wait_ge(max_ready, b)

            for b in range(2):
                for o in range(QK):
                    if b:
                        banks_free(b, o)
                    io(b, b, BT, o)

            def widen(b, k, n, o):
                if o == 0:
                    pe.wait_ge(ce_ready, b + 1)
                pe.wait_ge(wide_free, b * QK + o + 1)
                for i, r in enumerate((ce_hi[k], ce_lo[k])):
                    mm = pe.matmul(wide[o % 2][:, 0:n], c.sel[0:H, (o % CH) * P:(o % CH + 1) * P],
                                   r[:, o // CH, 0:n], start=i == 0, stop=i == 1)
                mm.then_inc(wide_mm, 1)

            def body(b, k, n, after):
                ahead = later_size(b, 2)
                quads = len(edges.quads_of(n))
                for half in range(2):
                    for q in (2 * half, 2 * half + 1):
                        if q < quads:
                            edges.spread_dst(pe, b, k, n, q)
                    for o in range(half * CH, (half + 1) * CH):
                        widen(b, k, n, o)
                        if ahead:
                            banks_free(b + 2, o)
                            io(b + 2, (k + 2) % U, ahead, o)
                    for q in (2 * half, 2 * half + 1):
                        if q < quads:
                            edges.sum_tile(pe, b, k, n, q)

            over_blocks(pe, U, body)
            pe.wait_ge(end_step, 7)
            pe.matmul(i_bank[:, 0:NB], c.row_sel[:, :], factor[:, :], start=True, stop=True).then_inc(end_mm, 1)

        @block.scalar
        def _(act):
            def gates(b, k, n):
                act.wait_ge(io_mm, b * 2 + 1)
                act.activation(gate[k][:, 0:n], i_bank[0:H, 0:n], ACT.Sigmoid).then_inc(gated, 1)

            def exponentials(b, k, n):
                act.wait_ge(max_ready, b + 1)
                act.activation(ce[k][:, 1, 0:n], o_bank[0:H, 0:n], ACT.Exp, bias=neg_max[k][:, :],
                               accum_out=exp_sum[k][:, :]).then_inc(exp_ready, 1)

            edges.begin_act(act)
            gates(0, 0, BT)
            exponentials(0, 0, BT)
            gates(1, 1, BT)

            def body(b, k, n, after):
                quads = len(edges.quads_of(n))
                if after:
                    exponentials(b + 1, (k + 1) % U, after)
                for q in range(quads):
                    edges.keep(act, b, k, n, q)
                    if q == 1 and later_size(b, 2):
                        gates(b + 2, (k + 2) % U, later_size(b, 2))

            over_blocks(act, U, body)
            act.wait_ge(end_step, 2)
            act.activation(rescale[:, :], neg_maxs[:, :], ACT.Exp, bias=top[:, :], scale=-1.0).then_inc(end_exp, 1)

        @block.vector
        def _(dve):
            edges.begin_dve(dve)
            head_matrix(dve, c, c.shares, built)
            dve.sem_inc(wide_free, 2)

            def maximum(b, k, n):
                dve.wait_ge(io_mm, b * 2 + 2)
                dve.tensor_reduce(neg_max[k][:, :], o_bank[0:H, 0:n], AX.X, ALU.max, negate=True
                                  ).then_inc(max_ready, 1)

            def scale_q(b, k, n):
                dve.wait_ge(gated, b + 1)
                dve.tensor_tensor(ce[k][:, 0, 0:n], gate[k][:, 0:n], c.inverse[0:H, cols(b, n)], ALU.mult
                                  ).then_inc(c_ready, 1)

            def scales_hi(b, k, n):
                dve.wait_ge(c_ready, b + 1)
                dve.wait_ge(exp_ready, b + 1)
                dve.tensor_copy(ce_hi[k][:, :, 0:n], ce[k][:, :, 0:n]).then_inc(hi_ready, 1)

            def scales_lo(b, k, n):
                dve.wait_ge(hi_ready, b + 1)
                dve.tensor_tensor(ce_lo[k][:, :, 0:n], ce[k][:, :, 0:n], ce_hi[k][:, :, 0:n].bitcast(F32),
                                  ALU.subtract).then_inc(ce_ready, 1)
                dve.wait_ge(max_ready, b + 1)
                dve.tensor_copy(neg_maxs[:, bass.ds(b, 1)], neg_max[k][:, :])
                dve.tensor_copy(exp_sums[:, bass.ds(b, 1)], exp_sum[k][:, :]).then_inc(noted, 1)

            maximum(0, 0, BT)
            scale_q(0, 0, BT)
            scales_hi(0, 0, BT)
            scales_lo(0, 0, BT)
            edges.prepare(dve, 0, 0, BT)

            def body(b, k, n, after):
                quads = len(edges.quads_of(n))
                if after:
                    maximum(b + 1, (k + 1) % U, after)
                for o in range(QK):
                    if o % CH < 2 and 2 * (o // CH) + o % CH < quads:
                        edges.select(dve, b, k, n, 2 * (o // CH) + o % CH)
                    dve.wait_ge(wide_mm, b * QK + o + 1)
                    dve.tensor_tensor(qk[k][:, o, 0:n], qk[k][:, o, 0:n], wide[o % 2][:, 0:n], ALU.mult
                                      ).then_inc(wide_free, 1)
                    if o in (1, 2, 5, 6):
                        q = 2 * (o // CH) + (o - 1) % CH
                        if q < quads:
                            edges.rows(dve, b, k, n, q)
                    if after:
                        if o == 2:
                            scale_q(b + 1, (k + 1) % U, after)
                            edges.prepare(dve, b + 1, (k + 1) % U, after)
                        if o == 4:
                            scales_hi(b + 1, (k + 1) % U, after)
                        if o == 6:
                            scales_lo(b + 1, (k + 1) % U, after)

            over_blocks(dve, U, body)
            dve.wait_ge(noted, NB)
            dve.tensor_reduce(top[:, :], neg_maxs[:, :], AX.X, ALU.min).then_inc(end_step, 2)
            dve.wait_ge(end_exp, 1)
            dve.tensor_tensor(weighted[:, :], rescale[:, :], exp_sums[:, :], ALU.mult).then_inc(end_step, 1)
            dve.wait_ge(end_step, 3)
            dve.tensor_reduce(total[:, :], weighted[:, :], AX.X, ALU.add).then_inc(end_step, 1)
            dve.wait_ge(end_step, 4)
            dve.reciprocal(total_inv[:, :], total[:, :]).then_inc(end_step, 1)
            dve.wait_ge(end_step, 5)
            dve.tensor_scalar(factor[:, :], rescale[:, :], total_inv[:, :], None, ALU.mult).then_inc(end_step, 2)
            dve.wait_ge(end_mm, 1)
            dve.tensor_copy(c.factors[:, :], i_bank[:, 0:NB]).then_inc(end_step, 1)
            dve.wait_ge(end_step, 8)

        @block.gpsimd
        def _(pool):
            for done in c.finished:
                pool.sem_clear(done)
            edges.begin_pool(pool)
            over_blocks(pool, U, lambda b, k, n, after: edges.scatter(pool, b, k, n))
            edges.finish_pool(pool)

    return edges


def mix_stage(nc, c):
    with ExitStack() as ctx:
        def sb(what, shape, dt=F32):
            return ctx.enter_context(nc.sbuf_tensor(f"mx_{what}", shape, dt))

        def bank(what):
            return ctx.enter_context(nc.psum_tensor(f"mx_{what}", [P, BT], F32))

        def sem(what):
            return ctx.enter_context(nc.semaphore(f"mx_{what}"))

        w1_hi = sb("w1_hi", [P, CH + 1, HID], F32R)
        w1_lo = sb("w1_lo", [P, CH + 1, HID], F32R)
        w2_hi = sb("w2_hi", [P, JH, DIM], F32R)
        w2_lo = sb("w2_lo", [P, JH, DIM], F32R)
        wo_hi = sb("wo_hi", [P, CH, DIM], F32R)
        wo_lo = sb("wo_lo", [P, CH, DIM], F32R)
        b1 = sb("b1", [P, JH])
        bias = sb("bias", [P, DIM])
        GROUPS = P // GT
        agg_raw = sb("agg_raw", [P, TABLES, CH, ECOLS])
        agg_sum = sb("agg_sum", [P, CH, ECOLS])
        agg_mean = sb("agg_mean", [P, CH, 2, EDIM])
        agg_cnt = sb("agg_cnt", [P, CH])
        agg_inv = sb("agg_inv", [P, CH])
        agg = sb("agg", [P, BT], F32R)
        qs = sb("qs", [P, HEADS, P])
        ks = sb("ks", [P, HEADS, P])
        kt = sb("kt", [P, P, HEADS])
        v = [sb(f"v{k}", [P, GROUPS, HDIM]) for k in range(2)]
        near = sb("near", [P, 4, P])
        factor = [sb(f"factor{k}", [P, 1]) for k in range(2)]
        with ExitStack() as first:
            raw = first.enter_context(nc.sbuf_tensor("mx_raw", [P, HID + 2 * JH * BT], F32))
        r_hi = [sb(f"r_hi{k}", [P, CH, P], F32R) for k in range(2)]
        r_lo = [sb(f"r_lo{k}", [P, CH, P], F32R) for k in range(2)]
        h_hi = sb("h_hi", [P, JH, BT], F32R)
        h_lo = sb("h_lo", [P, JH, BT], F32R)
        hid = sb("hid", [P, BT])
        x1 = [sb(f"x1_{k}", [P, DIM]) for k in range(2)]
        raw1, mv1, std1, rstd1 = sb("raw1", [P, 6]), sb("mv1", [P, 2]), sb("std1", [P, 1]), sb("rstd1", [P, 1])
        x1n = sb("x1n", [P, DIM])
        x1nT = [sb(f"x1nT{k}", [P, CH, P]) for k in range(2)]
        part = [sb(f"part{k}", [P, CH]) for k in range(2)]
        turn_bank = [bank(f"turn{k}") for k in range(2)]
        r_bank, s_bank = bank("r"), bank("s")
        h_bank = [bank(f"h{k}") for k in range(2)]
        acc = [bank(f"acc{k}") for k in range(2)]
        turn_free = [sem(f"turn_free{k}") for k in range(2)]
        with_xn, base_ready = sem("with_xn"), sem("base_ready")
        norm = Norm(ctx, nc, c, "mx_norm", turn_bank, 1, turn_free, with_xn)
        bias_in, bias_ready = sem("bias_in"), sem("bias_ready")
        w2_at = (DIM // P + 1) * HID
        weights = Weights(ctx, nc, "mx_w", [
            (c.w1[i * P:(i + 1) * P, :], raw[:, i * HID:(i + 1) * HID], w1_hi[:, i, :], w1_lo[:, i, :])
            for i in range(CH)]
            + [(c.w1[DIM:DIM + EDIM, :], raw[at:at + EDIM, CH * HID:(CH + 1) * HID],
                w1_hi[at:at + EDIM, CH, :], w1_lo[at:at + EDIM, CH, :]) for at in (0, EDIM)]
            + [(c.w2[a * P:(a + CH) * P, :].rearrange("(j p) d -> p j d", p=P),
                raw[:, w2_at + a * DIM:w2_at + (a + CH) * DIM].rearrange("p (j d) -> p j d", d=DIM),
                w2_hi[:, a:a + CH, :], w2_lo[:, a:a + CH, :]) for a in (0, CH)]
            + [(c.w_out.rearrange("(j p) d -> p j d", p=P), norm.x[1][:, :, :], wo_hi[:, :, :], wo_lo[:, :, :])])


        table_in, agg_step, agg_turned, agg_hi_ready = sem("table_in"), sem("agg_step"), sem("agg_turned"), sem("agg_hi_ready")
        qk_in, v_in = sem("qk_in"), [sem(f"v_in{k}") for k in range(2)]
        factor_ready = sem("factor_ready")
        kt_ready = sem("kt_ready")
        scored, near_ready, mixed = sem("scored"), sem("near_ready"), sem("mixed")
        r_hi_ready, r_ready = sem("r_hi_ready"), sem("r_ready")
        h_mm, hid_ready, h_hi_ready, h_ready = sem("h_mm"), sem("hid_ready"), sem("h_hi_ready"), sem("h_ready")
        acc_mm, x1_ready, x1_stored, x1_free = sem("acc_mm"), sem("x1_ready"), sem("x1_stored"), sem("x1_free")
        raw1_ready, mv1_ready, std1_ready, rstd1_ready = sem("raw1_ready"), sem("mv1_ready"), sem("std1_ready"), sem("rstd1_ready")
        x1n_ready, x1n_turned, x1nT_free, x1nT_stored = sem("x1n_ready"), sem("x1n_turned"), sem("x1nT_free"), sem("x1nT_stored")
        parts_added = sem("parts_added")
        block = ctx.enter_context(nc.Block())

        AHEAD = 2
        STEPS = BT // (4 * GT)
        SLOTS = JH + CH
        S_SLOT = (0, 1, 2, 3, 7, 8, 9, 10)
        V_SLOT = (1, 2, 3, 4, 8, 9, 10, 11)

        def groups(n, step):
            t0 = step * 4 * GT
            return [(t // P, t % P, min(GT, n - t)) for t in range(t0, min(t0 + 4 * GT, n), GT)]

        def steps(n):
            return [s for s in range(STEPS) if groups(n, s)]

        def last_step(n, sub):
            return max(s for s in steps(n) if groups(n, s)[0][0] == sub)

        def turning(n, after):
            subs = len(subtiles(n))
            order = [(JH - 1 + s // 2, s % 2, "x", s) for s in range(len(subtiles(after)))]
            order += [(JH + 1, 0, "x1", 0)] if subs > 1 else []
            order += [(JH + 1, 1, "agg", 0)] if after else []
            order += [(JH + 2, 0, "x1", 1), (JH + 3, 1, "x1", 2), (SLOTS, 0, "x1", 3)] if subs > 1 else []
            return order if subs > 1 else [(JH, 0, "x1", 0)]

        def turns(n, after, which):
            return len([t for t in turning(n, after) if t[1] == which])

        def turns_before(b, which):
            first = 2 + which
            if isinstance(b, int) and b == NB - 1:
                return first + (FULL - 1) * turns(BT, BT, which) + turns(BT, TAIL, which)
            return b * turns(BT, BT, which) + first

        def numbered(b, n, after):
            use = [turns_before(b, which) for which in range(2)]
            out = []
            for at, which, kind, s in turning(n, after):
                out.append((at, which, use[which], kind, s))
                use[which] = use[which] + 1
            return out

        def act_turned(act, b, n, after, item):
            _, which, _, kind, s = item
            if kind == "x":
                norm.split_hi(act, b + 1, 0, after, s)
            elif kind == "agg":
                act.wait_ge(agg_turned, b + 2)
                act.activation(agg[:, 0:after], turn_bank[1][:, 0:after], ACT.Copy).then_inc(agg_hi_ready, 1)
            else:
                r = subtiles(n)[s]
                act.wait_ge(x1n_turned, b * CH + (s + 1))
                act.wait_ge(x1nT_free, b * CH + s + 1)
                act.wait_ge(parts_added, b * CH + s)
                for ch in range(CH):
                    op = act.activation(x1nT[s % 2][:, ch, 0:r], turn_bank[which][:, ch * P:ch * P + r], ACT.Copy,
                                        accum_out=part[s % 2][:, ch:ch + 1])
                op.then_inc(turn_free[which], 1)

        @block.sync
        def _(sp):
            def load_unit(b, n, u):
                pieces = subtiles(n)[2 * u:2 * u + 2]
                for half, r in enumerate(pieces):
                    at = b * BT + (2 * u + half) * P
                    for dst, row in ((qs, 0), (ks, DIM)):
                        sp.dma_start(dst[half * HDIM:(half + 1) * HDIM, :, 0:r],
                                     c.qk_scaled[row:row + DIM, bass.ds(at, r)].rearrange("(h d) t -> d h t", d=HDIM)
                                     ).then_inc(qk_in, 16)

            def load_v(b, n, s):
                r = subtiles(n)[s]
                rows = c.v.rearrange("t (h e) -> (t h) e", h=HEADS)
                at = b * (BT * HEADS) + s * P * HEADS
                full = r // GT
                sp.dma_start(v[s % 2][:, 0:full, :],
                             rows[bass.ds(at, full * P), :].rearrange("(g p) e -> p g e", p=P)
                             ).then_inc(v_in[s % 2], 16)
                if r % GT:
                    left = (r % GT) * HEADS
                    sp.dma_start(v[s % 2][0:left, full, :], rows[bass.ds(at + full * P, left), :]
                                 ).then_inc(v_in[s % 2], 16)

            def load_tables(b, n):
                for t in range(TABLES):
                    if n == BT:
                        sp.dma_start(agg_raw[:, t, :, :], c.table[t][bass.ds(b * BT, n), :]
                                     .rearrange("(s p) e -> p s e", p=P)).then_inc(table_in, 16)
                    else:
                        sp.dma_start(agg_raw[0:n, t, 0, :], c.table[t][bass.ds(b * BT, n), :]
                                     ).then_inc(table_in, 16)

            sp.dma_start(c.gate_w[:, :, :], c.w_gate.rearrange("(c p) e -> p c e", p=P)).then_inc(c.gate_in, 16)
            sp.dma_start(c.gate_b[:, :], c.b_gate.rearrange("(a e) -> a e", a=1)).then_inc(c.gate_in, 16)
            sp.dma_start(b1[:, :], c.b1).then_inc(bias_in, 16)
            sp.dma_start(bias[:, :], c.b2.partition_broadcast(P)).then_inc(bias_in, 16)
            sp.dma_start(x1n[:, :], c.b_out.partition_broadcast(P)).then_inc(bias_in, 16)
            norm.load(sp, 0, 0, BT)
            load_tables(0, BT)
            load_unit(0, BT, 0)
            weights.load(sp)
            load_v(0, BT, 0)
            load_v(0, BT, 1)
            weights.wait(sp)

            def body(b, k, n, after):
                subs = len(subtiles(n))
                if after:
                    sp.wait_ge(acc_mm, b * CH + AHEAD)
                    sp.wait_ge(x1_ready, b * CH + AHEAD)
                    norm.load(sp, b + 1, 1 - k, after)
                    sp.wait_ge(agg_step, b * 4 + 4)
                    load_tables(b + 1, after)
                if subs > 2:
                    sp.wait_ge(scored, b * STEPS + 4)
                    load_unit(b, n, 1)
                    for s in (2, 3):
                        sp.wait_ge(mixed, b * STEPS + (AHEAD + last_step(n, s - 2) + 1))
                        load_v(b, n, s)
                if after:
                    sp.wait_ge(scored, b * STEPS + len(steps(n)))
                    sp.sem_inc(c.passed, 1)
                    load_unit(b + 1, after, 0)
                    for s in range(min(2, len(subtiles(after)))):
                        sp.wait_ge(mixed, b * STEPS + (AHEAD + last_step(n, subs - 2 + s) + 1))
                        load_v(b + 1, after, s)

            over_blocks(sp, 2, body)

        @block.tensor
        def _(pe):
            def turn_agg(b, n, use):
                pe.wait_ge(agg_step, b * 4 + 4)
                pe.wait_ge(turn_free[1], use)
                pe.sem_inc(c.passed, 1)
                for s, r in enumerate(subtiles(n)):
                    mm = pe.transpose(turn_bank[1][:, s * P:s * P + r],
                                      agg_mean[0:r, s, :, :].rearrange("p a e -> p (a e)"), c.ident[0:r, 0:r])
                mm.then_inc(agg_turned, 1)

            def turn_x1(b, n, s, which, use):
                r = subtiles(n)[s]
                pe.wait_ge(x1n_ready, b * CH + (s + 1))
                pe.wait_ge(turn_free[which], use)
                for ch in range(CH):
                    mm = pe.transpose(turn_bank[which][:, ch * P:ch * P + r], x1n[0:r, ch * P:(ch + 1) * P],
                                      c.ident[0:r, 0:r])
                mm.then_inc(x1n_turned, 1)

            def scores(b, n, step):
                gs = groups(n, step)
                if step % 4 == 0:
                    pe.wait_ge(kt_ready, b * 2 + step // 4 + 1)
                pe.wait_ge(near_ready, b * STEPS + (AHEAD + step))
                for j, (sub, t, w) in enumerate(gs):
                    half = slice((sub % 2) * HDIM, (sub % 2 + 1) * HDIM)
                    mm = pe.matmul(s_bank[0:w * HEADS, j * P:j * P + w * HEADS],
                                   kt[half, t:t + w, :].rearrange("d t h -> d (t h)"),
                                   qs[half, :, t:t + w].rearrange("d h t -> d t h"), start=True, stop=True)
                mm.then_inc(scored, 1)

            def mix(b, n, step):
                gs = groups(n, step)
                sub = gs[0][0]
                pe.wait_ge(near_ready, b * STEPS + (AHEAD + step + 1))
                if step == last_step(n, sub) - len([s for s in steps(n) if groups(n, s)[0][0] == sub]) + 1:
                    pe.wait_ge(r_ready, b * CH + sub)
                    loads = 2 if n % GT else 1
                    pe.wait_ge(v_in[sub % 2], b * 32 + 16 * (sub // 2) + 16 * loads)
                for j, (_, t, w) in enumerate(gs):
                    g = t // GT
                    rows = w * HEADS
                    view = near[0:rows, j, 0:rows].rearrange("p (t h) -> p t h", h=HEADS)
                    for parity in range(2):
                        out = r_bank[parity * HDIM:(parity + 1) * HDIM, :].rearrange("p (c t) -> p t c", c=CH)
                        mm = pe.matmul(out[:, t:t + w, :], v[sub % 2][0:rows, g, :], view[:, :, parity::2],
                                       start=True, stop=True)
                mm.then_inc(mixed, 1)

            def hidden(b, n, j):
                cut = slice(j * P, (j + 1) * P)
                pe.wait_ge(hid_ready, b * JH + j + 1)
                products(pe, h_bank[j % 2][:, 0:n],
                         [(w1_hi[:, ch, cut], w1_lo[:, ch, cut]) for ch in range(CH)],
                         norm.pairs(0, slice(0, n)), last=False)
                pe.matmul(h_bank[j % 2][:, 0:n], w1_hi[:, CH, cut], agg[:, 0:n], start=False, stop=False)
                pe.matmul(h_bank[j % 2][:, 0:n], w1_lo[0:EDIM, CH, cut], agg[0:EDIM, 0:n], start=False, stop=True
                          ).then_inc(h_mm, 1)

            def output(b, n, s):
                r = subtiles(n)[s]
                cut = slice(s * P, s * P + r)
                pe.wait_ge(h_ready, b * JH + JH)
                pe.wait_ge(x1_ready, b * CH + s + 1)
                products(pe, acc[s % 2][0:r, :], [(h_hi[:, j, cut], h_lo[:, j, cut]) for j in range(JH)],
                         [(w2_hi[:, j, :], w2_lo[:, j, :]) for j in range(JH)], last=False)
                pe.wait_ge(r_ready, b * CH + (s + 1))
                products(pe, acc[s % 2][0:r, :], [(r_hi[s % 2][:, ch, 0:r], r_lo[s % 2][:, ch, 0:r]) for ch in range(CH)],
                         [(wo_hi[:, ch, :], wo_lo[:, ch, :]) for ch in range(CH)], first=False).then_inc(acc_mm, 1)

            pe.sem_inc(mixed, AHEAD)
            pe.sem_inc(acc_mm, AHEAD)
            for s in range(CH):
                norm.turn(pe, 0, BT, s, s // 2)
            turn_agg(0, BT, 2)
            weights.wait(pe)

            def early(b, n, step_free):
                for which in range(2):
                    pe.wait_ge(turn_free[which], step_free[which])
                scores(b, n, 0)
                hidden(b, n, 0)

            early(0, BT, [turns_before(0, which) for which in range(2)])

            def body(b, k, n, after):
                order = numbered(b, n, after)
                ready = [t[2] + 1 for which in range(2)
                         for t in [[u for u in order if u[1] == which and u[3] != "x1"][-1]]] if after else None
                subs = len(subtiles(n))
                if subs == 1:
                    mix(b, n, 0)
                    for step in steps(n)[1:]:
                        scores(b, n, step)
                        mix(b, n, step)
                for slot in range(1, JH + subs + 1):
                    if slot == JH + subs:
                        if after:
                            early(b + 1, after, ready)
                    elif subs > 1:
                        for step in steps(n):
                            if S_SLOT[step] == slot:
                                scores(b, n, step)
                            if V_SLOT[step] == slot:
                                mix(b, n, step)
                    if slot < JH:
                        hidden(b, n, slot)
                    elif slot < JH + subs:
                        output(b, n, slot - JH)
                    while order and order[0][0] == slot:
                        _, which, use, kind, s = order.pop(0)
                        if kind == "x":
                            norm.turn(pe, b + 1, after, s, use)
                        elif kind == "agg":
                            turn_agg(b + 1, after, use)
                        else:
                            turn_x1(b, n, s, which, use)

            over_blocks(pe, 2, body)

        @block.scalar
        def _(act):
            act.sem_inc(hid_ready, AHEAD)
            norm.deviation(act, 0, BT)
            for s in range(CH):
                norm.split_hi(act, 0, 0, BT, s)
            act.wait_ge(agg_turned, 1)
            act.activation(agg[:, :], turn_bank[1][:, :], ACT.Copy).then_inc(agg_hi_ready, 1)

            def by_token(b, n, u):
                halves = len(subtiles(n)[2 * u:2 * u + 2])
                rows, r = halves * HDIM, subtiles(n)[2 * u]
                act.wait_ge(qk_in, b * 128 + (64 * u + 32 * halves))
                act.activation(kt[0:rows, 0:r, :], ks[0:rows, :, 0:r].rearrange("d h t -> d t h"), ACT.Copy
                               ).then_inc(kt_ready, 1)

            by_token(0, BT, 0)
            weights.split_hi(act)

            def split_r(b, n, s):
                r = subtiles(n)[s]
                act.wait_ge(mixed, b * STEPS + (AHEAD + last_step(n, s) + 1))
                act.wait_ge(acc_mm, b * CH + s + 1)
                bank = r_bank[:, :].rearrange("p (c t) -> p c t", c=CH)[:, :, 0:r]
                act.activation(r_hi[s % 2][:, :, 0:r], bank, ACT.Copy).then_inc(r_hi_ready, 1)

            def deviation1(b, n, s):
                r = subtiles(n)[s]
                act.wait_ge(mv1_ready, b * CH + (s + 1))
                act.activation(std1[0:r, :], mv1[0:r, 1:2], ACT.Sqrt, bias=c.eps[0:r, :]).then_inc(std1_ready, 1)

            def rectify(b, n, j):
                act.wait_ge(h_mm, b * JH + j + 1)
                act.wait_ge(h_ready, b * JH + j)
                act.activation(hid[:, 0:n], h_bank[j % 2][:, 0:n], ACT.Relu,
                               bias=b1[:, j:j + 1]).then_inc(hid_ready, 1)
                act.wait_ge(hid_ready, b * JH + (AHEAD + j + 1))
                if j == 0:
                    act.wait_ge(acc_mm, b * CH + AHEAD)
                act.activation(h_hi[:, j, 0:n], hid[:, 0:n], ACT.Copy).then_inc(h_hi_ready, 1)

            act.wait_ge(bias_in, 48)
            weights.wait(act)
            rectify(0, BT, 0)

            def body(b, k, n, after):
                order = numbered(b, n, after)
                subs = len(subtiles(n))
                if subs == 1:
                    split_r(b, n, 0)
                for slot in range(1, JH + subs + 1):
                    if subs > 1:
                        for s in range(subs):
                            if V_SLOT[last_step(n, s)] == slot:
                                split_r(b, n, s)
                    if slot < JH:
                        rectify(b, n, slot)
                        if after and slot == 5:
                            norm.deviation(act, b + 1, after)
                        if subs > 2 and slot == 4:
                            act.wait_ge(scored, b * STEPS + 4)
                            by_token(b, n, 1)
                    elif slot < JH + subs:
                        deviation1(b, n, slot - JH)
                        if after and slot == 10:
                            act.wait_ge(scored, b * STEPS + STEPS)
                            by_token(b + 1, after, 0)
                    elif after:
                        rectify(b + 1, after, 0)
                    while order and order[0][0] == slot:
                        act_turned(act, b, n, after, order.pop(0))

            over_blocks(act, 2, body)

        @block.vector
        def _(dve):
            def divide_sums(b, n):
                r, ns = subtiles(n)[-1], len(subtiles(n))
                dve.wait_ge(table_in, b * (16 * TABLES) + 16 * TABLES)
                dve.tensor_reduce(agg_sum[0:r, 0:ns, :], agg_raw[0:r, :, 0:ns, :].rearrange("p t s e -> p s e t"),
                                  AX.X, ALU.add).then_inc(agg_step, 1)
                dve.wait_ge(agg_step, b * 4 + 1)
                dve.tensor_scalar(agg_cnt[0:r, 0:ns], agg_sum[0:r, 0:ns, EDIM], 1.0, None, ALU.max).then_inc(agg_step, 1)
                dve.wait_ge(agg_step, b * 4 + 2)
                dve.reciprocal(agg_inv[0:r, 0:ns], agg_cnt[0:r, 0:ns]).then_inc(agg_step, 1)
                dve.wait_ge(agg_step, b * 4 + 3)
                dve.tensor_tensor(agg_mean[0:r, 0:ns, :, :],
                                  agg_sum[0:r, 0:ns, 0:EDIM].unsqueeze(2).to_broadcast([r, ns, 2, EDIM]),
                                  agg_inv[0:r, 0:ns].unsqueeze(2).unsqueeze(3).to_broadcast([r, ns, 2, EDIM]),
                                  ALU.mult).then_inc(agg_step, 1)

            def split_agg(b, n):
                dve.wait_ge(agg_hi_ready, b + 1)
                dve.tensor_tensor(agg[EDIM:P, 0:n], turn_bank[1][EDIM:P, 0:n], agg[EDIM:P, 0:n].bitcast(F32),
                                  ALU.subtract).then_inc(turn_free[1], 1)

            def take_factor(b, k):
                dve.tensor_copy(factor[k][:, :], c.factors[:, bass.ds(b, 1)]).then_inc(factor_ready, 1)

            def neighbours(b, k, n, step):
                gs = groups(n, step)
                if step == 0:
                    dve.wait_ge(factor_ready, b + 1)
                dve.wait_ge(scored, b * STEPS + step + 1)
                dve.wait_ge(mixed, b * STEPS + (AHEAD + step))
                whole = len([g for g in gs if g[2] == GT])
                if whole:
                    op = dve.scalar_tensor_tensor(
                        out=near[:, 0:whole, :],
                        in0=s_bank[:, 0:whole * P].rearrange("p (j f) -> p j f", f=P),
                        scalar=factor[k][:, :], in1=c.same_token[:, :].unsqueeze(1).to_broadcast([P, whole, P]),
                        op0=ALU.mult, op1=ALU.mult)
                if whole < len(gs):
                    rows = gs[-1][2] * HEADS
                    op = dve.scalar_tensor_tensor(
                        out=near[0:rows, whole, 0:rows], in0=s_bank[0:rows, whole * P:whole * P + rows],
                        scalar=factor[k][0:rows, :], in1=c.same_token[0:rows, 0:rows], op0=ALU.mult, op1=ALU.mult)
                op.then_inc(near_ready, 1)

            def split_r(b, n, s):
                r = subtiles(n)[s]
                dve.wait_ge(r_hi_ready, b * CH + (s + 1))
                bank = r_bank[:, :].rearrange("p (c t) -> p c t", c=CH)[:, :, 0:r]
                dve.tensor_tensor(r_lo[s % 2][:, :, 0:r], bank, r_hi[s % 2][:, :, 0:r].bitcast(F32),
                                  ALU.subtract).then_inc(r_ready, 1)

            def finish(b, k, n, s):
                r = subtiles(n)[s]
                at = b * CH + (s + 1)
                dve.wait_ge(acc_mm, at + AHEAD)
                dve.wait_ge(base_ready, at)
                dve.wait_ge(x1_free, b * CH + s + 1)
                dve.tensor_tensor(x1[s % 2][0:r, :], acc[s % 2][0:r, :], norm.x[k][0:r, s, :], ALU.add
                                  ).then_inc(x1_ready, 1)
                dve.wait_ge(x1_ready, at + AHEAD)
                dve.bn_stats(raw1[0:r, :], x1[s % 2][0:r, :]).then_inc(raw1_ready, 1)
                dve.wait_ge(raw1_ready, at)
                dve.sem_inc(c.passed, 1)
                dve.bn_aggr(mv1[0:r, :], raw1[0:r, :]).then_inc(mv1_ready, 1)
                dve.wait_ge(std1_ready, at)
                dve.reciprocal(rstd1[0:r, :], std1[0:r, :]).then_inc(rstd1_ready, 1)
                dve.wait_ge(rstd1_ready, at)
                dve.wait_ge(x1n_turned, b * CH + s)
                dve.tensor_scalar(x1n[0:r, :], x1[s % 2][0:r, :], mv1[0:r, 0:1], rstd1[0:r, :],
                                  ALU.subtract, ALU.mult).then_inc(x1n_ready, 1)

            def add_part(b, s, which, use):
                dve.wait_ge(turn_free[which], use + 1)
                dve.wait_ge(parts_added, b * CH + (s + 1))
                dve.tensor_tensor(c.token_sum[:, :], c.token_sum[:, :], part[s % 2][:, :], ALU.add
                                  ).then_inc(parts_added, 1)

            dve.sem_inc(near_ready, AHEAD)
            dve.sem_inc(x1_ready, AHEAD)
            dve.memset(c.token_sum[:, :], 0.0).then_inc(parts_added, 1)
            dve.wait_ge(bias_in, 48)
            dve.tensor_tensor(bias[:, :], bias[:, :], x1n[:, :], ALU.add).then_inc(bias_ready, 1)
            norm.first_on_dve(dve)
            divide_sums(0, BT)
            split_agg(0, BT)
            take_factor(0, 0)

            def low(b, n, j):
                dve.wait_ge(h_hi_ready, b * JH + j + 1)
                dve.tensor_tensor(h_lo[:, j, 0:n], hid[:, 0:n], h_hi[:, j, 0:n].bitcast(F32),
                                  ALU.subtract).then_inc(h_ready, 1)

            weights.split_lo(dve)
            neighbours(0, 0, BT, 0)
            low(0, BT, 0)

            def body(b, k, n, after):
                order = numbered(b, n, after)
                subs = len(subtiles(n))
                if subs == 1:
                    for step in steps(n)[1:]:
                        neighbours(b, k, n, step)
                    split_r(b, n, 0)
                for slot in range(1, JH + subs + 1):
                    if slot == JH + subs:
                        if after:
                            neighbours(b + 1, 1 - k, after, 0)
                            low(b + 1, after, 0)
                    elif subs > 1:
                        for step in steps(n):
                            if S_SLOT[step] == slot:
                                neighbours(b, k, n, step)
                        for s in range(subs):
                            if V_SLOT[last_step(n, s)] == slot:
                                split_r(b, n, s)
                    if slot < JH:
                        low(b, n, slot)
                    elif slot < JH + subs:
                        finish(b, k, n, slot - JH)
                    if after and slot <= len(subtiles(after)):
                        norm.stats(dve, b + 1, 1 - k, after, slot - 1)
                    if after and slot == 5:
                        norm.aggregate(dve, b + 1, 1 - k, after)
                    if after and slot == 6:
                        norm.invert(dve, b + 1, after)
                        take_factor(b + 1, 1 - k)
                        for s in range(min(2, len(subtiles(after)))):
                            norm.normalise(dve, b + 1, 1 - k, after, s)
                    if after and slot == 7:
                        divide_sums(b + 1, after)
                    while order and order[0][0] == slot:
                        _, which, use, kind, s = order.pop(0)
                        if kind == "x":
                            norm.split_lo(dve, b + 1, 0, after, s)
                            if s + 2 < len(subtiles(after)):
                                norm.normalise(dve, b + 1, 1 - k, after, s + 2)
                        elif kind == "agg":
                            split_agg(b + 1, after)
                        else:
                            add_part(b, s, which, use)

            over_blocks(dve, 2, body)

        @block.gpsimd
        def _(pool):
            def bases(b, k, n):
                for s, r in enumerate(subtiles(n)):
                    at = b * CH + (s + 1)
                    pool.wait_ge(norm.xn_ready, at)
                    pool.tensor_tensor(norm.x[k][0:r, s, :], norm.x[k][0:r, s, :], norm.xn[s % 2][0:r, :], ALU.add
                                       ).then_inc(with_xn, 1)
                    pool.wait_ge(with_xn, at)
                    pool.tensor_tensor(norm.x[k][0:r, s, :], norm.x[k][0:r, s, :], bias[0:r, :], ALU.add
                                       ).then_inc(base_ready, 1)

            pool.sem_inc(x1_free, AHEAD)
            pool.sem_inc(x1nT_free, AHEAD)
            pool.wait_ge(bias_ready, 1)
            bases(0, 0, BT)

            def body(b, k, n, after):
                turned = {s: (turn_free[which], use + 1) for _, which, use, kind, s in numbered(b, n, after)
                          if kind == "x1"}
                if after:
                    bases(b + 1, 1 - k, after)
                for s, r in enumerate(subtiles(n)):
                    at = b * BT + s * P
                    pool.wait_ge(x1_ready, b * CH + (AHEAD + s + 1))
                    pool.dma_start(c.x1[bass.ds(at, r), :], x1[s % 2][0:r, :]).then_inc(x1_stored, 16)
                    pool.wait_ge(*turned[s])
                    pool.dma_start(c.x1n[:, bass.ds(at, r)].rearrange("(c p) t -> p c t", p=P), x1nT[s % 2][:, :, 0:r]
                                   ).then_inc(x1nT_stored, 16)
                    pool.wait_ge(x1_stored, b * (16 * CH) + 16 * (s + 1))
                    pool.sem_inc(x1_free, 1)
                    pool.wait_ge(x1nT_stored, b * (16 * CH) + 16 * (s + 1))
                    pool.sem_inc(x1nT_free, 1)

            over_blocks(pool, 2, body)


def expert_stage(nc, c):
    with ExitStack() as ctx:
        def sb(what, shape, dt=F32):
            return ctx.enter_context(nc.sbuf_tensor(f"ex_{what}", shape, dt))

        def bank(what):
            return ctx.enter_context(nc.psum_tensor(f"ex_{what}", [P, BT], F32))

        def sem(what):
            return ctx.enter_context(nc.semaphore(f"ex_{what}"))

        U = 4
        mean = sb("mean", [P, CH])
        logit, prob_e, prob = sb("logit", [1, EXPERTS]), sb("prob_e", [1, EXPERTS]), sb("prob", [1, EXPERTS])
        neg_top, total, total_inv = sb("neg_top", [1, 1]), sb("total", [1, 1]), sb("total_inv", [1, 1])
        other, rank = sb("other", [1, EXPERTS]), sb("rank", [1, EXPERTS])
        pick = sb("pick", [1, 2])
        pick_all = sb("pick_all", [P, 2])
        row_f = sb("row_f", [P, CH])
        row = sb("row", [P, CH], I32)
        expert = sb("expert", [P, 1], I32)
        w_raw = sb("w_raw", [P, CH, DIM])
        w_hi = sb("w_hi", [P, CH, DIM], F32R)
        w_lo = sb("w_lo", [P, CH, DIM], F32R)
        b_raw = sb("b_raw", [P, DIM])
        xT = [sb(f"xT{k}", [P, CH, BT]) for k in range(U)]
        xT_hi = [sb(f"xT_hi{k}", [P, CH, BT], F32R) for k in range(U)]
        xT_lo = [sb(f"xT_lo{k}", [P, CH, BT], F32R) for k in range(U)]
        x1 = [sb(f"x1_{k}", [P, CH, DIM]) for k in range(U)]
        y = [sb(f"y{k}", [P, DIM]) for k in range(2)]
        done = [sb(f"done{k}", [P, CH, DIM]) for k in range(2)]
        small, wide = bank("small"), bank("wide")
        BANKS = 4
        y_bank = [bank(f"y_bank{k}") for k in range(BANKS)]
        gate_step, gate_mm, gate_exp = sem("gate_step"), sem("gate_mm"), sem("gate_exp")
        gathered, w_hi_ready, w_ready = sem("gathered"), sem("w_hi_ready"), sem("w_ready")
        x_in, x1_in = [sem(f"x_in{k}") for k in range(U)], [sem(f"x1_in{k}") for k in range(U)]
        xT_hi_ready, xT_ready = sem("xT_hi_ready"), sem("xT_ready")
        y_mm, y_ready, y_done, stored, done_free = sem("y_mm"), sem("y_ready"), sem("y_done"), sem("stored"), sem("done_free")
        block = ctx.enter_context(nc.Block())

        @block.sync
        def _(sp):
            def load_xT(b, k, n):
                sp.dma_start(xT[k][:, :, 0:n], c.x1n[:, cols(b, n)].rearrange("(c p) t -> p c t", p=P)
                             ).then_inc(x_in[k], 16)

            def load_x1(b, k, n):
                if n == BT:
                    sp.dma_start(x1[k][:, :, :], c.x1[cols(b, n), :].rearrange("(s p) d -> p s d", p=P)
                                 ).then_inc(x1_in[k], 16)
                else:
                    sp.dma_start(x1[k][0:n, 0, :], c.x1[cols(b, n), :]).then_inc(x1_in[k], 16)

            load_xT(0, 0, BT)
            sp.wait_ge(gathered, 16 * (CH + 1))
            load_x1(0, 0, BT)
            for b in (1, 2):
                load_xT(b, b, BT)
                load_x1(b, b, BT)

            def body(b, k, n, after):
                ns = len(subtiles(n))
                if later_size(b, 3):
                    sp.wait_ge(xT_ready, b)
                    load_xT(b + 3, (k + 3) % U, later_size(b, 3))
                    sp.wait_ge(y_done, b * CH)
                    load_x1(b + 3, (k + 3) % U, later_size(b, 3))
                sp.wait_ge(stored, b * 16)
                sp.sem_inc(done_free, 1)
                sp.wait_ge(y_done, b * CH + ns)
                sp.sem_inc(c.passed, 1)
                if n == BT:
                    sp.dma_start(c.out[cols(b, n), :].rearrange("(s p) d -> p s d", p=P), done[k % 2][:, :, :]
                                 ).then_inc(stored, 16)
                else:
                    sp.dma_start(c.out[cols(b, n), :], done[k % 2][0:n, 0, :]).then_inc(stored, 16)

            over_blocks(sp, U, body)
            sp.wait_ge(stored, 16 * NB)

        @block.gpsimd
        def _(pool):
            pool.wait_ge(gate_step, 13)
            for ch in range(CH):
                pool.indirect_dma_start(w_raw[:, ch, :], None, c.w_exp,
                                        bass.IndirectOffsetOnAxis(ap=row[:, ch:ch + 1], axis=0),
                                        bounds_check=EXPERTS * DIM - 1).then_inc(gathered, 16)
            pool.indirect_dma_start(b_raw[:, :], None, c.b_exp,
                                    bass.IndirectOffsetOnAxis(ap=expert[:, :], axis=0),
                                    bounds_check=EXPERTS - 1).then_inc(gathered, 16)

        @block.tensor
        def _(pe):
            pe.wait_ge(c.gate_in, 32)
            pe.wait_ge(gate_step, 1)
            for ch in range(CH):
                mm = pe.matmul(small[0:1, 0:EXPERTS], mean[:, ch:ch + 1], c.gate_w[:, ch, :], start=ch == 0,
                               stop=ch == CH - 1)
            mm.then_inc(gate_mm, 1)
            pe.wait_ge(gate_step, 10)
            pe.matmul(wide[:, 0:2], c.ones_row[:, :], pick[:, :], start=True, stop=True).then_inc(gate_mm, 1)
            pe.wait_ge(w_ready, CH)

            def body(b, k, n, after):
                pe.wait_ge(xT_ready, b + 1)
                for s, r in enumerate(subtiles(n)):
                    cut = slice(s * P, s * P + r)
                    pe.wait_ge(y_ready, b * CH + s + 1)
                    products(pe, y_bank[s % BANKS][0:r, :], [(xT_hi[k][:, ch, cut], xT_lo[k][:, ch, cut]) for ch in range(CH)],
                             [(w_hi[:, ch, :], w_lo[:, ch, :]) for ch in range(CH)]).then_inc(y_mm, 1)

            over_blocks(pe, U, body)

        @block.scalar
        def _(act):
            act.wait_ge(gate_step, 3)
            act.activation(prob_e[:, :], logit[:, :], ACT.Exp, bias=neg_top[:, :], accum_out=total[:, :]
                           ).then_inc(gate_exp, 1)
            def high(b, k, n):
                act.wait_ge(x_in[k], landed(b, k, U))
                act.activation(xT_hi[k][:, :, 0:n], xT[k][:, :, 0:n], ACT.Copy).then_inc(xT_hi_ready, 1)

            high(0, 0, BT)
            for ch in range(CH):
                act.wait_ge(gathered, 16 * (CH + 1))
                act.activation(w_hi[:, ch, :], w_raw[:, ch, :], ACT.Copy).then_inc(w_hi_ready, 1)
            high(1, 1, BT)

            def ahead(b, k, n, after):
                if later_size(b, 2):
                    act.wait_ge(y_mm, b * CH)
                    high(b + 2, (k + 2) % U, later_size(b, 2))

            over_blocks(act, U, ahead)

        @block.vector
        def _(dve):
            def step(op):
                op.then_inc(gate_step, 1)

            step(dve.tensor_scalar(mean[:, :], c.token_sum[:, :], 1.0 / TOKENS, None, ALU.mult))
            dve.wait_ge(gate_mm, 1)
            step(dve.tensor_tensor(logit[:, :], small[0:1, 0:EXPERTS], c.gate_b[:, :], ALU.add))
            dve.wait_ge(gate_step, 2)
            step(dve.tensor_reduce(neg_top[:, :], logit[:, :], AX.X, ALU.max, negate=True))
            dve.wait_ge(gate_exp, 1)
            step(dve.reciprocal(total_inv[:, :], total[:, :]))
            dve.wait_ge(gate_step, 4)
            step(dve.tensor_scalar(prob[:, :], prob_e[:, :], total_inv[:, :], None, ALU.mult))
            dve.wait_ge(gate_step, 5)
            step(dve.tensor_reduce(pick[:, 1:2], prob[:, :], AX.X, ALU.max))
            dve.wait_ge(gate_step, 6)
            step(dve.tensor_scalar(other[:, :], prob[:, :], pick[:, 1:2], None, ALU.is_lt))
            dve.wait_ge(gate_step, 7)
            step(dve.scalar_tensor_tensor(out=rank[:, :], in0=other[:, :], scalar=float(EXPERTS),
                                          in1=c.expert_no[:, :], op0=ALU.mult, op1=ALU.add))
            dve.wait_ge(gate_step, 8)
            dve.tensor_reduce(pick[:, 0:1], rank[:, :], AX.X, ALU.min).then_inc(gate_step, 2)
            dve.wait_ge(gate_mm, 2)
            step(dve.tensor_copy(pick_all[:, :], wide[:, 0:2]))
            dve.wait_ge(gate_step, 11)
            dve.tensor_copy(expert[:, :], pick_all[:, 0:1])
            step(dve.scalar_tensor_tensor(out=row_f[:, :], in0=pick_all[:, 0:1].to_broadcast([P, CH]),
                                          scalar=float(DIM), in1=c.feat[:, :], op0=ALU.mult, op1=ALU.add))
            dve.wait_ge(gate_step, 12)
            step(dve.tensor_copy(row[:, :], row_f[:, :]))
            def split(b, k, n):
                dve.wait_ge(xT_hi_ready, b + 1)
                dve.tensor_tensor(xT_lo[k][:, :, 0:n], xT[k][:, :, 0:n], xT_hi[k][:, :, 0:n].bitcast(F32),
                                  ALU.subtract).then_inc(xT_ready, 1)

            split(0, 0, BT)
            for ch in range(CH):
                dve.wait_ge(w_hi_ready, ch + 1)
                dve.tensor_tensor(w_lo[:, ch, :], w_raw[:, ch, :], w_hi[:, ch, :].bitcast(F32), ALU.subtract
                                  ).then_inc(w_ready, 1)

            dve.sem_inc(y_ready, BANKS)
            split(1, 1, BT)

            def body(b, k, n, after):
                dve.wait_ge(x1_in[k], landed(b, k, U))
                for s, r in enumerate(subtiles(n)):
                    at = b * CH + (s + 1)
                    dve.wait_ge(y_mm, at)
                    dve.tensor_tensor(y[s % 2][0:r, :], y_bank[s % BANKS][0:r, :], b_raw[0:r, :], ALU.add).then_inc(y_ready, 1)
                    dve.wait_ge(y_ready, at + BANKS)
                    if s == 0:
                        dve.wait_ge(done_free, b)
                    dve.scalar_tensor_tensor(out=done[k % 2][0:r, s, :], in0=y[s % 2][0:r, :], scalar=pick_all[0:r, 1:2],
                                             in1=x1[k][0:r, s, :], op0=ALU.mult, op1=ALU.add).then_inc(y_done, 1)
                    if s == 0 and later_size(b, 2):
                        split(b + 2, (k + 2) % U, later_size(b, 2))

            over_blocks(dve, U, body)

def kernel_body(nc, c):
    with ExitStack() as ctx:
        def sb(what, shape, dt=F32):
            return ctx.enter_context(nc.sbuf_tensor(what, shape, dt))

        c.scattered = [ctx.enter_context(nc.semaphore(f"scattered{t}")) for t in range(TABLES)]
        c.passed = ctx.enter_context(nc.semaphore("passed"))
        c.ident = sb("ident", [P, P])
        c.same_token = sb("same_token", [P, P])
        c.eps = sb("eps", [P, 1])
        c.ones_row = sb("ones_row", [1, P])
        c.feat = sb("feat", [P, CH])
        c.expert_no = sb("expert_no", [1, EXPERTS])
        c.factors = sb("factors", [P, NB])
        c.token_sum = sb("token_sum", [P, CH])
        c.gate_w = sb("gate_w", [P, CH, EXPERTS])
        c.gate_b = sb("gate_b", [1, EXPERTS])
        c.gate_in = ctx.enter_context(nc.semaphore("gate_in"))
        with ExitStack() as early:
            def sb2(what, shape, dt=F32):
                return early.enter_context(nc.sbuf_tensor(what, shape, dt))

            c.ident_r = sb2("ident_r", [P, P], F32R)
            c.upper = sb2("upper", [P, P])
            c.sel = sb2("sel", [2 * HEADS, QK * P], F32R)
            c.row_sel = sb2("row_sel", [HEADS, P])
            c.spare = sb2("spare", [P, 1])
            c.zero = sb2("zero", [P, TROWS // P * ECOLS // 5])
            c.bias_v = sb2("bias_v", [P, DIM])
            c.bias_qk = sb2("bias_qk", [P, QK])
            c.sums = sb2("sums", [P, QK])
            c.shares = sb2("shares", [P, QK])
            c.heads = sb2("heads", [P, QK, 2 * HEADS])
            constants_stage(nc, c)
            edges = project_stage(nc, c)
            with nc.sbuf_tensor("inverse", [2 * HEADS, TOKENS], F32) as c.inverse:
                edges = norms_stage(nc, c, edges)
                edges = scale_stage(nc, c, edges)
        mix_stage(nc, c)
        expert_stage(nc, c)


def _layouts(inp):
    import numpy as np
    arr = {n: np.asarray(a) for n, a in inp.items()}
    w = arr["L0_mix_W_qkv"].reshape(HEADS, 3, HDIM, DIM).transpose(1, 0, 2, 3).reshape(3 * DIM, DIM)
    bq = arr["L0_mix_b_qkv"].reshape(HEADS, 3, HDIM).transpose(1, 0, 2).reshape(3 * DIM)
    out = {
        "x": arr["x"], "dst": arr["dst"], "edge_attr": arr["edge_attr_64"],
        "w_qkv": w.T, "b_qk": bq[:2 * DIM].reshape(QK, P).T, "b_v": bq[2 * DIM:],
        "w1": arr["L0_gnn_W1"], "b1": arr["L0_gnn_b1"].reshape(JH, P).T, "w2": arr["L0_gnn_W2"], "b2": arr["L0_gnn_b2"],
        "w_out": arr["L0_mix_W_out"].T, "b_out": arr["L0_mix_b_out"],
        "w_gate": arr["L0_ffn_Wg"], "b_gate": arr["L0_ffn_bg"],
        "w_exp": arr["L0_ffn_We"].reshape(EXPERTS * DIM, DIM), "b_exp": arr["L0_ffn_be"],
    }
    return {n: np.ascontiguousarray(a) for n, a in out.items()}


def build(nc, shapes):
    c = Shared()

    def given(name):
        shape, dtype = shapes[name]
        return nc.dram_tensor(f"in_{name}", shape, dtype, kind="ExternalInput").ap()

    c.x, c.dst, c.edge_attr = given("x"), given("dst"), given("edge_attr")
    c.w_qkv, c.b_qk, c.b_v = given("w_qkv"), given("b_qk"), given("b_v")
    c.w1, c.b1, c.w2, c.b2 = given("w1"), given("b1"), given("w2"), given("b2")
    c.w_out, c.b_out = given("w_out"), given("b_out")
    c.w_gate, c.b_gate = given("w_gate"), given("b_gate")
    c.w_exp, c.b_exp = given("w_exp"), given("b_exp")
    c.out = nc.dram_tensor("out", (TOKENS, DIM), F32, kind="ExternalOutput").ap()
    c.v = nc.dram_tensor("v_rows", [TOKENS, DIM], F32, kind="Internal").ap()
    c.qk = nc.dram_tensor("qk_T", [2 * DIM, TOKENS], F32, kind="Internal").ap()
    c.qk_scaled = nc.dram_tensor("qk_scaled_T", [2 * DIM, TOKENS], F32, kind="Internal").ap()
    c.x1 = nc.dram_tensor("x1_rows", [TOKENS, DIM], F32, kind="Internal").ap()
    c.x1n = nc.dram_tensor("x1n_T", [DIM, TOKENS], F32, kind="Internal").ap()
    c.table = [nc.dram_tensor(f"table{t}", [TROWS, ECOLS], F32, kind="Internal").ap() for t in range(TABLES)]
    kernel_body(nc, c)


def kernel(**inputs):
    import numpy as _np
    import concourse.bacc as _bacc
    from concourse.bass_utils import run_bass_kernel_spmd as _run

    arrays = _layouts(inputs)
    nc = _bacc.Bacc("TRN2", target_bir_lowering=False, num_devices=1)
    build(nc, {n: (a.shape, mybir.dt.from_np(a.dtype)) for n, a in arrays.items()})
    r = _run(nc, [{f"in_{n}": a for n, a in arrays.items()}], core_ids=[0])
    return r.results[0]["out"]
```
